# Optimizing a Trainium2 kernel written in Bass

```python
import numpy as np
import jax
import jax.numpy as jnp

def _softmax(x, axis=-1):
    return jax.nn.softmax(x, axis=axis)

def _gelu(x):
    return jax.nn.gelu(x, approximate=True)

def _silu(x):
    return jax.nn.silu(x)

def _sigmoid(x):
    return jax.nn.sigmoid(x)

def _layernorm(x, axis=-1, eps=1e-05):
    m = jnp.mean(x, axis=axis, keepdims=True)
    v = jnp.var(x, axis=axis, keepdims=True)
    return (x - m) / jnp.sqrt(v + eps)

def _scatter_add(tgt, idx, src, axis=0):
    return tgt.at[idx].add(src)

def _segment_sum(src, seg, n):
    return jax.ops.segment_sum(src, seg, n)
kernel_name = 'mk_gnn_ffn_d2_gnn_r32_51f584'

def setup_inputs(seed: int=0):
    np.random.seed(seed)
    _w = jnp.asarray

    def _rec_inputs():
        import jax
        import jax.numpy as jnp
        _gk = jax.random.key(seed)
        x = -0.0003713 + 1 * jax.random.normal(jax.random.fold_in(_gk, 1), (3125, 256), jnp.float32)
        _s = jax.random.randint(jax.random.fold_in(_gk, 2), (25000,), 0, 3125, jnp.int32)
        _d = jax.random.randint(jax.random.fold_in(_gk, 3), (25000,), 0, 3125, jnp.int32)
        _loop = jnp.arange(3125, dtype=jnp.int32)
        src = jnp.concatenate([_s, _d, _loop])
        dst = jnp.concatenate([_d, _s, _loop])
        _o = jnp.argsort(dst, stable=True)
        src = src[_o]
        dst = dst[_o]
        edge_type_8 = jax.random.randint(jax.random.fold_in(_gk, 12), (53125,), 0, 8, jnp.int32)
        return (x, src, dst, edge_type_8)
    x, src, dst, edge_type_8 = _rec_inputs()

    def _L0_gnn_setup():
        import jax, jax.numpy as jnp
        import numpy as np
        N_NODES = 50000
        N_EDGES = 25000
        F_IN = 256
        HEADS = 4
        C_OUT = 64
        NEG_SLOPE = 0.2
        key = jax.random.key(seed)
        k0, k1, k2, k3, k4, k5 = jax.random.split(key, 6)
        x = jax.random.normal(k0, (N_NODES, F_IN), dtype=jnp.float32)
        edge_index = jax.random.randint(k1, (2, N_EDGES), 0, N_NODES, dtype=jnp.int64)
        s = 1.0 / np.sqrt(F_IN)
        W = jax.random.uniform(k2, (HEADS * C_OUT, F_IN), minval=-s, maxval=s, dtype=jnp.float32)
        att_src = jax.random.normal(k3, (HEADS, C_OUT), dtype=jnp.float32) * 0.1
        att_dst = jax.random.normal(k4, (HEADS, C_OUT), dtype=jnp.float32) * 0.1
        bias = jnp.zeros((HEADS * C_OUT,), dtype=jnp.float32)
        return {'x': x, 'edge_index': edge_index, 'W': W, 'att_src': att_src, 'att_dst': att_dst, 'bias': bias}
    _L0_gnn_all = _L0_gnn_setup()
    _L0_gnn_in = {k: v for k, v in _L0_gnn_all.items() if k in ('W', 'att_src', 'att_dst', 'bias')}
    del _L0_gnn_all

    def _L0_ffn_setup():
        import math
        import jax, jax.numpy as jnp
        import numpy as np
        CAPACITY_FACTOR = 1.25
        key = jax.random.key(seed)
        ks = jax.random.split(key, 5)
        B, L, D, F, E = (8, 256, 256, 1024, 8)
        h = jax.random.normal(ks[0], (B, L, D), dtype=jnp.float32)
        gate_w = jax.random.normal(ks[1], (D, E), dtype=jnp.float32) * 0.02
        gate_b = jnp.zeros((E,), dtype=jnp.float32)
        w1 = jax.random.normal(ks[2], (E, D, F), dtype=jnp.float32) * (1.0 / math.sqrt(D))
        b1 = jnp.zeros((E, F), dtype=jnp.float32)
        w2 = jax.random.normal(ks[3], (E, F, D), dtype=jnp.float32) * (1.0 / math.sqrt(F))
        b2 = jnp.zeros((E, D), dtype=jnp.float32)
        return {'h': h, 'gate_w': gate_w, 'gate_b': gate_b, 'w1': w1, 'b1': b1, 'w2': w2, 'b2': b2}
    _L0_ffn_all = _L0_ffn_setup()
    _L0_ffn_in = {k: v for k, v in _L0_ffn_all.items() if k in ('gate_w', 'gate_b', 'w1', 'b1', 'w2', 'b2')}
    del _L0_ffn_all

    def _L1_gnn_setup():
        import jax, jax.numpy as jnp
        import numpy as np
        N_NODES = 50000
        N_EDGES = 25000
        N_REL = 8
        DIM = 256

        def _rgcn_layer(x, W, b, src, dst, edge_type, num_nodes):
            xt = jnp.einsum('ni,rio->rno', x, W)
            msg = jax.nn.relu(xt[edge_type, src] + b)
            return jax.ops.segment_sum(msg, dst, num_segments=num_nodes)
        key = jax.random.key(seed)
        ks = jax.random.split(key, 6)
        x = jax.random.normal(ks[0], (N_NODES, DIM), dtype=jnp.float32)
        limit = float(np.sqrt(6.0 / (DIM + DIM)))
        W0 = jax.random.uniform(ks[1], (N_REL, DIM, DIM), dtype=jnp.float32, minval=-limit, maxval=limit)
        W1 = jax.random.uniform(ks[2], (N_REL, DIM, DIM), dtype=jnp.float32, minval=-limit, maxval=limit)
        b0 = jnp.zeros((DIM,), dtype=jnp.float32)
        b1 = jnp.zeros((DIM,), dtype=jnp.float32)
        edge_index = jax.random.randint(ks[3], (2, N_EDGES), 0, N_NODES, dtype=jnp.int64)
        edge_type = jax.random.randint(ks[4], (N_EDGES,), 0, N_REL, dtype=jnp.int64)
        return {'x': x, 'W0': W0, 'b0': b0, 'W1': W1, 'b1': b1, 'edge_index': edge_index, 'edge_type': edge_type}
    _L1_gnn_all = _L1_gnn_setup()
    _L1_gnn_in = {k: v for k, v in _L1_gnn_all.items() if k in ('W0', 'b0', 'W1', 'b1')}
    del _L1_gnn_all

    def _L1_ffn_setup():
        import jax, jax.numpy as jnp
        import numpy as np
        TOP_K = 2
        LN_EPS = 1e-05
        key = jax.random.key(seed)
        ks = jax.random.split(key, 8)
        B, S, D, E, H = (16, 1024, 256, 8, 1024)
        x = jax.random.normal(ks[0], (B, S, D), dtype=jnp.float32)
        Wr = jax.random.normal(ks[1], (D, E), dtype=jnp.float32) * 0.1
        br = jnp.zeros((E,), dtype=jnp.float32)
        ln_g = jnp.ones((E, D), dtype=jnp.float32)
        ln_b = jnp.zeros((E, D), dtype=jnp.float32)
        W1 = jax.random.normal(ks[2], (E, D, H), dtype=jnp.float32) * (1.0 / np.sqrt(D))
        b1 = jnp.zeros((E, H), dtype=jnp.float32)
        W2 = jax.random.normal(ks[3], (E, H, D), dtype=jnp.float32) * (1.0 / np.sqrt(H))
        b2 = jnp.zeros((E, D), dtype=jnp.float32)
        return {'x': x, 'Wr': Wr, 'br': br, 'ln_g': ln_g, 'ln_b': ln_b, 'W1': W1, 'b1': b1, 'W2': W2, 'b2': b2}
    _L1_ffn_all = _L1_ffn_setup()
    _L1_ffn_in = {k: v for k, v in _L1_ffn_all.items() if k in ('Wr', 'br', 'ln_g', 'ln_b', 'W1', 'b1', 'W2', 'b2')}
    del _L1_ffn_all
    return {'x': x, 'src': src, 'dst': dst, 'edge_type_8': edge_type_8, 'L0_gnn_W': _L0_gnn_in['W'], 'L0_gnn_att_src': _L0_gnn_in['att_src'], 'L0_gnn_att_dst': _L0_gnn_in['att_dst'], 'L0_gnn_bias': _L0_gnn_in['bias'], 'L0_ffn_gate_w': _L0_ffn_in['gate_w'], 'L0_ffn_gate_b': _L0_ffn_in['gate_b'], 'L0_ffn_w1': _L0_ffn_in['w1'], 'L0_ffn_b1': _L0_ffn_in['b1'], 'L0_ffn_w2': _L0_ffn_in['w2'], 'L0_ffn_b2': _L0_ffn_in['b2'], 'L1_gnn_W0': _L1_gnn_in['W0'], 'L1_gnn_b0': _L1_gnn_in['b0'], 'L1_gnn_W1': _L1_gnn_in['W1'], 'L1_gnn_b1': _L1_gnn_in['b1'], 'L1_ffn_Wr': _L1_ffn_in['Wr'], 'L1_ffn_br': _L1_ffn_in['br'], 'L1_ffn_ln_g': _L1_ffn_in['ln_g'], 'L1_ffn_ln_b': _L1_ffn_in['ln_b'], 'L1_ffn_W1': _L1_ffn_in['W1'], 'L1_ffn_b1': _L1_ffn_in['b1'], 'L1_ffn_W2': _L1_ffn_in['W2'], 'L1_ffn_b2': _L1_ffn_in['b2']}

def reference(x, src, dst, edge_type_8, L0_gnn_W, L0_gnn_att_src, L0_gnn_att_dst, L0_gnn_bias, L0_ffn_gate_w, L0_ffn_gate_b, L0_ffn_w1, L0_ffn_b1, L0_ffn_w2, L0_ffn_b2, L1_gnn_W0, L1_gnn_b0, L1_gnn_W1, L1_gnn_b1, L1_ffn_Wr, L1_ffn_br, L1_ffn_ln_g, L1_ffn_ln_b, L1_ffn_W1, L1_ffn_b1, L1_ffn_W2, L1_ffn_b2):
    import jax
    import jax.numpy as jnp

    def _L0_gnn_ref(x, edge_index, W, att_src, att_dst, bias):
        import jax, jax.numpy as jnp
        import numpy as np
        N_NODES = 50000
        N_EDGES = 25000
        F_IN = 256
        HEADS = 4
        C_OUT = 64
        NEG_SLOPE = 0.2
        N = x.shape[0]
        H, C = att_src.shape
        loops = jnp.arange(N, dtype=edge_index.dtype)
        src = jnp.concatenate([edge_index[0], loops])
        dst = jnp.concatenate([edge_index[1], loops])
        h = (x @ W.T).reshape(N, H, C)
        a_s = jnp.einsum('nhc,hc->nh', h, att_src)
        a_d = jnp.einsum('nhc,hc->nh', h, att_dst)
        e = jax.nn.leaky_relu(a_s[src] + a_d[dst], NEG_SLOPE)
        m = jax.ops.segment_max(e, dst, num_segments=N)
        m = jnp.where(jnp.isfinite(m), m, 0.0)
        p = jnp.exp(e - m[dst])
        denom = jax.ops.segment_sum(p, dst, num_segments=N)
        alpha = p / (denom[dst] + 1e-16)
        msg = alpha[:, :, None] * h[src]
        out = jax.ops.segment_sum(msg, dst, num_segments=N)
        out = out.reshape(N, H * C) + bias
        out = jax.nn.elu(out) + x
        return out

    def _L0_ffn_ref(h, gate_w, gate_b, w1, b1, w2, b2):
        import math
        import jax, jax.numpy as jnp
        import numpy as np
        CAPACITY_FACTOR = 1.25
        B, L, D = h.shape
        E = gate_w.shape[1]
        T = B * L
        C = max(1, math.ceil(CAPACITY_FACTOR * T / E))
        x = h.reshape(T, D)
        logits = x @ gate_w + gate_b
        probs = jax.nn.softmax(logits, axis=-1)
        idx = jnp.argmax(probs, axis=-1)
        prb = jnp.take_along_axis(probs, idx[:, None], axis=1)[:, 0]
        one_hot = jax.nn.one_hot(idx, E, dtype=jnp.float32)
        pos = (jnp.cumsum(one_hot, axis=0) * one_hot).sum(-1).astype(jnp.int32) - 1
        kept = pos < C
        pos_safe = jnp.where(kept, pos, C)
        buf = jnp.zeros((E, C, D), dtype=h.dtype).at[idx, pos_safe].set(x, mode='drop')
        hmid = jax.nn.relu(jnp.einsum('ecd,edf->ecf', buf, w1) + b1[:, None, :])
        ybuf = jnp.einsum('ecf,efd->ecd', hmid, w2) + b2[:, None, :]
        pos_g = jnp.minimum(pos, C - 1)
        y_tok = ybuf[idx, pos_g] * (prb * kept)[:, None]
        y = y_tok.reshape(B, L, D)
        y = jnp.nan_to_num(y, nan=0.0, posinf=10000.0, neginf=-10000.0)
        return y

    def _L1_gnn_ref(x, W0, b0, W1, b1, edge_index, edge_type):
        import jax, jax.numpy as jnp
        import numpy as np
        N_NODES = 50000
        N_EDGES = 25000
        N_REL = 8
        DIM = 256

        def _rgcn_layer(x, W, b, src, dst, edge_type, num_nodes):
            xt = jnp.einsum('ni,rio->rno', x, W)
            msg = jax.nn.relu(xt[edge_type, src] + b)
            return jax.ops.segment_sum(msg, dst, num_segments=num_nodes)
        src, dst = (edge_index[0], edge_index[1])
        h = _rgcn_layer(x, W0, b0, src, dst, edge_type, x.shape[0])
        h = _rgcn_layer(h, W1, b1, src, dst, edge_type, x.shape[0])
        return h

    def _L1_ffn_ref(x, Wr, br, ln_g, ln_b, W1, b1, W2, b2):
        import jax, jax.numpy as jnp
        import numpy as np
        TOP_K = 2
        LN_EPS = 1e-05
        B, S, D = x.shape
        N = B * S
        xt = x.reshape(N, D)
        logits = xt @ Wr + br
        probs = jax.nn.softmax(logits, axis=-1)
        top_p, top_idx = jax.lax.top_k(probs, TOP_K)
        weights = top_p / top_p.sum(axis=-1, keepdims=True)
        mu = xt.mean(axis=-1, keepdims=True)
        var = ((xt - mu) ** 2).mean(axis=-1, keepdims=True)
        xn = (xt - mu) * jax.lax.rsqrt(var + LN_EPS)
        xe = xn[None, :, :] * ln_g[:, None, :] + ln_b[:, None, :]
        h = jax.nn.gelu(jnp.einsum('end,edh->enh', xe, W1) + b1[:, None, :], approximate=False)
        y = jnp.einsum('enh,ehd->end', h, W2) + b2[:, None, :]
        y_tok = jnp.transpose(y, (1, 0, 2))
        sel = jnp.take_along_axis(y_tok, top_idx[:, :, None], axis=1)
        out = (weights[:, :, None] * sel).sum(axis=1)
        return out.reshape(B, S, D)
    edge_index = jnp.stack([src, dst])
    x = x + _L0_gnn_ref(_layernorm(x, axis=-1), edge_index, L0_gnn_W, L0_gnn_att_src, L0_gnn_att_dst, L0_gnn_bias)
    x = x + _L0_ffn_ref(_layernorm(x, axis=-1)[None], L0_ffn_gate_w, L0_ffn_gate_b, L0_ffn_w1, L0_ffn_b1, L0_ffn_w2, L0_ffn_b2)[0]
    x = x + _L1_gnn_ref(_layernorm(x, axis=-1), L1_gnn_W0, L1_gnn_b0, L1_gnn_W1, L1_gnn_b1, edge_index, edge_type_8)
    x = x + _L1_ffn_ref(_layernorm(x, axis=-1)[None], L1_ffn_Wr, L1_ffn_br, L1_ffn_ln_g, L1_ffn_ln_b, L1_ffn_W1, L1_ffn_b1, L1_ffn_W2, L1_ffn_b2)[0]
    return x

_drawn_inputs = setup_inputs


def setup_inputs(seed=0):
    import zlib

    import numpy as np

    out = dict(_drawn_inputs(seed))
    spreads = {'L0_gnn_bias': (0.0, 0.582),
     'L0_ffn_gate_b': (0.0, 0.8),
     'L0_ffn_b1': (0.0, 0.8),
     'L0_ffn_b2': (0.0, 0.8),
     'L1_gnn_b0': (0.0, 0.1),
     'L1_gnn_b1': (0.0, 0.556),
     'L1_ffn_br': (0.0, 0.8),
     'L1_ffn_ln_g': (1.0, 0.6),
     'L1_ffn_ln_b': (0.0, 0.8),
     'L1_ffn_b1': (0.0, 0.8),
     'L1_ffn_b2': (0.0, 0.8)}
    factors = {'L0_gnn_W': 5.122,
     'L0_gnn_att_src': 8.0,
     'L0_gnn_att_dst': 8.0,
     'L0_ffn_gate_w': 6.48,
     'L0_ffn_w1': 7.272,
     'L0_ffn_w2': 5.721,
     'L1_ffn_Wr': 8.0,
     'L1_ffn_W1': 7.318,
     'L1_ffn_W2': 6.659}
    for name, (base, spread) in spreads.items():
        noise = np.random.default_rng([zlib.crc32(name.encode()), seed]).standard_normal(out[name].shape)
        drawn = base * np.exp(spread * noise) if base else spread * noise
        out[name] = jnp.asarray(drawn.astype(out[name].dtype))
    for name, factor in factors.items():
        out[name] = (out[name] * factor).astype(out[name].dtype)
    return out
```

```python
import numpy as np
import concourse.bass as bass
from concourse import mybir
from contextlib import ExitStack

F32 = mybir.dt.float32
I32 = mybir.dt.int32
ALU = mybir.AluOpType
ACT = mybir.ActivationFunctionType
AX = mybir.AxisListType

P = 128
N = 3125
D = 256
KD = D // P
NT = -(-N // P)
NP = NT * P
LAST = N - (NT - 1) * P
HEADS, CH = 4, 64
E0 = 53125
T = 440
E = T * P
HALF = 10
RING = 2 * HALF
LANES, LC = 110, 4
EPAD = 128
WIN = P
AW = NP + WIN
HROW = D + 2 * HEADS
FILL_SRC = NP - 1
NREL = 8
FILL_TYPE = NREL
ZERO_ROW = NREL * NP
BIG = 1.0e30
NEG_SLOPE = 0.2
EPS = 1e-5
NE = 8
F = 1024
FC = F // P
CAP = -(-5 * N // (4 * NE))
B0 = 512
B1 = 256
NB1 = (2 * N + NE * (B1 - 1)) // B1
assert (T * P >= E0 + N) and CAP <= B0


class Places:
    pass


class Steps:

    def __init__(self, eng, sem):
        self.eng, self.sem, self.n = eng, sem, 0

    def __call__(self, ins):
        ins.then_inc(self.sem, 1)
        self.n = self.n + 1
        self.eng.wait_ge(self.sem, self.n)


def stage(nc, g, program, *args):
    taken = []

    def sem(name):
        taken.append(nc.alloc_semaphore(name=name))
        return taken[-1]

    g.sem = sem
    program(nc, g, *args)
    nc.clear_and_free_semaphores(taken)
    nc.all_engine_barrier()


def bcast(ap, axis, n):
    a = ap.unsqueeze(axis)
    shape = list(a.shape)
    shape[axis] = n
    return a.to_broadcast(shape)


def edges_stage(nc, g):
    with ExitStack() as ctx:
        fill = ctx.enter_context(nc.sbuf_tensor("fill", [1, 3, E - E0], I32))
        edge = ctx.enter_context(nc.sbuf_tensor("edge", [1, 2], I32))
        di = ctx.enter_context(nc.sbuf_tensor("di", [P, T], I32))
        dp = ctx.enter_context(nc.sbuf_tensor("dp", [P, T], I32))
        diff = ctx.enter_context(nc.sbuf_tensor("diff", [P, T], F32))
        b1 = ctx.enter_context(nc.sbuf_tensor("brk1", [P, T], F32))
        b2 = ctx.enter_context(nc.sbuf_tensor("brk2", [P, T], F32))
        bs = ctx.enter_context(nc.sbuf_tensor("brks", [P, 1], F32))
        tot = ctx.enter_context(nc.psum_tensor("brk_tot", [1, 1], F32))
        s_fill = g.sem("fill"); s_copy = g.sem("edge_copy"); s_load = g.sem("edge_load")
        s_chain = g.sem("edge_dve"); s_tot = g.sem("edge_tot"); s_sum = g.sem("edge_sum")
        block = ctx.enter_context(nc.Block())

        @block.gpsimd
        def _(pool):
            pool.memset(fill[:, 0, :], FILL_SRC).then_inc(s_fill, 1)
            pool.memset(fill[:, 1, :], N - 1).then_inc(s_fill, 1)
            pool.memset(fill[:, 2, :], FILL_TYPE).then_inc(s_fill, 1)
            pool.memset(edge[:, 0:1], -1).then_inc(s_fill, 1)
            pool.memset(edge[:, 1:2], N).then_inc(s_fill, 1)
            pool.iota(g.iota_i[:], [[1, P]], base=0, channel_multiplier=0).then_inc(s_fill, 1)
            pool.iota(g.iotap_i[:], [[0, P]], base=0, channel_multiplier=1).then_inc(s_fill, 1)
            pool.memset(g.ones[:], 1.0).then_inc(s_fill, 1)
            pool.memset(g.zrow[:], 0.0).then_inc(s_fill, 1)

        @block.sync
        def _(sp):
            for dram, a in ((g.S_src, g.src), (g.S_dst, g.dst), (g.S_typ, g.typ)):
                sp.dma_start(dram[EPAD:EPAD + E0].rearrange("(a b) -> a b", b=425),
                             a.rearrange("(a b) -> a b", b=425)).then_inc(s_copy, 16)
            sp.wait_ge(s_fill, 5)
            for k, dram in enumerate((g.S_src, g.S_dst, g.S_typ)):
                sp.dma_start(dram[EPAD + E0:EPAD + E].unsqueeze(0), fill[:, k, :]).then_inc(s_copy, 16)
            sp.dma_start(g.S_dst[EPAD - 1:EPAD].unsqueeze(0), edge[:, 0:1]).then_inc(s_copy, 16)
            sp.dma_start(g.S_dst[EPAD + E:EPAD + E + 1].unsqueeze(0), edge[:, 1:2]).then_inc(s_copy, 16)
            sp.wait_ge(s_copy, 8 * 16)
            sp.dma_start(di[:], g.S_dst[EPAD:EPAD + E].rearrange("(p j) -> p j", p=P)).then_inc(s_load, 16)
            sp.dma_start(dp[:], g.S_dst[EPAD - 1:EPAD - 1 + E].rearrange("(p j) -> p j", p=P)).then_inc(s_load, 16)

        @block.vector
        def _(dve):
            step = Steps(dve, s_chain)
            dve.wait_ge(s_fill, 9)
            dve.tensor_copy(g.iota[:], g.iota_i[:]).then_inc(s_fill, 1)
            step(dve.tensor_copy(g.iotap[:], g.iotap_i[:]))
            dve.wait_ge(s_fill, 10)
            step(dve.tensor_tensor(g.ident[:], g.iota[:], g.iotap[:], ALU.is_equal))
            step(dve.tensor_tensor(g.upper[:], g.iota[:], g.iotap[:], ALU.is_ge))
            step(dve.tensor_scalar(g.valid[:], g.iotap[:, 0:1], float(LAST), None, ALU.is_lt))
            dve.wait_ge(s_load, 32)
            step(dve.tensor_tensor(diff[:], di[:], dp[:], ALU.subtract))
            step(dve.tensor_scalar(b1[:], diff[:], 0.0, None, ALU.is_lt))
            step(dve.tensor_scalar(b2[:], diff[:], 1.0, None, ALU.is_gt))
            step(dve.tensor_tensor(b1[:], b1[:], b2[:], ALU.add))
            dve.tensor_reduce(bs[:], b1[:], AX.X, ALU.add).then_inc(s_sum, 1)
            dve.wait_ge(s_tot, 1)
            step(dve.tensor_copy(g.unsorted[:], tot[:]))

        @block.tensor
        def _(pe):
            pe.wait_ge(s_sum, 1)
            nc.tensor.matmul(tot[:], g.ones[:, 0:1], bs[:], start=True, stop=True).then_inc(s_tot, 1)


def sort_stage(nc, g):
    CH_E = 3520
    with ExitStack() as ctx:
        sb = lambda n, s, d: ctx.enter_context(nc.sbuf_tensor(n, s, d))
        node = sb("srt_node", [1, N], I32)
        rec = sb("srt_rec", [P, T, 4], I32)
        cols = sb("srt_cols", [P, 3, T], I32)
        dcol = sb("srt_dcol", [P, T], F32)
        ecol_i = sb("srt_ecol_i", [P, T], I32)
        ecol = sb("srt_ecol", [P, T], F32)
        rank = sb("srt_rank", [P, T], F32)
        rank_i = sb("srt_rank_i", [P, T], I32)
        row_i = sb("srt_row_i", [P, CH_E], I32)
        row = sb("srt_row", [P, CH_E], F32)
        place_i = sb("srt_place_i", [P, CH_E], I32)
        place = sb("srt_place", [P, CH_E], F32)
        before = sb("srt_before", [P, CH_E], F32)
        junk = sb("srt_junk", [P, CH_E], F32)
        lt = sb("srt_lt", [P, 1], F32)
        eq = sb("srt_eq", [P, 1], F32)
        idx1 = sb("srt_idx1", [P, 1], I32)
        rec1 = sb("srt_rec1", [P, 4], I32)
        s_io = g.sem("srt_iota"); s_dma = g.sem("srt_dma"); s_row = g.sem("srt_row")
        s_used = g.sem("srt_row_used"); s_rank = g.sem("srt_ranked"); s_st = g.sem("srt_staged")
        s_sc = g.sem("srt_scattered"); s_dve = g.sem("srt_dve"); s_out = g.sem("srt_out")
        s_sep = g.sem("srt_separate"); s_turn = g.sem("srt_turn")
        block = ctx.enter_context(nc.Block())
        arrays = (g.S_dst, g.S_src, g.S_typ)

        def flat(a):
            return a[EPAD:EPAD + E].rearrange("(p j) -> p j", p=P)

        @block.sync
        def _(sp):
            unsorted = sp.value_load(g.unsorted[0:1, 0:1], min_val=0, max_val=E)
            with sp.If(unsorted > 0):
                sp.wait_ge(s_io, 3)
                sp.dma_start(g.S_dst[EPAD + E0:EPAD + E0 + N].unsqueeze(0), node[:]).then_inc(s_dma, 16)
                sp.wait_ge(s_dma, 16)
                for k, a in enumerate(arrays):
                    sp.dma_start(cols[:, k, :], flat(a)).then_inc(s_dma, 16)
                with sp.Fori(0, E // CH_E) as c:
                    sp.wait_ge(s_used, c + 1)
                    sp.dma_start(row_i[:], g.S_dst[bass.ds(c * CH_E + EPAD, CH_E)].partition_broadcast(P)).then_inc(s_row, 16)
                sp.wait_ge(s_sc, 16 * T)
                sp.dma_start(rec[:], g.S_rec.rearrange("(p j) w -> p j w", p=P)).then_inc(s_out, 16)
                sp.wait_ge(s_sep, 1)
                for k, a in enumerate(arrays):
                    sp.dma_start(flat(a), cols[:, k, :]).then_inc(s_out, 16)
                sp.wait_ge(s_out, 64)

        @block.gpsimd
        def _(pool):
            unsorted = pool.value_load(g.unsorted[0:1, 0:1], min_val=0, max_val=E)
            with pool.If(unsorted > 0):
                pool.iota(node[:], [[1, N]], base=0, channel_multiplier=0).then_inc(s_io, 1)
                pool.iota(ecol_i[:], [[1, T]], base=0, channel_multiplier=T).then_inc(s_io, 1)
                pool.iota(place_i[:], [[1, CH_E]], base=0, channel_multiplier=0).then_inc(s_io, 1)
                pool.wait_ge(s_rank, 1)
                with pool.Fori(0, T) as j:
                    pool.tensor_copy(idx1[:], rank_i[:, bass.ds(j, 1)]).then_inc(s_st, 1)
                    pool.tensor_copy(rec1[:], rec[:, bass.ds(j, 1), :].rearrange("p a w -> p (a w)")).then_inc(s_st, 1)
                    pool.wait_ge(s_st, 2 * j + 2)
                    pool.sem_inc(s_turn, 1)
                    pool.indirect_dma_start(g.S_rec, bass.IndirectOffsetOnAxis(idx1[:], axis=0), rec1[:], None).then_inc(s_sc, 16)
                    pool.wait_ge(s_sc, 16 * j + 16)

        @block.vector
        def _(dve):
            unsorted = dve.value_load(g.unsorted[0:1, 0:1], min_val=0, max_val=E)
            with dve.If(unsorted > 0):
                step = Steps(dve, s_dve)
                dve.wait_ge(s_io, 3)
                dve.wait_ge(s_dma, 64)
                step(dve.memset(rec[:], 0))
                for k in range(3):
                    step(dve.tensor_copy(rec[:, :, k], cols[:, k, :]))
                step(dve.tensor_copy(dcol[:], cols[:, 0, :]))
                step(dve.tensor_copy(ecol[:], ecol_i[:]))
                step(dve.tensor_copy(place[:], place_i[:]))
                step(dve.memset(rank[:], 0.0))
                dve.sem_inc(s_used, 1)
                n0 = step.n
                per = 2 + 5 * T
                with dve.Fori(0, E // CH_E) as c:
                    step.n = n0 + c * per
                    dve.wait_ge(s_row, 16 * c + 16)
                    step(dve.tensor_copy(row[:], row_i[:]))
                    dve.sem_inc(s_used, 1)
                    n1 = step.n
                    with dve.Fori(0, T) as j:
                        step.n = n1 + j * 5
                        d1, e1, r1 = (x[:, bass.ds(j, 1)] for x in (dcol, ecol, rank))
                        step(dve.tensor_scalar(before[:], place[:], e1, None, ALU.is_lt))
                        dve.scalar_tensor_tensor(junk[:], row[:], d1, before[:], ALU.is_equal, ALU.mult, accum_out=eq[:]).then_inc(s_dve, 1)
                        dve.wait_ge(s_dve, step.n + 1)
                        dve.tensor_scalar(junk[:], row[:], d1, 0.0, ALU.is_lt, ALU.add, accum_out=lt[:]).then_inc(s_dve, 1)
                        step.n = step.n + 2
                        dve.wait_ge(s_dve, step.n)
                        step(dve.tensor_tensor(r1, r1, lt[:], ALU.add))
                        step(dve.tensor_tensor(r1, r1, eq[:], ALU.add))
                    step.n = n1 + 5 * T
                    step(dve.tensor_scalar(ecol[:], ecol[:], float(CH_E), None, ALU.subtract))
                dve.tensor_copy(rank_i[:], rank[:]).then_inc(s_rank, 1)
                dve.wait_ge(s_out, 16)
                for k in range(3):
                    ins = dve.tensor_copy(cols[:, k, :], rec[:, :, k])
                ins.then_inc(s_sep, 1)


def tables_stage(nc, g):
    with ExitStack() as ctx:
        sb = lambda n, s, d: ctx.enter_context(nc.sbuf_tensor(n, s, d))
        lane_i = sb("lane_i", [LANES, 3, LC, P], I32)
        prev_i = sb("prev_i", [LANES, 2, LC, P], I32)
        lane = sb("lane", [LANES, 3, LC, P], F32)
        dstT = sb("dstT", [P, T], F32)
        ps = [ctx.enter_context(nc.psum_tensor(f"tab_ps{k}", [P, 512], F32)) for k in range(4)]
        s_ld = g.sem("tab_load"); s_dve = g.sem("tab_dve"); s_lane = g.sem("tab_lane")
        s_tr = g.sem("tab_tr"); s_dT = g.sem("tab_dT"); s_base = g.sem("tab_base")
        block = ctx.enter_context(nc.Block())

        def lanes(a, shift=0):
            return a[EPAD + shift:EPAD + shift + E].rearrange("(c q f) -> q c f", c=LC, f=P)

        @block.sync
        def _(sp):
            for k, a in enumerate((g.S_dst, g.S_src, g.S_typ)):
                sp.dma_start(lane_i[:, k], lanes(a)).then_inc(s_ld, 16)
            sp.dma_start(prev_i[:, 0], lanes(g.S_dst, -1)).then_inc(s_ld, 16)
            sp.dma_start(prev_i[:, 1], lanes(g.S_dst, 1)).then_inc(s_ld, 16)

        @block.vector
        def _(dve):
            step = Steps(dve, s_dve)
            dve.wait_ge(s_ld, 80)
            step(dve.tensor_copy(lane[:], lane_i[:]))
            step(dve.scalar_tensor_tensor(lane[:, 2], lane[:, 2], float(NP), lane[:, 1], ALU.mult, ALU.add))
            step(dve.tensor_scalar(lane[:, 2], lane[:, 2], float(ZERO_ROW), None, ALU.min))
            step(dve.tensor_tensor(g.first[:], lane[:, 0], prev_i[:, 0], ALU.not_equal))
            dve.tensor_tensor(g.endneg[:], lane[:, 0], prev_i[:, 1], ALU.not_equal).then_inc(s_lane, 1)
            step(dve.tensor_scalar(g.firstneg[:], g.first[:], -BIG, None, ALU.mult))
            dve.wait_ge(s_lane, 1)
            step(dve.tensor_scalar(g.endneg[:], g.endneg[:], -BIG, None, ALU.mult))
            dve.memset(g.srcI[:, T:], 0).then_inc(s_dve, 1)
            dve.memset(g.relI[:, T:], 0).then_inc(s_dve, 1)
            dve.memset(g.dstI[:, T:], 0).then_inc(s_dve, 1)
            step.n += 3
            step(dve.memset(g.dstrel[:, T:], 0.0))
            dve.wait_ge(s_tr, 1)
            dve.tensor_copy(dstT[:], ps[0][:, 0:T]).then_inc(s_dT, 1)
            step(dve.tensor_copy(g.dstI[:, 0:T], ps[0][:, 0:T]))
            dve.wait_ge(s_tr, 2)
            step(dve.tensor_copy(g.srcI[:, 0:T], ps[1][:, 0:T]))
            dve.wait_ge(s_tr, 3)
            step(dve.tensor_copy(g.relI[:, 0:T], ps[2][:, 0:T]))
            dve.wait_ge(s_base, 1)
            step(dve.tensor_tensor(g.dstrel[:, 0:T], dstT[:], ps[3][:, 0:T], ALU.subtract))
            step(dve.tensor_copy(g.base[:], ps[3][0:1, 0:T]))

        @block.tensor
        def _(pe):
            pe.wait_ge(s_lane, 1)
            for k in range(3):
                for c in range(LC):
                    ins = nc.tensor.transpose(ps[k][:, c * LANES:(c + 1) * LANES], lane[:, k, c, :], g.ident[0:LANES, 0:LANES])
                ins.then_inc(s_tr, 1)
            pe.wait_ge(s_dT, 1)
            nc.tensor.matmul(ps[3][:, 0:T], g.ones[0:1, :], dstT[0:1, :], start=True, stop=True).then_inc(s_base, 1)


def layernorm(nc, g, dve, step, s_var, s_sqrt, k, src, dst):
    st, mean, var, r, t1, t2 = g.ln_st, g.ln_mean, g.ln_var, g.ln_r, g.ln_t1, g.ln_t2
    n0 = step.n
    with dve.Fori(0, NT) as t:
        nc.vector.bn_stats(st[:, bass.ds(t, 1), :].rearrange("p a w -> p (a w)"),
                           src[:, bass.ds(t, 1), :].rearrange("p a w -> p (a w)")).then_inc(step.sem, 1)
    step.n = n0 + NT
    dve.wait_ge(step.sem, step.n)
    step(dve.tensor_tensor(mean[:], st[:, :, 1], st[:, :, 4], ALU.add))
    step(dve.tensor_scalar(mean[:], mean[:], 0.5, None, ALU.mult))
    step(dve.tensor_tensor(t1[:], st[:, :, 1], st[:, :, 4], ALU.subtract))
    step(dve.tensor_tensor(t1[:], t1[:], t1[:], ALU.mult))
    step(dve.tensor_tensor(t2[:], st[:, :, 2], st[:, :, 5], ALU.add))
    step(dve.scalar_tensor_tensor(t1[:], t1[:], float(D) / 4, t2[:], ALU.mult, ALU.add))
    step(dve.tensor_scalar(var[:], t1[:], 1.0 / D, EPS, ALU.mult, ALU.add))
    dve.sem_inc(s_var, 1)
    dve.wait_ge(s_sqrt, k)
    step(dve.reciprocal(r[:], g.ln_s[:]))
    step(dve.tensor_tensor(t1[:], r[:], r[:], ALU.mult))
    step(dve.tensor_tensor(t1[:], t1[:], var[:], ALU.mult))
    step(dve.tensor_scalar(t1[:], t1[:], -0.5, 1.5, ALU.mult, ALU.add))
    step(dve.tensor_tensor(r[:], r[:], t1[:], ALU.mult))
    n0 = step.n
    with dve.Fori(0, NT) as t:
        nc.vector.tensor_scalar(dst[:, bass.ds(t, 1), :].rearrange("p a w -> p (a w)"),
                                src[:, bass.ds(t, 1), :].rearrange("p a w -> p (a w)"),
                                mean[:, bass.ds(t, 1)], r[:, bass.ds(t, 1)], ALU.subtract, ALU.mult).then_inc(step.sem, 1)
    step.n = n0 + NT
    dve.wait_ge(step.sem, step.n)


def gat_table_stage(nc, g):
    with ExitStack() as ctx:
        sb = lambda n, s, d: ctx.enter_context(nc.sbuf_tensor(n, s, d))
        w = sb("gat_w", [P, KD, D], F32)
        attT = sb("gat_attT", [8, P], F32)
        att = sb("gat_att", [P, KD, 8], F32)
        attc = sb("gat_attc", [P, 4], F32)
        wt = sb("gat_wt", [P, KD, HROW], F32)
        xT = sb("gat_xT", [P, 2, KD, P], F32)
        hst = sb("gat_hst", [P, 2, HROW], F32)
        pads = sb("gat_pads", [P, 1], F32)
        ps_t = [ctx.enter_context(nc.psum_tensor(f"gt_t{k}", [P, 512], F32)) for k in range(2)]
        ps_h = [ctx.enter_context(nc.psum_tensor(f"gt_h{k}", [P, 512], F32)) for k in range(2)]
        ps_w = ctx.enter_context(nc.psum_tensor("gt_w", [P, 512], F32))
        s_ld = g.sem("gt_load"); s_x = g.sem("gt_x"); s_dve = g.sem("gt_dve"); s_act = g.sem("gt_act"); s_var = g.sem("gt_var")
        s_z = g.sem("gt_zero"); s_ln = g.sem("gt_ln"); s_tr = g.sem("gt_tr"); s_xT = g.sem("gt_xT")
        s_h = g.sem("gt_h"); s_hst = g.sem("gt_hst"); s_w = g.sem("gt_wtr"); s_wt = g.sem("gt_wt"); s_att = g.sem("gt_att")
        s_st = [g.sem("gt_store0"), g.sem("gt_store1")]
        s_a = g.sem("gt_attT"); s_wa = g.sem("gt_wa"); s_zr = g.sem("gt_zr")
        block = ctx.enter_context(nc.Block())

        @block.sync
        def _(sp):
            sp.wait_ge(s_z, 1)
            sp.dma_start(g.X[:, 0:NT - 1, :], g.x[0:(NT - 1) * P, :].rearrange("(t p) d -> p t d", p=P)).then_inc(s_x, 16)
            sp.dma_start(g.X[0:LAST, NT - 1, :], g.x[(NT - 1) * P:N, :]).then_inc(s_x, 16)
            sp.dma_start(w[:], g.gat_w.rearrange("(k p) i -> p k i", p=P)).then_inc(s_ld, 16)
            sp.dma_start(attT[0:2, :], g.att_src.rearrange("(k h) c -> k (h c)", k=KD)).then_inc(s_ld, 16)
            sp.dma_start(attT[2:4, :], g.att_dst.rearrange("(k h) c -> k (h c)", k=KD)).then_inc(s_ld, 16)
            sp.dma_start(g.Gtab[ZERO_ROW:ZERO_ROW + 1, :], g.zrow[0:1, 0:D]).then_inc(s_zr, 16)
            for t in range(NT):
                sp.wait_ge(s_hst, t + 1)
                sp.dma_start(g.Htab[t * P:(t + 1) * P, :], hst[:, t % 2, :]).then_inc(s_st[t % 2], 16)
                sp.dma_start(g.Atab[t * P:(t + 1) * P, :], hst[:, t % 2, D:HROW]).then_inc(s_st[t % 2], 16)
            sp.wait_ge(s_st[0], 32 * ((NT + 1) // 2))
            sp.wait_ge(s_st[1], 32 * (NT // 2))
            sp.wait_ge(s_zr, 16)

        @block.vector
        def _(dve):
            step = Steps(dve, s_dve)
            dve.memset(g.X[:, NT - 1, :], 0.0).then_inc(s_z, 1)
            step(dve.memset(att[:], 0.0))
            dve.wait_ge(s_a, 1)
            for k in range(KD):
                for h in range(2):
                    sl = slice(h * CH, (h + 1) * CH)
                    dve.tensor_copy(att[sl, k, 2 * k + h:2 * k + h + 1], ps_w[sl, k:k + 1])
                    ins = dve.tensor_copy(att[sl, k, 4 + 2 * k + h:5 + 2 * k + h], ps_w[sl, 2 + k:3 + k])
            ins.then_inc(s_att, 1)
            dve.wait_ge(s_x, 32)
            layernorm(nc, g, dve, step, s_var, s_act, 1, g.X, g.Y)
            dve.sem_inc(s_ln, 1)
            step(dve.tensor_scalar(pads[:], g.valid[:], 1.0, BIG, ALU.subtract, ALU.mult))
            for t in range(NT):
                dve.wait_ge(s_h, t + 1)
                if t >= 2:
                    dve.wait_ge(s_st[t % 2], 32 * (t // 2))
                if t < NT - 1:
                    dve.tensor_copy(hst[:, t % 2, :], ps_h[t % 2][:, 0:HROW]).then_inc(s_hst, 1)
                else:
                    step(dve.tensor_copy(hst[:, t % 2, :], ps_h[t % 2][:, 0:HROW]))
                    dve.tensor_scalar(hst[:, t % 2, D:D + HEADS], ps_h[t % 2][:, D:D + HEADS], pads[:], None, ALU.add).then_inc(s_hst, 1)

        @block.scalar
        def _(act):
            act.wait_ge(s_w, 1)
            for j in range(KD):
                ins = nc.scalar.activation(wt[:, j, 0:D], ps_t[j][:, 0:D], ACT.Copy)
            ins.then_inc(s_wt, 1)
            act.wait_ge(s_wa, 1)
            nc.scalar.activation(wt[:, :, D:HROW], ps_w[:, 16:16 + KD * 8].rearrange("p (k a) -> p k a", k=KD), ACT.Copy).then_inc(s_wt, 1)
            act.wait_ge(s_var, 1)
            nc.scalar.activation(g.ln_s[:], g.ln_var[:], ACT.Sqrt).then_inc(s_act, 1)
            for t in range(NT):
                act.wait_ge(s_tr, t + 1)
                if t >= 2:
                    act.wait_ge(s_h, t - 1)
                nc.scalar.activation(xT[:, t % 2], ps_t[t % 2][:, 0:D].rearrange("p (k n) -> p k n", k=KD), ACT.Copy).then_inc(s_xT, 1)

        @block.tensor
        def _(pe):
            pe.wait_ge(s_ld, 48)
            nc.tensor.transpose(ps_w[:, 0:4], attT[0:4, :], g.ident[0:4, 0:4]).then_inc(s_a, 1)
            for j in range(KD):
                for k in range(KD):
                    ins = nc.tensor.transpose(ps_t[j][:, k * P:(k + 1) * P], w[:, k, j * P:(j + 1) * P], g.ident[:])
            ins.then_inc(s_w, 1)
            pe.wait_ge(s_att, 1)
            for j in range(KD):
                for k in range(KD):
                    ins = nc.tensor.matmul(ps_w[:, 16 + j * 8:24 + j * 8], w[:, k, j * P:(j + 1) * P], att[:, k, :], start=(k == 0), stop=(k == KD - 1))
            ins.then_inc(s_wa, 1)
            pe.wait_ge(s_wt, 2)
            pe.wait_ge(s_ln, 1)

            def transposes(t):
                if t >= 2:
                    pe.wait_ge(s_xT, t - 1)
                for k in range(KD):
                    ins = nc.tensor.transpose(ps_t[t % 2][:, k * P:(k + 1) * P], g.Y[:, t, k * P:(k + 1) * P], g.ident[:])
                ins.then_inc(s_tr, 1)

            transposes(0)
            for t in range(NT):
                if t + 1 < NT:
                    transposes(t + 1)
                pe.wait_ge(s_xT, t + 1)
                if t >= 2:
                    pe.wait_ge(s_hst, t - 1)
                for k in range(KD):
                    ins = nc.tensor.matmul(ps_h[t % 2][:, 0:HROW], xT[:, t % 2, k, :], wt[:, k, :], start=(k == 0), stop=(k == KD - 1))
                ins.then_inc(s_h, 1)


def scores_stage(nc, g):
    with ExitStack() as ctx:
        sb = lambda n, s, d: ctx.enter_context(nc.sbuf_tensor(n, s, d))
        G = 20
        H = G // 2
        ixs = sb("sc_ixs", [P, 2, 2, H], I32)
        rs = sb("sc_rs", [P, G, 2, 8], F32)
        s_ix = g.sem("sc_idx"); s_turn = g.sem("sc_turn"); s_use = g.sem("sc_used")
        s_g = [g.sem(f"sc_g{k}") for k in range(2)]
        block = ctx.enter_context(nc.Block())
        atab = g.Htab

        @block.gpsimd
        def _(pool):
            with pool.Fori(0, T // G) as i:
                for h in range(2):
                    pool.wait_ge(s_use, 2 * i + h + 1)
                    pool.sem_inc(s_turn, 1)
                    pool.tensor_copy(ixs[:, h, 0, :], g.srcI[:, bass.ds(i * G + h * H, H)]).then_inc(s_ix, 1)
                    pool.tensor_copy(ixs[:, h, 1, :], g.dstI[:, bass.ds(i * G + h * H, H)]).then_inc(s_ix, 1)
                    pool.wait_ge(s_ix, 4 * i + 2 * h + 2)
                    pool.sem_inc(s_turn, 1)
                    for k in range(H):
                        for w in range(2):
                            pool.indirect_dma_start(rs[:, h * H + k, w, :], None, g.Atab, bass.IndirectOffsetOnAxis(ixs[:, h, w, k:k + 1], axis=0)).then_inc(s_g[h], 16)

        @block.vector
        def _(dve):
            dve.sem_inc(s_use, 2)
            with dve.Fori(0, T // G) as i:
                for h in range(2):
                    dve.wait_ge(s_g[h], (i + 1) * (16 * 2 * H))
                    dve.tensor_copy(g.AS[:, bass.ds(i * G + h * H, H), 0:4], rs[:, h * H:(h + 1) * H, 0, 0:4])
                    dve.tensor_copy(g.AS[:, bass.ds(i * G + h * H, H), 4:12], rs[:, h * H:(h + 1) * H, 1, :]).then_inc(s_use, 1)


def softmax_stage(nc, g):
    with ExitStack() as ctx:
        sb = lambda n, s, d: ctx.enter_context(nc.sbuf_tensor(n, s, d))
        L = sb("sm_L", [LANES, 12, LC, P], F32)
        fw = sb("sm_fw", [LANES, HEADS, LC, P], F32)
        bw = sb("sm_bw", [LANES, HEADS, LC, P], F32)
        tails = sb("sm_tails", [LANES, 2, LC, 8], F32)
        rowt = sb("sm_rowt", [HEADS, 2, 2, T], F32)
        inc = sb("sm_inc", [HEADS, 2, T + 1], F32)
        carry = sb("sm_carry", [LANES, 2, LC, HEADS], F32)
        notfirst = sb("sm_notfirst", [LANES, LC, P], F32)
        pe_out = sb("sm_p", [LANES, 8, LC, P], F32)
        ps = [ctx.enter_context(nc.psum_tensor(f"sm_ps{k}", [P, 512], F32)) for k in range(4)]
        ps_r = [ctx.enter_context(nc.psum_tensor(f"sm_row{k}", [HEADS, 512], F32)) for k in range(4)]
        s_tr = g.sem("sm_tr"); s_L = g.sem("sm_L"); s_dve = g.sem("sm_dve"); s_tail = g.sem("sm_tail")
        s_row = g.sem("sm_row"); s_inc = g.sem("sm_inc"); s_car = g.sem("sm_carry")
        s_z = g.sem("sm_z"); s_p = g.sem("sm_pe"); s_pt = g.sem("sm_pt"); s_cp = g.sem("sm_cp")
        block = ctx.enter_context(nc.Block())

        @block.tensor
        def _(pe):
            for a in range(12):
                if a >= 4:
                    pe.wait_ge(s_L, a - 3)
                for c in range(LC):
                    ins = nc.tensor.transpose(ps[a % 4][0:LANES, c * P:(c + 1) * P], g.AS[:, c * LANES:(c + 1) * LANES, a], g.ident[:])
                ins.then_inc(s_tr, 1)
            pe.wait_ge(s_tail, 1)
            for d in range(2):
                for w in range(2):
                    for c in range(LC):
                        ins = nc.tensor.transpose(ps_r[d * 2 + w][:, c * LANES:(c + 1) * LANES], tails[:, d, c, 4 * w:4 * w + 4], g.ident[0:LANES, 0:LANES])
            ins.then_inc(s_row, 1)
            pe.wait_ge(s_inc, 1)
            for d in range(2):
                for c in range(LC):
                    src = inc[:, 0, c * LANES:(c + 1) * LANES] if d == 0 else inc[:, 1, c * LANES + 1:(c + 1) * LANES + 1]
                    ins = nc.tensor.transpose(ps[0][0:LANES, (d * LC + c) * 4:(d * LC + c) * 4 + 4], src, g.ident[0:HEADS, 0:HEADS])
            ins.then_inc(s_car, 1)
            for a in range(8):
                pe.wait_ge(s_p, a + 1)
                if a >= 4:
                    pe.wait_ge(s_pt, a - 3)
                for c in range(LC):
                    ins = nc.tensor.transpose(ps[a % 4][:, c * LANES:(c + 1) * LANES], pe_out[:, a, c, :], g.ident[0:LANES, 0:LANES])
                ins.then_inc(s_cp, 1)

        @block.scalar
        def _(act):
            for a in range(12):
                act.wait_ge(s_tr, a + 1)
                nc.scalar.activation(L[:, a], ps[a % 4][0:LANES, :].rearrange("p (c f) -> p c f", c=LC), ACT.Copy).then_inc(s_L, 1)
            for a in range(8):
                act.wait_ge(s_z, a + 1)
                nc.scalar.activation(pe_out[:, a], pe_out[:, a], ACT.Exp).then_inc(s_p, 1)

        @block.vector
        def _(dve):
            step = Steps(dve, s_dve)
            step(dve.tensor_scalar(notfirst[:], g.first[:], 1.0, BIG, ALU.subtract, ALU.mult))
            dve.wait_ge(s_L, 12)

            def scan(out, d, c, h, initial):
                v, m = L[:, h, c, :], (g.firstneg if d == 0 else g.endneg)[:, c, :]
                o = out[:, h, c, :]
                if d:
                    v, m, o = v[:, ::-1], m[:, ::-1], o[:, ::-1]
                return dve.tensor_tensor_scan(o, m, v, initial, ALU.add, ALU.max)

            n = 0
            for d, out in ((0, fw), (1, bw)):
                for h in range(HEADS):
                    for c in range(LC):
                        scan(out, d, c, h, -BIG).then_inc(s_dve, 1)
                        n += 1
            step.n = step.n + n
            dve.wait_ge(s_dve, step.n)
            dve.tensor_copy(tails[:, 0, :, 0:4].rearrange("q c h -> q h c"), fw[:, :, :, P - 1])
            step(dve.tensor_copy(tails[:, 1, :, 0:4].rearrange("q c h -> q h c"), bw[:, :, :, 0]))
            step(dve.tensor_reduce(tails[:, 0, :, 4], g.firstneg[:], AX.X, ALU.min))
            step(dve.tensor_reduce(tails[:, 1, :, 4], g.endneg[:], AX.X, ALU.min))
            dve.tensor_copy(tails[:, 0, :, 5:8], bcast(tails[:, 0, :, 4], 2, 3))
            step(dve.tensor_copy(tails[:, 1, :, 5:8], bcast(tails[:, 1, :, 4], 2, 3)))
            dve.sem_inc(s_tail, 1)
            dve.memset(inc[:, 0, 0:1], -BIG)
            step(dve.memset(inc[:, 1, T:T + 1], -BIG))
            dve.wait_ge(s_row, 1)
            for d in range(2):
                for w in range(2):
                    step(dve.tensor_copy(rowt[:, d, w, :], ps_r[d * 2 + w][:, 0:T]))
            dve.tensor_tensor_scan(inc[:, 0, 1:T + 1], rowt[:, 0, 1, :], rowt[:, 0, 0, :], -BIG, ALU.add, ALU.max)
            step(dve.tensor_tensor_scan(inc[:, 1, 0:T][:, ::-1], rowt[:, 1, 1, :][:, ::-1], rowt[:, 1, 0, :][:, ::-1], -BIG, ALU.add, ALU.max))
            dve.sem_inc(s_inc, 1)
            dve.wait_ge(s_car, 1)
            step(dve.tensor_copy(carry[:], ps[0][0:LANES, 0:2 * LC * 4].rearrange("p (d c h) -> p d c h", d=2, c=LC)))
            for d, out in ((0, fw), (1, bw)):
                for h in range(HEADS):
                    for c in range(LC):
                        scan(out, d, c, h, carry[:, d, c, h:h + 1]).then_inc(s_dve, 1)
                        step.n += 1
            dve.wait_ge(s_dve, step.n)
            f2 = lambda ap: ap.rearrange("q h c f -> q (h c f)")
            a_s, a_sd, a_d = f2(L[:, 0:4]), f2(L[:, 4:8]), f2(L[:, 8:12])
            M, B = f2(fw[:]), f2(bw[:])
            step(dve.tensor_tensor(M, M, B, ALU.max))
            step(dve.tensor_tensor(M, M, a_sd, ALU.max))
            step(dve.tensor_tensor(M, M, a_d, ALU.add))
            step(dve.scalar_tensor_tensor(M, M, NEG_SLOPE, M, ALU.mult, ALU.max))
            for w, a in ((0, a_s), (1, a_sd)):
                z = f2(pe_out[:, 4 * w:4 * w + 4])
                step(dve.tensor_tensor(z, a, a_d, ALU.add))
                step(dve.scalar_tensor_tensor(z, z, NEG_SLOPE, z, ALU.mult, ALU.max))
                step(dve.tensor_tensor(z, z, M, ALU.subtract))
                if w == 1:
                    step(dve.tensor_tensor(pe_out[:, 4:8], pe_out[:, 4:8], bcast(notfirst[:], 1, HEADS), ALU.add))
                dve.sem_inc(s_z, 4)
            dve.wait_ge(s_p, 8)
            for a in range(8):
                dve.wait_ge(s_cp, a + 1)
                dve.tensor_copy(g.PT[:, 0:T, a], ps[a % 4][:, 0:T]).then_inc(s_pt, 1)


def edge_pass(nc, g, kind, table, index, n_pass):
    gat = kind == "gat"
    width = HROW if gat else D
    with ExitStack() as ctx:
        sb = lambda n, s, d: ctx.enter_context(nc.sbuf_tensor(n, s, d))
        ix = sb(f"ix{n_pass}", [P, 2, HALF], I32)
        ring = sb(f"ring{n_pass}", [P, RING, HROW], F32)
        hot = sb(f"hot{n_pass}", [P, 2, HALF, WIN], F32)
        NBK = 4
        ps = [ctx.enter_context(nc.psum_tensor(f"ep{n_pass}_{k}", [P, 512], F32)) for k in range(NBK)]
        s_ix = g.sem(f"ep_idx{n_pass}"); s_turn = g.sem(f"ep_turn{n_pass}")
        s_g = [g.sem(f"ep_g{n_pass}_{k}") for k in range(RING)]
        s_hot = g.sem(f"ep_hot{n_pass}"); s_msg = g.sem(f"ep_msg{n_pass}")
        s_mm = g.sem(f"ep_mm{n_pass}"); s_acc = g.sem(f"ep_acc{n_pass}"); s_dve = g.sem(f"ep_dve{n_pass}")
        s_half = g.sem(f"ep_half{n_pass}")
        block = ctx.enter_context(nc.Block())

        @block.gpsimd
        def _(pool):
            with pool.Fori(0, T // RING) as i:
                for h in range(2):
                    pool.wait_ge(s_half, 2 * i + h + 1)
                    pool.sem_inc(s_turn, 1)
                    pool.tensor_copy(ix[:, h, :], index[:, bass.ds(i * RING + h * HALF, HALF)]).then_inc(s_ix, 1)
                    pool.wait_ge(s_ix, 2 * i + h + 1)
                    pool.sem_inc(s_turn, 1)
                    for k in range(HALF):
                        pool.indirect_dma_start(ring[:, h * HALF + k, 0:width], None, table,
                                                bass.IndirectOffsetOnAxis(ix[:, h, k:k + 1], axis=0)).then_inc(s_g[h * HALF + k], 16)

        @block.tensor
        def _(pe):
            pe.sem_inc(s_half, 2)
            with pe.Fori(0, T // RING) as i:
                for h in range(2):
                    pe.wait_ge(s_hot, 2 * i + h + 1)
                    if gat:
                        pe.wait_ge(s_msg, 2 * i + h + 1)
                    for k in range(HALF):
                        slot = h * HALF + k
                        if not gat:
                            pe.wait_ge(s_g[slot], 16 * i + 16)
                        pe.wait_ge(s_acc, i * RING + (slot + 1))
                        b = ps[slot % NBK]
                        for j in range(KD):
                            ins = nc.tensor.matmul(b[:, j * WIN:(j + 1) * WIN], ring[:, slot, j * P:(j + 1) * P], hot[:, h, k, :], start=True, stop=True)
                        if gat:
                            ins = nc.tensor.matmul(b[0:8, KD * WIN:(KD + 1) * WIN], ring[:, slot, D:D + 8], hot[:, h, k, :], start=True, stop=True)
                        ins.then_inc(s_mm, 1)

        @block.vector
        def _(dve):
            dve.memset(g.ACC[:], 0.0).then_inc(s_dve, 1)
            if gat:
                dve.memset(g.DEN[:], 0.0).then_inc(s_dve, 1)
            dve.wait_ge(s_dve, 2 if gat else 1)
            dve.sem_inc(s_acc, NBK)

            def build(h, first):
                ins = dve.tensor_tensor(hot[:, h], bcast(g.iota[:], 1, HALF),
                                        bcast(g.dstrel[:, bass.ds(first, HALF)], 2, WIN), ALU.is_equal)
                ins.then_inc(s_hot, 1)

            def weigh(h, first, r):
                for k in range(HALF):
                    dve.wait_ge(s_g[h * HALF + k], r)
                rows = ring[:, h * HALF:(h + 1) * HALF, 0:D].rearrange("p k (a c) -> p k a c", a=HEADS)
                dve.tensor_tensor(rows, rows, bcast(g.PT[:, bass.ds(first, HALF), 0:4], 3, CH), ALU.mult)
                dve.tensor_copy(ring[:, h * HALF:(h + 1) * HALF, D:D + 8], g.PT[:, bass.ds(first, HALF), :]).then_inc(s_msg, 1)

            build(0, 0)
            if gat:
                weigh(0, 0, 16)

            def round_(i, last=False):
                for h in range(2):
                    first = i * RING + (h + 1) * HALF
                    more = not (last and h == 1)
                    if more:
                        build(1 - h, first)
                    for k in range(HALF):
                        slot = h * HALF + k
                        tile = i * RING + slot
                        start = dve.value_load(g.base[0:1, bass.ds(tile, 1)], min_val=0, max_val=N - 1)
                        dve.wait_ge(s_mm, tile + 1)
                        b = ps[slot % NBK]
                        acc = g.ACC[:, :, bass.ds(start, WIN)]
                        dve.wait_ge(s_acc, tile + NBK)
                        ins = dve.tensor_tensor(acc, acc, b[:, 0:KD * WIN].rearrange("p (j w) -> p j w", j=KD), ALU.add)
                        if gat:
                            den = g.DEN[:, bass.ds(start, WIN)]
                            ins = dve.tensor_tensor(den, den, b[0:8, KD * WIN:(KD + 1) * WIN], ALU.add)
                        ins.then_inc(s_acc, 1)
                    dve.sem_inc(s_half, 1)
                    if gat and more:
                        weigh(1 - h, first, 16 * i + 16 * (h + 1))

            with dve.Fori(0, T // RING - 1) as i:
                round_(i)
            round_(T // RING - 1, last=True)


def gat_finish_stage(nc, g):
    with ExitStack() as ctx:
        sb = lambda n, s, d: ctx.enter_context(nc.sbuf_tensor(n, s, d))
        Hs = sb("gf_h", [P, NT, D], F32)
        den8 = sb("gf_den8", [P, NT, 8], F32)
        den = sb("gf_den", [P, NT, HEADS], F32)
        bias = sb("gf_bias", [P, D], F32)
        ps = [ctx.enter_context(nc.psum_tensor(f"gf_ps{k}", [P, 512], F32)) for k in range(4)]
        s_ld = g.sem("gf_load"); s_tr = g.sem("gf_tr"); s_cp = g.sem("gf_cp"); s_dve = g.sem("gf_dve")
        s_m = g.sem("gf_min"); s_e = g.sem("gf_exp")
        block = ctx.enter_context(nc.Block())

        @block.sync
        def _(sp):
            sp.dma_start(Hs[:], g.Htab[:, 0:D].rearrange("(t p) d -> p t d", p=P)).then_inc(s_ld, 16)
            sp.dma_start(bias[:], g.gat_bias.partition_broadcast(P)).then_inc(s_ld, 16)

        @block.tensor
        def _(pe):
            for t in range(NT):
                if t >= 4:
                    pe.wait_ge(s_cp, t - 3)
                b = ps[t % 4]
                for j in range(KD):
                    nc.tensor.transpose(b[:, j * P:(j + 1) * P], g.ACC[:, j, t * P:(t + 1) * P], g.ident[:])
                nc.tensor.transpose(b[:, D:D + 8], g.DEN[:, t * P:(t + 1) * P], g.ident[0:8, 0:8]).then_inc(s_tr, 1)

        @block.scalar
        def _(act):
            for t in range(NT):
                act.wait_ge(s_tr, t + 1)
                nc.scalar.activation(g.Z[:, t, :], ps[t % 4][:, 0:D], ACT.Copy)
                nc.scalar.activation(den8[:, t, :], ps[t % 4][:, D:D + 8], ACT.Copy).then_inc(s_cp, 1)
            act.wait_ge(s_m, 1)
            nc.scalar.activation(Hs[:], Hs[:], ACT.Exp).then_inc(s_e, 1)

        @block.vector
        def _(dve):
            step = Steps(dve, s_dve)
            dve.wait_ge(s_ld, 32)
            step(dve.tensor_tensor(g.X[:], g.X[:], g.Y[:], ALU.add))
            dve.wait_ge(s_cp, NT)
            heads = lambda ap: ap.rearrange("p t (a c) -> p t a c", a=HEADS)
            step(dve.tensor_tensor(den[:], den8[:, :, 0:4], den8[:, :, 4:8], ALU.add))
            step(dve.tensor_scalar(den[:], den[:], 1e-16, None, ALU.add))
            step(dve.reciprocal(den[:], den[:]))
            step(dve.tensor_tensor(heads(Hs[:]), heads(Hs[:]), bcast(den8[:, :, 4:8], 3, CH), ALU.mult))
            step(dve.tensor_tensor(g.Z[:], g.Z[:], Hs[:], ALU.add))
            step(dve.tensor_tensor(heads(g.Z[:]), heads(g.Z[:]), bcast(den[:], 3, CH), ALU.mult))
            step(dve.tensor_tensor(g.Z[:], g.Z[:], bcast(bias[:], 1, NT), ALU.add))
            step(dve.tensor_scalar(Hs[:], g.Z[:], 0.0, None, ALU.min))
            dve.sem_inc(s_m, 1)
            step(dve.scalar_tensor_tensor(g.X[:], g.Z[:], 0.0, g.X[:], ALU.max, ALU.add))
            dve.wait_ge(s_e, 1)
            step(dve.scalar_tensor_tensor(g.X[:], Hs[:], -1.0, g.X[:], ALU.add, ALU.add))


def router_stage(nc, g, which):
    pre = f"rt{which}_"
    gw_dram, gb_dram = (g.gate_w, g.gate_b) if which == 0 else (g.Wr, g.br)
    trash = NE * B0 if which == 0 else NB1 * B1
    with ExitStack() as ctx:
        sb = lambda n, s, d=F32: ctx.enter_context(nc.sbuf_tensor(pre + n, s, d))
        gw = sb("gw", [P, KD, NE]); gb = sb("gb", [P, NE])
        xT = sb("xT", [P, 2, KD, P])
        L = sb("L", [P, NT, NE]); e1 = sb("e1", [P, NT, NE]); e2 = sb("e2", [P, NT, NE])
        oh = [sb("oh0", [P, NT, NE]), sb("oh1", [P, NT, NE])]
        both = sb("both", [P, NT, NE]); pos = sb("pos", [P, NT, NE]); tot = sb("tot", [P, NT, NE])
        run = sb("run", [P, NT, NE])
        mx = [sb("mx0", [P, NT]), sb("mx1", [P, NT])]
        low = sb("low", [P, NT]); a = sb("a", [P, NT]); b = sb("b", [P, NT]); c = sb("c", [P, NT])
        rtok = sb("rtok", [P, NT]); rtok_i = sb("rtok_i", [P, NT], I32)
        nblk = sb("nblk", [P, NE]); nblk_i = sb("nblk_i", [P, NE], I32); ends = sb("ends", [P, NE]); onesr = sb("onesr", [P, NT])
        start = sb("start", [P, NE]); blk = sb("blk", [1, NB1, NE]); blkn = sb("blkn", [1, NB1])
        slot = sb("slot", [P, 2, NT], I32)
        ps_t = [ctx.enter_context(nc.psum_tensor(f"{pre}t{k}", [P, 512], F32)) for k in range(2)]
        ps_l = ctx.enter_context(nc.psum_tensor(pre + "l", [P, 512], F32))
        ps_p = ctx.enter_context(nc.psum_tensor(pre + "p", [P, 512], F32))
        ps_q = ctx.enter_context(nc.psum_tensor(pre + "q", [P, 512], F32))
        s_ld = g.sem(pre + "load"); s_dve = g.sem(pre + "dve"); s_var = g.sem(pre + "var"); s_sq = g.sem(pre + "sqrt")
        s_ln = g.sem(pre + "ln"); s_tr = g.sem(pre + "tr"); s_xT = g.sem(pre + "xT"); s_lg = g.sem(pre + "logits")
        s_e = g.sem(pre + "exp"); s_ex = g.sem(pre + "exped"); s_oh = g.sem(pre + "onehot"); s_pp = g.sem(pre + "prefix")
        s_slot = g.sem(pre + "slot"); s_sc = g.sem(pre + "scatter"); s_z = g.sem(pre + "zeroed"); s_io = g.sem(pre + "iota")
        s_ln2 = g.sem(pre + "ln2")
        block = ctx.enter_context(nc.Block())
        tokens = g.Y if which == 0 else g.Z

        @block.sync
        def _(sp):
            sp.dma_start(gw[:], gw_dram.rearrange("(k p) e -> p k e", p=P)).then_inc(s_ld, 16)
            sp.dma_start(gb[:], gb_dram.partition_broadcast(P)).then_inc(s_ld, 16)
            rows = g.XB[0:trash, :].rearrange("(r p) d -> p r d", p=P)
            for r in range(0, trash // P, 16):
                sp.dma_start(rows[:, r:r + 16, :], bcast(g.zrow[:], 1, 16)).then_inc(s_z, 16)

        @block.tensor
        def _(pe):
            pe.wait_ge(s_ld, 32)
            pe.wait_ge(s_ln, 1)
            for t in range(NT + 1):
                if t < NT:
                    if t >= 2:
                        pe.wait_ge(s_xT, t - 1)
                    for k in range(KD):
                        ins = nc.tensor.transpose(ps_t[t % 2][:, k * P:(k + 1) * P], g.Y[:, t, k * P:(k + 1) * P], g.ident[:])
                    ins.then_inc(s_tr, 1)
                if t >= 1:
                    u = t - 1
                    pe.wait_ge(s_xT, u + 1)
                    for k in range(KD):
                        ins = nc.tensor.matmul(ps_l[:, u * NE:(u + 1) * NE], xT[:, u % 2, k, :], gw[:, k, :], start=(k == 0), stop=(k == KD - 1))
                    ins.then_inc(s_lg, 1)
            pe.wait_ge(s_oh, 1)
            src = both[:].rearrange("p t e -> p (t e)")
            nc.tensor.matmul(ps_p[:, 0:NT * NE], g.upper[:], src, start=True, stop=True)
            nc.tensor.matmul(ps_q[:, 0:NT * NE], g.ones[:], src, start=True, stop=True).then_inc(s_pp, 1)

        @block.scalar
        def _(act):
            act.wait_ge(s_var, 1)
            nc.scalar.activation(g.ln_s[:], g.ln_var[:], ACT.Sqrt).then_inc(s_sq, 1)
            for t in range(NT):
                act.wait_ge(s_tr, t + 1)
                if t >= 2:
                    act.wait_ge(s_lg, t - 1)
                nc.scalar.activation(xT[:, t % 2], ps_t[t % 2][:, 0:D].rearrange("p (k n) -> p k n", k=KD), ACT.Copy).then_inc(s_xT, 1)
            if which == 1:
                act.wait_ge(s_var, 2)
                nc.scalar.activation(g.ln_s[:], g.ln_var[:], ACT.Sqrt).then_inc(s_sq, 1)
            act.wait_ge(s_e, 1)
            if which == 0:
                nc.scalar.activation(e1[:], e1[:], ACT.Exp).then_inc(s_ex, 1)
            else:
                nc.scalar.activation(a[:], a[:], ACT.Exp).then_inc(s_ex, 1)

        @block.gpsimd
        def _(pool):
            pool.iota(rtok_i[:], [[P, NT]], base=trash, channel_multiplier=1).then_inc(s_io, 1)
            pool.wait_ge(s_slot, 1)
            pool.wait_ge(s_z, 16 * (-(-(trash // P) // 16)))
            n = 0
            for k in range(which + 1):
                for t in range(NT):
                    pool.indirect_dma_start(g.XB, bass.IndirectOffsetOnAxis(slot[:, k, t:t + 1], axis=0), tokens[:, t, :], None).then_inc(s_sc, 16)
                    n += 16
            pool.wait_ge(s_sc, n)

        @block.vector
        def _(dve):
            step = Steps(dve, s_dve)
            layernorm(nc, g, dve, step, s_var, s_sq, 1, g.X, g.Y)
            dve.sem_inc(s_ln, 1)
            if which == 1:
                layernorm(nc, g, dve, step, s_var, s_sq, 2, g.Y, g.Z)
            dve.wait_ge(s_lg, NT)
            lg = ps_l[:, 0:NT * NE].rearrange("p (t e) -> p t e", t=NT)
            step(dve.tensor_tensor(L[:], lg, bcast(gb[:], 1, NT), ALU.add))
            iota8 = bcast(g.iota[:, 0:NE], 1, NT)

            def best(values, m, hot):
                step(dve.tensor_reduce(m[:], values[:], AX.X, ALU.max))
                step(dve.tensor_tensor(hot[:], values[:], bcast(m[:], 2, NE), ALU.is_equal))
                step(dve.scalar_tensor_tensor(e2[:], hot[:], -64.0, iota8, ALU.mult, ALU.add))
                step(dve.tensor_reduce(low[:], e2[:], AX.X, ALU.min))
                step(dve.tensor_tensor(hot[:], e2[:], bcast(low[:], 2, NE), ALU.is_equal))

            best(L, mx[0], oh[0])
            if which == 0:
                step(dve.tensor_tensor(e1[:], L[:], bcast(mx[0][:], 2, NE), ALU.subtract))
            else:
                step(dve.scalar_tensor_tensor(L[:], oh[0][:], -BIG, L[:], ALU.mult, ALU.add))
                best(L, mx[1], oh[1])
                step(dve.tensor_tensor(a[:], mx[1][:], mx[0][:], ALU.subtract))
            dve.sem_inc(s_e, 1)
            for k in range(which + 1):
                step(dve.tensor_scalar(oh[k][:, NT - 1, :], oh[k][:, NT - 1, :], g.valid[:], None, ALU.mult))
            if which == 0:
                step(dve.tensor_copy(both[:], oh[0][:]))
            else:
                step(dve.tensor_tensor(both[:], oh[0][:], oh[1][:], ALU.add))
            dve.sem_inc(s_oh, 1)
            dve.wait_ge(s_ex, 1)
            if which == 0:
                step(dve.tensor_reduce(a[:], e1[:], AX.X, ALU.add))
                step(dve.reciprocal(g.wgt[:, 0, :], a[:]))
            else:
                step(dve.tensor_scalar(b[:], a[:], 1.0, None, ALU.add))
                step(dve.reciprocal(g.wgt[:, 0, :], b[:]))
                step(dve.tensor_tensor(g.wgt[:, 1, :], g.wgt[:, 0, :], a[:], ALU.mult))
            dve.wait_ge(s_pp, 1)
            flat = lambda x: x[:].rearrange("p t e -> p (t e)")
            step(dve.tensor_copy(flat(tot), ps_q[:, 0:NT * NE]))
            step(dve.memset(onesr[:], 1.0))
            for e in range(NE):
                dve.tensor_tensor_scan(run[:, :, e], onesr[:], tot[:, :, e], 0.0, ALU.mult, ALU.add).then_inc(s_dve, 1)
            step.n += NE
            dve.wait_ge(s_dve, step.n)
            step(dve.tensor_tensor(flat(pos), ps_p[:, 0:NT * NE], flat(run), ALU.add))
            step(dve.tensor_tensor(pos[:], pos[:], tot[:], ALU.subtract))
            if which == 0:
                step(dve.tensor_scalar(start[:], g.iota[:, 0:NE], float(B0), -1.0, ALU.mult, ALU.add))
            else:
                step(dve.tensor_scalar(nblk_i[:], run[:, NT - 1, :], float(B1 - 1), None, ALU.add))
                step(dve.tensor_scalar(nblk_i[:], nblk_i[:], B1.bit_length() - 1, None, ALU.arith_shift_right))
                step(dve.tensor_copy(nblk[:], nblk_i[:]))
                step(dve.tensor_tensor_scan(ends[:], onesr[:, 0:NE], nblk[:], 0.0, ALU.mult, ALU.add))
                step(dve.tensor_tensor(start[:], ends[:], nblk[:], ALU.subtract))
                step(dve.tensor_scalar(start[:], start[:], float(B1), -1.0, ALU.mult, ALU.add))
                step(dve.tensor_tensor(blk[:], bcast(ends[0:1, :], 1, NB1), bcast(g.iota[0:1, 0:NB1], 2, NE), ALU.is_le))
                step(dve.tensor_reduce(blkn[:], blk[:], AX.X, ALU.add))
                step(dve.tensor_scalar(blkn[:], blkn[:], float(NE - 1), None, ALU.min))
                step(dve.tensor_copy(g.blk_expert[:], blkn[:]))
            dve.wait_ge(s_io, 1)
            step(dve.tensor_copy(rtok[:], rtok_i[:]))
            step(dve.tensor_tensor(tot[:], pos[:], bcast(start[:], 1, NT), ALU.add))
            for k in range(which + 1):
                step(dve.tensor_tensor(e2[:], tot[:], oh[k][:], ALU.mult))
                step(dve.tensor_reduce(a[:], e2[:], AX.X, ALU.add))
                step(dve.tensor_reduce(c[:], oh[k][:], AX.X, ALU.add))
                if which == 0:
                    step(dve.tensor_tensor(e2[:], pos[:], oh[k][:], ALU.mult))
                    step(dve.tensor_reduce(b[:], e2[:], AX.X, ALU.add))
                    step(dve.tensor_scalar(low[:], b[:], float(CAP), None, ALU.is_le))
                    step(dve.tensor_tensor(c[:], c[:], low[:], ALU.mult))
                    step(dve.tensor_tensor(g.wgt[:, 0, :], g.wgt[:, 0, :], c[:], ALU.mult))
                    step(dve.tensor_scalar(low[:], b[:], float(CAP), 0.0, ALU.subtract, ALU.max))
                    step(dve.tensor_tensor(b[:], a[:], low[:], ALU.subtract))
                    step(dve.tensor_copy(g.gslot[:, k, :], b[:]))
                else:
                    step(dve.tensor_copy(g.gslot[:, k, :], a[:]))
                step(dve.tensor_tensor(a[:], a[:], rtok[:], ALU.subtract))
                step(dve.tensor_tensor(a[:], a[:], c[:], ALU.mult))
                step(dve.tensor_tensor(slot[:, k, :], a[:], rtok[:], ALU.add))
                step(dve.tensor_scalar(rtok[:], rtok[:], float(NP), None, ALU.add))
            dve.sem_inc(s_slot, 1)


def experts_stage(nc, g, which):
    pre = f"ex{which}_"
    B, NB = (B0, NE) if which == 0 else (B1, NB1)
    S = B // P
    W1, b1, W2, b2 = (g.f0_w1, g.f0_b1, g.f0_w2, g.f0_b2) if which == 0 else (g.f1_w1, g.f1_b1, g.f1_w2, g.f1_b2)
    func = ACT.Relu if which == 0 else ACT.Gelu
    with ExitStack() as ctx:
        sb = lambda n, s, d=F32: ctx.enter_context(nc.sbuf_tensor(pre + n, s, d))
        w1 = sb("w1", [P, 2, KD, F]); w2 = sb("w2", [P, 2, FC, D]); xb = sb("xb", [P, 2, S, D])
        xT = sb("xT", [P, 2, KD, B]); hT = sb("hT", [P, FC, B]); y = sb("y", [P, 2, S, D])
        b1r = sb("b1r", [NE * FC, P]); b1c = sb("b1c", [P, NE * FC]); b2b = sb("b2b", [P, NE, D])
        lnr = sb("lnr", [NE * KD, 2, P]); lnc = sb("lnc", [P, 2, NE * KD])
        ps_x = ctx.enter_context(nc.psum_tensor(pre + "px", [P, KD, 512], F32))
        ps_h = [ctx.enter_context(nc.psum_tensor(f"{pre}ph{k}", [P, 512], F32)) for k in range(2)]
        ps_y = [ctx.enter_context(nc.psum_tensor(f"{pre}py{k}", [P, 512], F32)) for k in range(2)]
        s_c = g.sem(pre + "const"); s_ct = g.sem(pre + "const_tr"); s_cc = g.sem(pre + "const_cp")
        s_w1 = [g.sem(f"{pre}w1_{k}") for k in range(2)]; s_w2 = [g.sem(f"{pre}w2_{k}") for k in range(2)]
        s_xb = [g.sem(f"{pre}xb_{k}") for k in range(2)]; s_yst = [g.sem(f"{pre}yst_{k}") for k in range(2)]
        s_tr = g.sem(pre + "tr")
        s_xT = g.sem(pre + "xT")
        s_h = g.sem(pre + "h")
        s_hT = g.sem(pre + "hT")
        s_y2 = g.sem(pre + "y2")
        s_py = g.sem(pre + "py")
        s_turn = g.sem(pre + "turn")
        block = ctx.enter_context(nc.Block())

        def rounds(eng, body):
            with eng.Fori(0, NB // 2 - 1) as i:
                body(i * 2, i, 0, False)
                body(i * 2 + 1, i, 1, False)
            body(NB - 2, NB // 2 - 1, 0, False)
            body(NB - 1, NB // 2 - 1, 1, True)

        def expert(eng, n):
            return n if which == 0 else eng.value_load(g.blk_expert[0:1, bass.ds(n, 1)], min_val=0, max_val=NE - 1)

        @block.sync
        def _(sp):
            sp.dma_start(b1r[:], b1.rearrange("e (c p) -> (e c) p", p=P)).then_inc(s_c, 16)
            sp.dma_start(b2b[:], b2.partition_broadcast(P)).then_inc(s_c, 16)
            if which == 1:
                sp.dma_start(lnr[:, 0, :], g.ln_g.rearrange("e (k p) -> (e k) p", p=P)).then_inc(s_c, 16)
                sp.dma_start(lnr[:, 1, :], g.ln_b.rearrange("e (k p) -> (e k) p", p=P)).then_inc(s_c, 16)

            def load(n, i, par, last):
                e = expert(sp, n)
                sp.wait_ge(s_h, (n + 1) * FC)
                sp.dma_start(xb[:, par], g.XB[bass.ds(n * B, B), :].rearrange("(s p) d -> p s d", p=P)).then_inc(s_xb[par], 16)
                sp.dma_start(w1[:, par], W1[bass.ds(e, 1)].rearrange("a (k p) f -> p (a k) f", p=P)).then_inc(s_w1[par], 16)
                sp.wait_ge(s_y2, (n + 1) * S)
                sp.dma_start(w2[:, par], W2[bass.ds(e, 1)].rearrange("a (c p) d -> p (a c) d", p=P)).then_inc(s_w2[par], 16)

            rounds(sp, load)

        @block.gpsimd
        def _(pool):
            def store(n, i, par, last):
                pool.wait_ge(s_py, n * S + (S + 2))
                pool.sem_inc(s_turn, 1)
                pool.dma_start(g.YB[bass.ds(n * B, B), :].rearrange("(s p) d -> p s d", p=P), y[:, par]).then_inc(s_yst[par], 16)

            for par in range(2):
                pool.dma_start(g.scrap[par:par + 1, :], g.zrow[0:1, :]).then_inc(s_yst[par], 16)
            rounds(pool, store)
            for par in range(2):
                pool.wait_ge(s_yst[par], 16 * (NB // 2) + 16)

        @block.tensor
        def _(pe):
            pe.wait_ge(s_c, 32 + 32 * which)
            ins = nc.tensor.transpose(ps_h[0][:, 0:NE * FC], b1r[:], g.ident[0:NE * FC, 0:NE * FC])
            if which == 1:
                for k in range(2):
                    ins = nc.tensor.transpose(ps_h[1][:, k * 16:k * 16 + 16], lnr[:, k, :], g.ident[0:NE * KD, 0:NE * KD])
            ins.then_inc(s_ct, 1)
            pe.wait_ge(s_cc, 2)
            pe.sem_inc(s_h, 2 * FC)
            pe.sem_inc(s_y2, 2 * S)

            def transposes(par, i):
                pe.wait_ge(s_xb[par], 16 * i + 16)
                for s in range(S):
                    for k in range(KD):
                        ins = nc.tensor.transpose(ps_x[:, k, s * P:(s + 1) * P], xb[:, par, s, k * P:(k + 1) * P], g.ident[:])
                ins.then_inc(s_tr, 1)

            def products(n, i, par, last):
                pe.wait_ge(s_w1[par], 16 * i + 16)
                pe.wait_ge(s_xT, n * KD + KD)
                for c in range(FC):
                    pe.wait_ge(s_hT, n * FC + (c + 1))
                    for k in range(KD):
                        ins = nc.tensor.matmul(ps_h[c % 2][:, 0:B], w1[:, par, k, c * P:(c + 1) * P], xT[:, par, k, :], start=(k == 0), stop=(k == KD - 1))
                    ins.then_inc(s_h, 1)
                if not last:
                    transposes(1 - par, i + par)
                pe.wait_ge(s_w2[par], 16 * i + 16)
                pe.wait_ge(s_hT, n * FC + (FC + 2))
                for s in range(S):
                    pe.wait_ge(s_py, n * S + (s + 1))
                    for c in range(FC):
                        ins = nc.tensor.matmul(ps_y[s % 2][:, 0:D], hT[:, c, s * P:(s + 1) * P], w2[:, par, c, :], start=(c == 0), stop=(c == FC - 1))
                    ins.then_inc(s_y2, 1)

            transposes(0, 0)
            rounds(pe, products)

        @block.scalar
        def _(act):
            act.wait_ge(s_ct, 1)
            nc.scalar.activation(b1c[:], ps_h[0][:, 0:NE * FC], ACT.Copy).then_inc(s_cc, 1)
            act.wait_ge(s_cc, 2)
            act.sem_inc(s_hT, 2)

            def activate(n, i, par, last):
                e = expert(act, n)
                act.wait_ge(s_y2, (n + 2) * S)
                for c in range(FC):
                    act.wait_ge(s_h, n * FC + (c + 1 + 2 * FC))
                    nc.scalar.activation(hT[:, c, :], ps_h[c % 2][:, 0:B], func, bias=b1c[:, bass.ds(e * FC + c, 1)]).then_inc(s_hT, 1)

            rounds(act, activate)

        @block.vector
        def _(dve):
            dve.wait_ge(s_ct, 1)
            if which == 1:
                nc.vector.tensor_copy(lnc[:], ps_h[1][:, 0:32].rearrange("p (a e) -> p a e", a=2)).then_inc(s_cc, 1)
                dve.wait_ge(s_cc, 2)
            else:
                dve.sem_inc(s_cc, 1)
            dve.sem_inc(s_py, 2)

            def copy_xT(n, par):
                dve.wait_ge(s_tr, n + 1)
                e = None if which == 0 else expert(dve, n)
                for k in range(KD):
                    if which == 0:
                        ins = nc.vector.tensor_copy(xT[:, par, k, :], ps_x[:, k, 0:B])
                    else:
                        ins = nc.vector.tensor_scalar(xT[:, par, k, :], ps_x[:, k, 0:B], lnc[:, 0, bass.ds(e * KD + k, 1)], lnc[:, 1, bass.ds(e * KD + k, 1)], ALU.mult, ALU.add)
                    ins.then_inc(s_xT, 1)

            def results(n, i, par, last):
                if not last:
                    copy_xT(n + 1, 1 - par)
                e = expert(dve, n)
                dve.wait_ge(s_yst[par], 16 * i + 16)
                for s in range(S):
                    dve.wait_ge(s_y2, n * S + (s + 1 + 2 * S))
                    nc.vector.tensor_tensor(y[:, par, s, :], ps_y[s % 2][:, 0:D], b2b[:, bass.ds(e, 1), :].rearrange("p a d -> p (a d)"), ALU.add).then_inc(s_py, 1)

            copy_xT(0, 0)
            rounds(dve, results)


def combine_stage(nc, g, which):
    pre = f"cb{which}_"
    with ExitStack() as ctx:
        sb = lambda n, s, d=F32: ctx.enter_context(nc.sbuf_tensor(pre + n, s, d))
        bad = sb("bad", [P, NT, D], I32)
        low = sb("low", [P, 3, D])
        s_g = g.sem(pre + "gather"); s_dve = g.sem(pre + "dve"); s_out = g.sem(pre + "out"); s_x = g.sem(pre + "x")
        block = ctx.enter_context(nc.Block())
        rows = (g.Z, g.Y)
        filled = g.YB[0:NE * B0 if which == 0 else NB1 * B1, :]

        @block.gpsimd
        def _(pool):
            for k in range(which + 1):
                for t in range(NT):
                    pool.indirect_dma_start(rows[k][:, t, :], None, filled, bass.IndirectOffsetOnAxis(g.gslot[:, k, t:t + 1], axis=0)).then_inc(s_g, 16)

        @block.vector
        def _(dve):
            step = Steps(dve, s_dve)
            dve.wait_ge(s_g, 16 * NT * (which + 1))
            for k in range(which + 1):
                r = rows[k]
                step(dve.tensor_tensor(r[:], r[:], bcast(g.wgt[:, k, :], 2, D), ALU.mult))
                if which == 0:
                    for j, v in enumerate((0.0, 1.0e4, -1.0e4)):
                        step(dve.memset(low[:, j, :], v))
                    step(dve.tensor_tensor(bad[:], r[:], r[:], ALU.not_equal))
                    step(dve.copy_predicated(r[:], bad[:], bcast(low[:, 0, :], 1, NT)))
                    step(dve.tensor_scalar(bad[:], r[:], 3.4028234e38, None, ALU.is_gt))
                    step(dve.copy_predicated(r[:], bad[:], bcast(low[:, 1, :], 1, NT)))
                    step(dve.tensor_scalar(bad[:], r[:], -3.4028234e38, None, ALU.is_lt))
                    step(dve.copy_predicated(r[:], bad[:], bcast(low[:, 2, :], 1, NT)))
                step(dve.tensor_tensor(g.X[:], g.X[:], r[:], ALU.add))
            dve.sem_inc(s_x, 1)

        @block.sync
        def _(sp):
            if which == 1:
                sp.wait_ge(s_x, 1)
                sp.dma_start(g.out[0:(NT - 1) * P, :].rearrange("(t p) d -> p t d", p=P), g.X[:, 0:NT - 1, :]).then_inc(s_out, 16)
                sp.dma_start(g.out[(NT - 1) * P:N, :], g.X[0:LAST, NT - 1, :]).then_inc(s_out, 16)
                sp.wait_ge(s_out, 32)


def rgcn_table_stage(nc, g, layer):
    pre = f"rg{layer}_"
    W, bias = (g.rW0, g.rb0) if layer == 0 else (g.rW1, g.rb1)
    R2 = NREL // 2
    with ExitStack() as ctx:
        sb = lambda n, s, d=F32: ctx.enter_context(nc.sbuf_tensor(pre + n, s, d))
        w = sb("w", [P, KD, NREL, D]); b2 = sb("b2", [P, 2, D]); xs = sb("xs", [P, 2, KD, P])
        rows = sb("rows", [P, 2, R2, 2 * D])
        ps_t = [ctx.enter_context(nc.psum_tensor(f"{pre}t{k}", [P, 512], F32)) for k in range(2)]
        ps = [ctx.enter_context(nc.psum_tensor(f"{pre}p{k}", [P, 512], F32)) for k in range(4)]
        s_ld = g.sem(pre + "load"); s_dve = g.sem(pre + "dve"); s_var = g.sem(pre + "var"); s_sq = g.sem(pre + "sqrt")
        s_ln = g.sem(pre + "ln"); s_tr = g.sem(pre + "tr"); s_T = g.sem(pre + "T")
        s_xs = g.sem(pre + "xs"); s_mm = g.sem(pre + "mm"); s_add = g.sem(pre + "add"); s_relu = g.sem(pre + "relu")
        s_st = [g.sem(f"{pre}st{k}") for k in range(2)]
        block = ctx.enter_context(nc.Block())

        def rounds(eng, body):
            with eng.Fori(0, NT // 2) as i:
                body(i * 2, i, 0)
                body(i * 2 + 1, i, 1)
            body(NT - 1, NT // 2, 0)

        @block.gpsimd
        def _(pool):
            pool.wait_ge(s_T, NT if layer == 0 else 1)

            def stage(t, i, par):
                pool.wait_ge(s_mm, t * R2 + R2)
                pool.sem_inc(s_ln, 1)
                pool.tensor_copy(xs[:, par], g.ACC[:, :, bass.ds(t * P, P)]).then_inc(s_xs, 1)

            rounds(pool, stage)

        @block.tensor
        def _(pe):
            if layer == 0:
                pe.wait_ge(s_ln, 1)
                for t in range(NT):
                    if t >= 2:
                        pe.wait_ge(s_T, t - 1)
                    for k in range(KD):
                        ins = nc.tensor.transpose(ps_t[t % 2][:, k * P:(k + 1) * P], g.Y[:, t, k * P:(k + 1) * P], g.ident[:])
                    ins.then_inc(s_tr, 1)
            pe.sem_inc(s_mm, 2 * R2)
            pe.wait_ge(s_ld, 48)

            def products(t, i, par):
                pe.wait_ge(s_xs, t + 1)
                for r in range(R2):
                    pe.wait_ge(s_add, t * R2 + (r + 1))
                    for k in range(KD):
                        ins = nc.tensor.matmul(ps[r][:], xs[:, par, k, :], w[:, k, 2 * r:2 * r + 2, :].rearrange("p r d -> p (r d)"), start=(k == 0), stop=(k == KD - 1))
                    ins.then_inc(s_mm, 1)

            rounds(pe, products)

        @block.vector
        def _(dve):
            step = Steps(dve, s_dve)
            if layer == 0:
                layernorm(nc, g, dve, step, s_var, s_sq, 1, g.X, g.Y)
                dve.sem_inc(s_ln, 1)
            dve.sem_inc(s_add, R2)
            dve.wait_ge(s_ld, 48)

            def add(t, i, par):
                dve.wait_ge(s_st[par], 16 * i + 16)
                for r in range(R2):
                    dve.wait_ge(s_mm, t * R2 + (r + 1 + 2 * R2))
                    nc.vector.tensor_tensor(rows[:, par, r, :], ps[r][:], b2[:].rearrange("p r d -> p (r d)"), ALU.add).then_inc(s_add, 1)

            rounds(dve, add)

        @block.scalar
        def _(act):
            if layer == 0:
                act.wait_ge(s_var, 1)
                nc.scalar.activation(g.ln_s[:], g.ln_var[:], ACT.Sqrt).then_inc(s_sq, 1)
                for t in range(NT):
                    act.wait_ge(s_tr, t + 1)
                    nc.scalar.activation(g.ACC[:, :, t * P:(t + 1) * P], ps_t[t % 2][:, 0:D].rearrange("p (k n) -> p k n", k=KD), ACT.Copy).then_inc(s_T, 1)
            else:
                act.sem_inc(s_T, 1)

            def relu(t, i, par):
                for r in range(R2):
                    act.wait_ge(s_add, t * R2 + (r + 1 + R2))
                    nc.scalar.activation(rows[:, par, r, :], rows[:, par, r, :], ACT.Relu).then_inc(s_relu, 1)

            rounds(act, relu)

        @block.sync
        def _(sp):
            sp.dma_start(w[:, 0], W[:, 0:P, :].rearrange("r p o -> p r o")).then_inc(s_ld, 16)
            sp.dma_start(w[:, 1], W[:, P:2 * P, :].rearrange("r p o -> p r o")).then_inc(s_ld, 16)
            sp.dma_start(b2[:], bcast(bias, 0, 2).partition_broadcast(P)).then_inc(s_ld, 16)
            table = g.Gtab[0:ZERO_ROW, :].rearrange("(r n) d -> n r d", n=NP)

            def store(t, i, par):
                sp.wait_ge(s_relu, t * R2 + R2)
                sp.dma_start(table[bass.ds(t * P, P), :, :], rows[:, par].rearrange("p a (b d) -> p (a b) d", b=2)).then_inc(s_st[par], 16)

            for par in range(2):
                sp.dma_start(g.scrap[par:par + 1, :], g.zrow[0:1, :]).then_inc(s_st[par], 16)
            rounds(sp, store)
            sp.wait_ge(s_st[0], 16 * (NT // 2 + 1) + 16)
            sp.wait_ge(s_st[1], 16 * (NT // 2) + 16)


def add_sums_stage(nc, g):
    with ExitStack() as ctx:
        ps = [ctx.enter_context(nc.psum_tensor(f"as_ps{k}", [P, 512], F32)) for k in range(4)]
        s_tr = g.sem("as_tr"); s_add = g.sem("as_add")
        block = ctx.enter_context(nc.Block())

        @block.tensor
        def _(pe):
            for t in range(NT):
                if t >= 4:
                    pe.wait_ge(s_add, t - 3)
                for j in range(KD):
                    ins = nc.tensor.transpose(ps[t % 4][:, j * P:(j + 1) * P], g.ACC[:, j, t * P:(t + 1) * P], g.ident[:])
                ins.then_inc(s_tr, 1)

        @block.vector
        def _(dve):
            for t in range(NT):
                dve.wait_ge(s_tr, t + 1)
                nc.vector.tensor_tensor(g.X[:, t, :], g.X[:, t, :], ps[t % 4][:, 0:D], ALU.add).then_inc(s_add, 1)


def build(nc, ins, out):
    with ExitStack() as top:
        g = Places()
        g.x, g.src, g.dst, g.typ, g.gat_w, g.att_src = (ins["x"], ins["src"], ins["dst"], ins["typ"], ins["gat_w"], ins["att_src"])
        g.att_dst, g.gat_bias, g.gate_w, g.gate_b, g.f0_w1, g.f0_b1 = (ins["att_dst"], ins["gat_bias"], ins["gate_w"], ins["gate_b"], ins["f0_w1"], ins["f0_b1"])
        g.f0_w2, g.f0_b2, g.rW0, g.rb0, g.rW1, g.rb1 = (ins["f0_w2"], ins["f0_b2"], ins["rW0"], ins["rb0"], ins["rW1"], ins["rb1"])
        g.Wr, g.br, g.ln_g, g.ln_b, g.f1_w1, g.f1_b1 = (ins["Wr"], ins["br"], ins["ln_g"], ins["ln_b"], ins["f1_w1"], ins["f1_b1"])
        g.f1_w2, g.f1_b2 = (ins["f1_w2"], ins["f1_b2"])
        g.out = out
        dram = lambda name, shape, dt=F32: nc.dram_tensor(name, shape, dt, kind="Internal").ap()
        sb = lambda name, shape, dt=F32: top.enter_context(nc.sbuf_tensor(name, shape, dt))
        g.S_src, g.S_dst, g.S_typ = (dram(n, (E + 2 * EPAD,), I32) for n in ("s_src_d", "s_dst_d", "s_typ_d"))
        g.S_rec = dram("s_rec_d", (E, 4), I32)
        g.Htab = dram("h_table", (NP, HROW))
        g.Atab = dram("a_table", (NP, 8))
        g.Gtab = dram("rel_table", (ZERO_ROW + 1, D))
        g.XB = dram("slots_in", (NB1 * B1 + 2 * NP, D))
        g.YB = dram("slots_out", (NB1 * B1, D))
        g.scrap = dram("scrap", (2, D))
        g.iota_i = sb("iota_i", [P, P], I32); g.iotap_i = sb("iotap_i", [P, P], I32)
        g.iota = sb("iota", [P, P]); g.iotap = sb("iotap", [P, P]); g.ident = sb("ident", [P, P])
        g.upper = sb("upper", [P, P]); g.ones = sb("ones", [P, P]); g.zrow = sb("zrow", [P, D]); g.valid = sb("valid", [P, 1])
        g.unsorted = sb("unsorted", [1, 1], I32)
        g.ln_st = sb("ln_st", [P, NT, 6])
        g.ln_mean, g.ln_var, g.ln_r, g.ln_t1, g.ln_t2, g.ln_s = (sb(f"ln_{n}", [P, NT]) for n in ("mean", "var", "r", "t1", "t2", "s"))
        g.wgt = sb("wgt", [P, 2, NT]); g.gslot = sb("gslot", [P, 2, NT], I32); g.blk_expert = sb("blk_expert", [1, NB1], I32)

        stage(nc, g, edges_stage)
        stage(nc, g, sort_stage)
        TP = T + HALF
        g.relI = sb("relI", [P, TP], I32); g.dstrel = sb("dstrel", [P, TP]); g.base = sb("base", [1, T], I32)
        g.X = sb("X", [P, NT, D]); g.Y = sb("Y", [P, NT, D])
        with ExitStack() as gat:
            gsb = lambda name, shape, dt=F32: gat.enter_context(nc.sbuf_tensor(name, shape, dt))
            g.srcI = gsb("srcI", [P, TP], I32); g.dstI = gsb("dstI", [P, TP], I32)
            g.PT = gsb("PT", [P, TP, 8])
            with ExitStack() as lanes:
                lsb = lambda name, shape, dt=F32: lanes.enter_context(nc.sbuf_tensor(name, shape, dt))
                g.first = lsb("first", [LANES, LC, P]); g.firstneg = lsb("firstneg", [LANES, LC, P]); g.endneg = lsb("endneg", [LANES, LC, P])
                stage(nc, g, tables_stage)
                stage(nc, g, gat_table_stage)
                g.AS = lsb("AS", [P, T, 12])
                stage(nc, g, scores_stage)
                stage(nc, g, softmax_stage)
            g.ACC = gsb("ACC", [P, KD, AW]); g.DEN = gsb("DEN", [8, AW])
            stage(nc, g, edge_pass, "gat", g.Htab, g.srcI, 0)
            g.Z = gsb("Z", [P, NT, D])
            stage(nc, g, gat_finish_stage)
        g.Z = sb("Z1", [P, NT, D])
        stage(nc, g, router_stage, 0)
        stage(nc, g, experts_stage, 0)
        stage(nc, g, combine_stage, 0)
        with ExitStack() as rg:
            g.ACC = rg.enter_context(nc.sbuf_tensor("ACC1", [P, KD, AW], F32))
            for layer in range(2):
                stage(nc, g, rgcn_table_stage, layer)
                stage(nc, g, edge_pass, "rgcn", g.Gtab, g.relI, 1 + layer)
            stage(nc, g, add_sums_stage)
        stage(nc, g, router_stage, 1)
        stage(nc, g, experts_stage, 1)
        stage(nc, g, combine_stage, 1)


NAMES = {
    "x": "x", "src": "src", "dst": "dst", "edge_type_8": "typ",
    "L0_gnn_W": "gat_w", "L0_gnn_att_src": "att_src", "L0_gnn_att_dst": "att_dst", "L0_gnn_bias": "gat_bias",
    "L0_ffn_gate_w": "gate_w", "L0_ffn_gate_b": "gate_b",
    "L0_ffn_w1": "f0_w1", "L0_ffn_b1": "f0_b1", "L0_ffn_w2": "f0_w2", "L0_ffn_b2": "f0_b2",
    "L1_gnn_W0": "rW0", "L1_gnn_b0": "rb0", "L1_gnn_W1": "rW1", "L1_gnn_b1": "rb1",
    "L1_ffn_Wr": "Wr", "L1_ffn_br": "br", "L1_ffn_ln_g": "ln_g", "L1_ffn_ln_b": "ln_b",
    "L1_ffn_W1": "f1_w1", "L1_ffn_b1": "f1_b1", "L1_ffn_W2": "f1_w2", "L1_ffn_b2": "f1_b2",
}


def kernel(**inputs):
    import concourse.bacc as bacc
    from concourse.bass_utils import run_bass_kernel_spmd

    nc = bacc.Bacc("TRN2", target_bir_lowering=False, num_devices=1)
    arrays, ins = {}, {}
    for name, short in NAMES.items():
        a = np.ascontiguousarray(inputs[name])
        arrays["in_" + name] = a
        ins[short] = nc.dram_tensor("in_" + name, a.shape, mybir.dt.from_np(a.dtype), kind="ExternalInput").ap()
    out = nc.dram_tensor("out_0", (N, D), F32, kind="ExternalOutput").ap()
    build(nc, ins, out)
    r = run_bass_kernel_spmd(nc, [arrays], core_ids=[0])
    return r.results[0]["out_0"]
```

```python
import numpy as np
import concourse.bass as bass
from concourse import mybir
from contextlib import ExitStack

F32 = mybir.dt.float32
I32 = mybir.dt.int32
BF16 = mybir.dt.bfloat16
ALU = mybir.AluOpType
ACT = mybir.ActivationFunctionType
AX = mybir.AxisListType

P = 128
N = 3125
D = 256
KD = D // P
NT = -(-N // P)
NP = NT * P
LAST = N - (NT - 1) * P
HEADS, CH = 4, 64
E0 = 53125
T = 440
E = T * P
HALF = 10
RING = 2 * HALF
LANES, LC = 110, 4
EPAD = 128
WIN = P
AW = NP + WIN
HROW = D + 2 * HEADS
FILL_SRC = NP - 1
NREL = 8
FILL_TYPE = NREL
ZERO_ROW = NREL * NP
BIG = 1.0e30
NEG_SLOPE = 0.2
EPS = 1e-5
NE = 8
F = 1024
FC = F // P
CAP = -(-5 * N // (4 * NE))
B0 = 512
B1 = 256
NB1 = (2 * N + NE * (B1 - 1)) // B1
assert (T * P >= E0 + N) and CAP <= B0


class Places:
    pass


class Steps:

    def __init__(self, eng, sem):
        self.eng, self.sem, self.n = eng, sem, 0

    def __call__(self, ins):
        ins.then_inc(self.sem, 1)
        self.n = self.n + 1
        self.eng.wait_ge(self.sem, self.n)


def stage(nc, g, program, *args):
    taken = []
    g.stages += 1

    def sem(name):
        taken.append(nc.alloc_semaphore(name=f"{name}_s{g.stages}"))
        return taken[-1]

    g.sem = sem
    program(nc, g, *args)
    nc.clear_and_free_semaphores(taken)
    nc.all_engine_barrier()


def load_values(nc, engine, ap, most):
    return nc.values_load_multi_w_load_instructions(ap, engines=(engine,), min_val=0, max_val=most)[1]


def bcast(ap, axis, n):
    a = ap.unsqueeze(axis)
    shape = list(a.shape)
    shape[axis] = n
    return a.to_broadcast(shape)


def edges_stage(nc, g):
    with ExitStack() as ctx:
        fill = ctx.enter_context(nc.sbuf_tensor("fill", [1, 3, E - E0], I32))
        edge = ctx.enter_context(nc.sbuf_tensor("edge", [1, 2], I32))
        di = ctx.enter_context(nc.sbuf_tensor("di", [P, T], I32))
        dp = ctx.enter_context(nc.sbuf_tensor("dp", [P, T], I32))
        diff = ctx.enter_context(nc.sbuf_tensor("diff", [P, T], F32))
        b1 = ctx.enter_context(nc.sbuf_tensor("brk1", [P, T], F32))
        b2 = ctx.enter_context(nc.sbuf_tensor("brk2", [P, T], F32))
        bs = ctx.enter_context(nc.sbuf_tensor("brks", [P, 1], F32))
        tot = ctx.enter_context(nc.psum_tensor("brk_tot", [1, 1], F32))
        s_fill = g.sem("fill"); s_copy = g.sem("edge_copy"); s_load = g.sem("edge_load")
        s_chain = g.sem("edge_dve"); s_tot = g.sem("edge_tot"); s_sum = g.sem("edge_sum")
        block = ctx.enter_context(nc.Block())

        @block.gpsimd
        def _(pool):
            pool.memset(fill[:, 0, :], FILL_SRC).then_inc(s_fill, 1)
            pool.memset(fill[:, 1, :], N - 1).then_inc(s_fill, 1)
            pool.memset(fill[:, 2, :], FILL_TYPE).then_inc(s_fill, 1)
            pool.memset(edge[:, 0:1], -1).then_inc(s_fill, 1)
            pool.memset(edge[:, 1:2], N).then_inc(s_fill, 1)
            pool.iota(g.iota_i[:], [[1, P]], base=0, channel_multiplier=0).then_inc(s_fill, 1)
            pool.iota(g.iotap_i[:], [[0, P]], base=0, channel_multiplier=1).then_inc(s_fill, 1)
            pool.memset(g.ones[:], 1.0).then_inc(s_fill, 1)
            pool.memset(g.zrow[:], 0.0).then_inc(s_fill, 1)

        @block.sync
        def _(sp):
            for dram, a in ((g.S_src, g.src), (g.S_dst, g.dst), (g.S_typ, g.typ)):
                sp.dma_start(dram[EPAD:EPAD + E0].rearrange("(a b) -> a b", b=425),
                             a.rearrange("(a b) -> a b", b=425)).then_inc(s_copy, 16)
            sp.wait_ge(s_fill, 5)
            for k, dram in enumerate((g.S_src, g.S_dst, g.S_typ)):
                sp.dma_start(dram[EPAD + E0:EPAD + E].unsqueeze(0), fill[:, k, :]).then_inc(s_copy, 16)
            sp.dma_start(g.S_dst[EPAD - 1:EPAD].unsqueeze(0), edge[:, 0:1]).then_inc(s_copy, 16)
            sp.dma_start(g.S_dst[EPAD + E:EPAD + E + 1].unsqueeze(0), edge[:, 1:2]).then_inc(s_copy, 16)
            sp.wait_ge(s_copy, 8 * 16)
            sp.dma_start(di[:], g.S_dst[EPAD:EPAD + E].rearrange("(p j) -> p j", p=P)).then_inc(s_load, 16)
            sp.dma_start(dp[:], g.S_dst[EPAD - 1:EPAD - 1 + E].rearrange("(p j) -> p j", p=P)).then_inc(s_load, 16)

        @block.vector
        def _(dve):
            step = Steps(dve, s_chain)
            dve.wait_ge(s_fill, 9)
            dve.tensor_copy(g.iota[:], g.iota_i[:]).then_inc(s_fill, 1)
            step(dve.tensor_copy(g.iotap[:], g.iotap_i[:]))
            dve.wait_ge(s_fill, 10)
            step(dve.tensor_tensor(g.ident[:], g.iota[:], g.iotap[:], ALU.is_equal))
            step(dve.tensor_tensor(g.upper[:], g.iota[:], g.iotap[:], ALU.is_ge))
            step(dve.tensor_scalar(g.valid[:], g.iotap[:, 0:1], float(LAST), None, ALU.is_lt))
            dve.wait_ge(s_load, 32)
            step(dve.tensor_tensor(diff[:], di[:], dp[:], ALU.subtract))
            step(dve.tensor_scalar(b1[:], diff[:], 0.0, None, ALU.is_lt))
            step(dve.tensor_scalar(b2[:], diff[:], 1.0, None, ALU.is_gt))
            step(dve.tensor_tensor(b1[:], b1[:], b2[:], ALU.add))
            dve.tensor_reduce(bs[:], b1[:], AX.X, ALU.add).then_inc(s_sum, 1)
            dve.wait_ge(s_tot, 1)
            step(dve.tensor_copy(g.unsorted[:], tot[:]))

        @block.tensor
        def _(pe):
            pe.wait_ge(s_sum, 1)
            nc.tensor.matmul(tot[:], g.ones[:, 0:1], bs[:], start=True, stop=True).then_inc(s_tot, 1)


def sort_stage(nc, g):
    CH_E = 3520
    with ExitStack() as ctx:
        sb = lambda n, s, d: ctx.enter_context(nc.sbuf_tensor(n, s, d))
        node = sb("srt_node", [1, N], I32)
        rec = sb("srt_rec", [P, T, 4], I32)
        cols = sb("srt_cols", [P, 3, T], I32)
        dcol = sb("srt_dcol", [P, T], F32)
        ecol_i = sb("srt_ecol_i", [P, T], I32)
        ecol = sb("srt_ecol", [P, T], F32)
        rank = sb("srt_rank", [P, T], F32)
        rank_i = sb("srt_rank_i", [P, T], I32)
        row_i = sb("srt_row_i", [P, CH_E], I32)
        row = sb("srt_row", [P, CH_E], F32)
        place_i = sb("srt_place_i", [P, CH_E], I32)
        place = sb("srt_place", [P, CH_E], F32)
        before = sb("srt_before", [P, CH_E], F32)
        junk = sb("srt_junk", [P, CH_E], F32)
        lt = sb("srt_lt", [P, 1], F32)
        eq = sb("srt_eq", [P, 1], F32)
        idx1 = sb("srt_idx1", [P, 1], I32)
        rec1 = sb("srt_rec1", [P, 4], I32)
        s_io = g.sem("srt_iota"); s_dma = g.sem("srt_dma"); s_row = g.sem("srt_row")
        s_used = g.sem("srt_row_used"); s_rank = g.sem("srt_ranked"); s_st = g.sem("srt_staged")
        s_sc = g.sem("srt_scattered"); s_dve = g.sem("srt_dve"); s_out = g.sem("srt_out")
        s_sep = g.sem("srt_separate"); s_turn = g.sem("srt_turn")
        block = ctx.enter_context(nc.Block())
        arrays = (g.S_dst, g.S_src, g.S_typ)

        def flat(a):
            return a[EPAD:EPAD + E].rearrange("(p j) -> p j", p=P)

        @block.sync
        def _(sp):
            unsorted = sp.value_load(g.unsorted[0:1, 0:1], min_val=0, max_val=E)
            with sp.If(unsorted > 0):
                sp.wait_ge(s_io, 3)
                sp.dma_start(g.S_dst[EPAD + E0:EPAD + E0 + N].unsqueeze(0), node[:]).then_inc(s_dma, 16)
                sp.wait_ge(s_dma, 16)
                for k, a in enumerate(arrays):
                    sp.dma_start(cols[:, k, :], flat(a)).then_inc(s_dma, 16)
                with sp.Fori(0, E // CH_E) as c:
                    sp.wait_ge(s_used, c + 1)
                    sp.dma_start(row_i[:], g.S_dst[bass.ds(c * CH_E + EPAD, CH_E)].partition_broadcast(P)).then_inc(s_row, 16)
                sp.wait_ge(s_sc, 16 * T)
                sp.dma_start(rec[:], g.S_rec.rearrange("(p j) w -> p j w", p=P)).then_inc(s_out, 16)
                sp.wait_ge(s_sep, 1)
                for k, a in enumerate(arrays):
                    sp.dma_start(flat(a), cols[:, k, :]).then_inc(s_out, 16)
                sp.wait_ge(s_out, 64)

        @block.gpsimd
        def _(pool):
            unsorted = pool.value_load(g.unsorted[0:1, 0:1], min_val=0, max_val=E)
            with pool.If(unsorted > 0):
                pool.iota(node[:], [[1, N]], base=0, channel_multiplier=0).then_inc(s_io, 1)
                pool.iota(ecol_i[:], [[1, T]], base=0, channel_multiplier=T).then_inc(s_io, 1)
                pool.iota(place_i[:], [[1, CH_E]], base=0, channel_multiplier=0).then_inc(s_io, 1)
                pool.wait_ge(s_rank, 1)
                with pool.Fori(0, T) as j:
                    pool.tensor_copy(idx1[:], rank_i[:, bass.ds(j, 1)]).then_inc(s_st, 1)
                    pool.tensor_copy(rec1[:], rec[:, bass.ds(j, 1), :].rearrange("p a w -> p (a w)")).then_inc(s_st, 1)
                    pool.wait_ge(s_st, 2 * j + 2)
                    pool.sem_inc(s_turn, 1)
                    pool.indirect_dma_start(g.S_rec, bass.IndirectOffsetOnAxis(idx1[:], axis=0), rec1[:], None).then_inc(s_sc, 16)
                    pool.wait_ge(s_sc, 16 * j + 16)

        @block.vector
        def _(dve):
            unsorted = dve.value_load(g.unsorted[0:1, 0:1], min_val=0, max_val=E)
            with dve.If(unsorted > 0):
                step = Steps(dve, s_dve)
                dve.wait_ge(s_io, 3)
                dve.wait_ge(s_dma, 64)
                step(dve.memset(rec[:], 0))
                for k in range(3):
                    step(dve.tensor_copy(rec[:, :, k], cols[:, k, :]))
                step(dve.tensor_copy(dcol[:], cols[:, 0, :]))
                step(dve.tensor_copy(ecol[:], ecol_i[:]))
                step(dve.tensor_copy(place[:], place_i[:]))
                step(dve.memset(rank[:], 0.0))
                dve.sem_inc(s_used, 1)
                n0 = step.n
                per = 2 + 5 * T
                with dve.Fori(0, E // CH_E) as c:
                    step.n = n0 + c * per
                    dve.wait_ge(s_row, 16 * c + 16)
                    step(dve.tensor_copy(row[:], row_i[:]))
                    dve.sem_inc(s_used, 1)
                    n1 = step.n
                    with dve.Fori(0, T) as j:
                        step.n = n1 + j * 5
                        d1, e1, r1 = (x[:, bass.ds(j, 1)] for x in (dcol, ecol, rank))
                        step(dve.tensor_scalar(before[:], place[:], e1, None, ALU.is_lt))
                        dve.scalar_tensor_tensor(junk[:], row[:], d1, before[:], ALU.is_equal, ALU.mult, accum_out=eq[:]).then_inc(s_dve, 1)
                        dve.wait_ge(s_dve, step.n + 1)
                        dve.tensor_scalar(junk[:], row[:], d1, 0.0, ALU.is_lt, ALU.add, accum_out=lt[:]).then_inc(s_dve, 1)
                        step.n = step.n + 2
                        dve.wait_ge(s_dve, step.n)
                        step(dve.tensor_tensor(r1, r1, lt[:], ALU.add))
                        step(dve.tensor_tensor(r1, r1, eq[:], ALU.add))
                    step.n = n1 + 5 * T
                    step(dve.tensor_scalar(ecol[:], ecol[:], float(CH_E), None, ALU.subtract))
                dve.tensor_copy(rank_i[:], rank[:]).then_inc(s_rank, 1)
                dve.wait_ge(s_out, 16)
                for k in range(3):
                    ins = dve.tensor_copy(cols[:, k, :], rec[:, :, k])
                ins.then_inc(s_sep, 1)


def tables_stage(nc, g):
    with ExitStack() as ctx:
        sb = lambda n, s, d: ctx.enter_context(nc.sbuf_tensor(n, s, d))
        lane_i = sb("lane_i", [LANES, 3, LC, P], I32)
        prev_i = sb("prev_i", [LANES, 2, LC, P], I32)
        lane = sb("lane", [LANES, 3, LC, P], F32)
        dstT = sb("dstT", [P, T], F32)
        ps = [ctx.enter_context(nc.psum_tensor(f"tab_ps{k}", [P, 512], F32)) for k in range(4)]
        s_ld = g.sem("tab_load"); s_dve = g.sem("tab_dve"); s_lane = g.sem("tab_lane")
        s_tr = g.sem("tab_tr"); s_dT = g.sem("tab_dT"); s_base = g.sem("tab_base")
        block = ctx.enter_context(nc.Block())

        def lanes(a, shift=0):
            return a[EPAD + shift:EPAD + shift + E].rearrange("(c q f) -> q c f", c=LC, f=P)

        @block.sync
        def _(sp):
            for k, a in enumerate((g.S_dst, g.S_src, g.S_typ)):
                sp.dma_start(lane_i[:, k], lanes(a)).then_inc(s_ld, 16)
            sp.dma_start(prev_i[:, 0], lanes(g.S_dst, -1)).then_inc(s_ld, 16)
            sp.dma_start(prev_i[:, 1], lanes(g.S_dst, 1)).then_inc(s_ld, 16)

        @block.vector
        def _(dve):
            step = Steps(dve, s_dve)
            dve.wait_ge(s_ld, 80)
            step(dve.tensor_copy(lane[:], lane_i[:]))
            step(dve.scalar_tensor_tensor(lane[:, 2], lane[:, 2], float(NP), lane[:, 1], ALU.mult, ALU.add))
            step(dve.tensor_scalar(lane[:, 2], lane[:, 2], float(ZERO_ROW), None, ALU.min))
            step(dve.tensor_tensor(g.first[:], lane[:, 0], prev_i[:, 0], ALU.not_equal))
            dve.tensor_tensor(g.endneg[:], lane[:, 0], prev_i[:, 1], ALU.not_equal).then_inc(s_lane, 1)
            step(dve.tensor_scalar(g.firstneg[:], g.first[:], -BIG, None, ALU.mult))
            dve.wait_ge(s_lane, 1)
            step(dve.tensor_scalar(g.endneg[:], g.endneg[:], -BIG, None, ALU.mult))
            dve.memset(g.srcI[:, T:], 0).then_inc(s_dve, 1)
            dve.memset(g.relI[:, T:], 0).then_inc(s_dve, 1)
            dve.memset(g.dstI[:, T:], 0).then_inc(s_dve, 1)
            step.n += 3
            step(dve.memset(g.dstrel[:, T:], 0.0))
            dve.wait_ge(s_tr, 1)
            dve.tensor_copy(dstT[:], ps[0][:, 0:T]).then_inc(s_dT, 1)
            step(dve.tensor_copy(g.dstI[:, 0:T], ps[0][:, 0:T]))
            dve.wait_ge(s_tr, 2)
            step(dve.tensor_copy(g.srcI[:, 0:T], ps[1][:, 0:T]))
            dve.wait_ge(s_tr, 3)
            step(dve.tensor_copy(g.relI[:, 0:T], ps[2][:, 0:T]))
            dve.wait_ge(s_base, 1)
            step(dve.tensor_tensor(g.dstrel[:, 0:T], dstT[:], ps[3][:, 0:T], ALU.subtract))
            step(dve.tensor_copy(g.base[:], ps[3][0:1, 0:T]))

        @block.tensor
        def _(pe):
            pe.wait_ge(s_lane, 1)
            for k in range(3):
                for c in range(LC):
                    ins = nc.tensor.transpose(ps[k][:, c * LANES:(c + 1) * LANES], lane[:, k, c, :], g.ident[0:LANES, 0:LANES])
                ins.then_inc(s_tr, 1)
            pe.wait_ge(s_dT, 1)
            nc.tensor.matmul(ps[3][:, 0:T], g.ones[0:1, :], dstT[0:1, :], start=True, stop=True).then_inc(s_base, 1)


def layernorm(nc, g, dve, step, s_var, s_sqrt, k, src, dst):
    st, mean, var, r, t1, t2 = g.ln_st, g.ln_mean, g.ln_var, g.ln_r, g.ln_t1, g.ln_t2
    n0 = step.n
    with dve.Fori(0, NT) as t:
        nc.vector.bn_stats(st[:, bass.ds(t, 1), :].rearrange("p a w -> p (a w)"),
                           src[:, bass.ds(t, 1), :].rearrange("p a w -> p (a w)")).then_inc(step.sem, 1)
    step.n = n0 + NT
    dve.wait_ge(step.sem, step.n)
    step(dve.tensor_tensor(mean[:], st[:, :, 1], st[:, :, 4], ALU.add))
    step(dve.tensor_scalar(mean[:], mean[:], 0.5, None, ALU.mult))
    step(dve.tensor_tensor(t1[:], st[:, :, 1], st[:, :, 4], ALU.subtract))
    step(dve.tensor_tensor(t1[:], t1[:], t1[:], ALU.mult))
    step(dve.tensor_tensor(t2[:], st[:, :, 2], st[:, :, 5], ALU.add))
    step(dve.scalar_tensor_tensor(t1[:], t1[:], float(D) / 4, t2[:], ALU.mult, ALU.add))
    step(dve.tensor_scalar(var[:], t1[:], 1.0 / D, EPS, ALU.mult, ALU.add))
    dve.sem_inc(s_var, 1)
    dve.wait_ge(s_sqrt, k)
    step(dve.reciprocal(r[:], g.ln_s[:]))
    step(dve.tensor_tensor(t1[:], r[:], r[:], ALU.mult))
    step(dve.tensor_tensor(t1[:], t1[:], var[:], ALU.mult))
    step(dve.tensor_scalar(t1[:], t1[:], -0.5, 1.5, ALU.mult, ALU.add))
    step(dve.tensor_tensor(r[:], r[:], t1[:], ALU.mult))
    n0 = step.n
    with dve.Fori(0, NT) as t:
        nc.vector.tensor_scalar(dst[:, bass.ds(t, 1), :].rearrange("p a w -> p (a w)"),
                                src[:, bass.ds(t, 1), :].rearrange("p a w -> p (a w)"),
                                mean[:, bass.ds(t, 1)], r[:, bass.ds(t, 1)], ALU.subtract, ALU.mult).then_inc(step.sem, 1)
    step.n = n0 + NT
    dve.wait_ge(step.sem, step.n)


def gat_table_stage(nc, g):
    with ExitStack() as ctx:
        sb = lambda n, s, d: ctx.enter_context(nc.sbuf_tensor(n, s, d))
        w = sb("gat_w", [P, KD, D], F32)
        attT = sb("gat_attT", [8, P], F32)
        att = sb("gat_att", [P, KD, 8], F32)
        attc = sb("gat_attc", [P, 4], F32)
        wt = sb("gat_wt", [P, KD, HROW], F32)
        xT = sb("gat_xT", [P, 2, KD, P], F32)
        hst = sb("gat_hst", [P, 2, HROW], F32)
        pads = sb("gat_pads", [P, 1], F32)
        ps_t = [ctx.enter_context(nc.psum_tensor(f"gt_t{k}", [P, 512], F32)) for k in range(2)]
        ps_h = [ctx.enter_context(nc.psum_tensor(f"gt_h{k}", [P, 512], F32)) for k in range(2)]
        ps_w = ctx.enter_context(nc.psum_tensor("gt_w", [P, 512], F32))
        s_ld = g.sem("gt_load"); s_x = g.sem("gt_x"); s_dve = g.sem("gt_dve"); s_act = g.sem("gt_act"); s_var = g.sem("gt_var")
        s_z = g.sem("gt_zero"); s_ln = g.sem("gt_ln"); s_tr = g.sem("gt_tr"); s_xT = g.sem("gt_xT")
        s_h = g.sem("gt_h"); s_hst = g.sem("gt_hst"); s_w = g.sem("gt_wtr"); s_wt = g.sem("gt_wt"); s_att = g.sem("gt_att")
        s_st = [g.sem("gt_store0"), g.sem("gt_store1")]
        s_a = g.sem("gt_attT"); s_wa = g.sem("gt_wa"); s_zr = g.sem("gt_zr")
        block = ctx.enter_context(nc.Block())

        @block.sync
        def _(sp):
            sp.wait_ge(s_z, 1)
            sp.dma_start(g.X[:, 0:NT - 1, :], g.x[0:(NT - 1) * P, :].rearrange("(t p) d -> p t d", p=P)).then_inc(s_x, 16)
            sp.dma_start(g.X[0:LAST, NT - 1, :], g.x[(NT - 1) * P:N, :]).then_inc(s_x, 16)
            sp.dma_start(w[:], g.gat_w.rearrange("(k p) i -> p k i", p=P)).then_inc(s_ld, 16)
            sp.dma_start(attT[0:2, :], g.att_src.rearrange("(k h) c -> k (h c)", k=KD)).then_inc(s_ld, 16)
            sp.dma_start(attT[2:4, :], g.att_dst.rearrange("(k h) c -> k (h c)", k=KD)).then_inc(s_ld, 16)
            sp.dma_start(g.Gtab[ZERO_ROW:ZERO_ROW + 1, :], g.zrow[0:1, 0:D]).then_inc(s_zr, 16)
            for t in range(NT):
                sp.wait_ge(s_hst, t + 1)
                sp.dma_start(g.Htab[t * P:(t + 1) * P, :], hst[:, t % 2, 0:D]).then_inc(s_st[t % 2], 16)
                sp.dma_start(g.Atab[t * P:(t + 1) * P, :], hst[:, t % 2, D:HROW]).then_inc(s_st[t % 2], 16)
            sp.wait_ge(s_st[0], 32 * ((NT + 1) // 2))
            sp.wait_ge(s_st[1], 32 * (NT // 2))
            sp.wait_ge(s_zr, 16)

        @block.vector
        def _(dve):
            step = Steps(dve, s_dve)
            dve.memset(g.X[:, NT - 1, :], 0.0).then_inc(s_z, 1)
            step(dve.memset(att[:], 0.0))
            dve.wait_ge(s_a, 1)
            for k in range(KD):
                for h in range(2):
                    sl = slice(h * CH, (h + 1) * CH)
                    dve.tensor_copy(att[sl, k, 2 * k + h:2 * k + h + 1], ps_w[sl, k:k + 1])
                    ins = dve.tensor_copy(att[sl, k, 4 + 2 * k + h:5 + 2 * k + h], ps_w[sl, 2 + k:3 + k])
            ins.then_inc(s_att, 1)
            dve.wait_ge(s_x, 32)
            layernorm(nc, g, dve, step, s_var, s_act, 1, g.X, g.Y)
            dve.sem_inc(s_ln, 1)
            step(dve.tensor_scalar(pads[:], g.valid[:], 1.0, BIG, ALU.subtract, ALU.mult))
            for t in range(NT):
                dve.wait_ge(s_h, t + 1)
                if t >= 2:
                    dve.wait_ge(s_st[t % 2], 32 * (t // 2))
                if t < NT - 1:
                    dve.tensor_copy(hst[:, t % 2, :], ps_h[t % 2][:, 0:HROW]).then_inc(s_hst, 1)
                else:
                    step(dve.tensor_copy(hst[:, t % 2, :], ps_h[t % 2][:, 0:HROW]))
                    dve.tensor_scalar(hst[:, t % 2, D:D + HEADS], ps_h[t % 2][:, D:D + HEADS], pads[:], None, ALU.add).then_inc(s_hst, 1)

        @block.scalar
        def _(act):
            act.wait_ge(s_w, 1)
            for j in range(KD):
                ins = nc.scalar.activation(wt[:, j, 0:D], ps_t[j][:, 0:D], ACT.Copy)
            ins.then_inc(s_wt, 1)
            act.wait_ge(s_wa, 1)
            nc.scalar.activation(wt[:, :, D:HROW], ps_w[:, 16:16 + KD * 8].rearrange("p (k a) -> p k a", k=KD), ACT.Copy).then_inc(s_wt, 1)
            act.wait_ge(s_var, 1)
            nc.scalar.activation(g.ln_s[:], g.ln_var[:], ACT.Sqrt).then_inc(s_act, 1)
            for t in range(NT):
                act.wait_ge(s_tr, t + 1)
                if t >= 2:
                    act.wait_ge(s_h, t - 1)
                nc.scalar.activation(xT[:, t % 2], ps_t[t % 2][:, 0:D].rearrange("p (k n) -> p k n", k=KD), ACT.Copy).then_inc(s_xT, 1)

        @block.tensor
        def _(pe):
            pe.wait_ge(s_ld, 48)
            nc.tensor.transpose(ps_w[:, 0:4], attT[0:4, :], g.ident[0:4, 0:4]).then_inc(s_a, 1)
            for j in range(KD):
                for k in range(KD):
                    ins = nc.tensor.transpose(ps_t[j][:, k * P:(k + 1) * P], w[:, k, j * P:(j + 1) * P], g.ident[:])
            ins.then_inc(s_w, 1)
            pe.wait_ge(s_att, 1)
            for j in range(KD):
                for k in range(KD):
                    ins = nc.tensor.matmul(ps_w[:, 16 + j * 8:24 + j * 8], w[:, k, j * P:(j + 1) * P], att[:, k, :], start=(k == 0), stop=(k == KD - 1))
            ins.then_inc(s_wa, 1)
            pe.wait_ge(s_wt, 2)
            pe.wait_ge(s_ln, 1)

            def transposes(t):
                if t >= 2:
                    pe.wait_ge(s_xT, t - 1)
                for k in range(KD):
                    ins = nc.tensor.transpose(ps_t[t % 2][:, k * P:(k + 1) * P], g.Y[:, t, k * P:(k + 1) * P], g.ident[:])
                ins.then_inc(s_tr, 1)

            transposes(0)
            for t in range(NT):
                if t + 1 < NT:
                    transposes(t + 1)
                pe.wait_ge(s_xT, t + 1)
                if t >= 2:
                    pe.wait_ge(s_hst, t - 1)
                for k in range(KD):
                    ins = nc.tensor.matmul(ps_h[t % 2][:, 0:HROW], xT[:, t % 2, k, :], wt[:, k, :], start=(k == 0), stop=(k == KD - 1))
                ins.then_inc(s_h, 1)


def scores_stage(nc, g):
    with ExitStack() as ctx:
        sb = lambda n, s, d=F32: ctx.enter_context(nc.sbuf_tensor(n, s, d))
        vals = sb("sc_vals", [P, NT + 1, 8])
        rest = sb("sc_rest", [P, NT + 1, 8])
        part = sb("sc_part", [P, 3, NT + 1, 8], BF16)
        ident = sb("sc_ident", [P, P], BF16)
        lane_i = sb("sc_lane_i", [LANES, 2, LC, P], I32)
        rem_i = sb("sc_rem_i", [LANES, 2, LC, P], I32)
        rem = sb("sc_rem", [LANES, 2, LC, P], BF16)
        colq = sb("sc_colq", [P, 2, T], I32)
        baseq_i = sb("sc_baseq_i", [P, T], I32)
        baseq = sb("sc_baseq", [P, T])
        qs = sb("sc_qs", [P, T]); upw = sb("sc_upw", [P, 2, T])
        hot = sb("sc_hot", [P, 2, 2, LC * P], BF16)
        gap = sb("sc_gap", [P, 2, LC * P])
        hotq = sb("sc_hotq", [P, 2, LC, NT])
        hit = sb("sc_hit", [P, 2, LC, NT, HEADS])
        two = sb("sc_two", [P, 2, LC, 2, 8])
        negr = sb("sc_negr", [P, 1])
        ps_b = [[ctx.enter_context(nc.psum_tensor(f"sc_b{k}{w}", [P, 512], F32)) for w in range(2)] for k in range(2)]
        ps_v = [[ctx.enter_context(nc.psum_tensor(f"sc_v{k}{w}", [P, 512], F32)) for w in range(2)] for k in range(2)]
        s_ld = g.sem("sc_load"); s_dve = g.sem("sc_dve"); s_set = g.sem("sc_set")
        s_b = g.sem("sc_bcast")
        s_hs = g.sem("sc_hot_src"); s_hd = g.sem("sc_hot_dst"); s_gap = g.sem("sc_gap")
        s_v = g.sem("sc_values")
        s_out = g.sem("sc_out")
        s_pick = g.sem("sc_pick")
        block = ctx.enter_context(nc.Block())
        MASK, SHIFT = P - 1, P.bit_length() - 1

        @block.sync
        def _(sp):
            for k, a in enumerate((g.S_src, g.S_dst)):
                sp.dma_start(lane_i[:, k], a[EPAD:EPAD + E].rearrange("(c q f) -> q c f", c=LC, f=P)).then_inc(s_ld, 16)
            sp.dma_start(vals[:, 0:NT, :], g.Atab.rearrange("(t p) a -> p t a", p=P)).then_inc(s_ld, 16)

        @block.vector
        def _(dve):
            step = Steps(dve, s_dve)
            step(dve.memset(vals[:, NT, :], 0.0))
            step(dve.tensor_copy(ident[:], g.ident[:]))
            step(dve.tensor_scalar(negr[:], g.iotap[:, 0:1], -1.0, None, ALU.mult))
            dve.wait_ge(s_ld, 48)
            step(dve.tensor_scalar(rem_i[:], lane_i[:], MASK, None, ALU.bitwise_and))
            step(dve.tensor_copy(rem[:], rem_i[:]))
            step(dve.tensor_copy(part[:, 0], vals[:]))
            step(dve.tensor_tensor(rest[:], vals[:], part[:, 0], ALU.subtract))
            step(dve.tensor_copy(part[:, 1], rest[:]))
            step(dve.tensor_tensor(rest[:], rest[:], part[:, 1], ALU.subtract))
            step(dve.tensor_copy(part[:, 2], rest[:]))
            step(dve.tensor_scalar(colq[:, 0], g.srcI[:, 0:T], SHIFT, None, ALU.arith_shift_right))
            step(dve.tensor_scalar(colq[:, 1], g.dstI[:, 0:T], SHIFT, None, ALU.arith_shift_right))
            step(dve.tensor_tensor(baseq_i[:], g.dstI[:, 0:T], g.dstrel[:, 0:T], ALU.subtract))
            step(dve.tensor_scalar(baseq_i[:], baseq_i[:], SHIFT, None, ALU.arith_shift_right))
            step(dve.tensor_copy(g.baseq[:].rearrange("a (q c) -> a c q", c=LC), baseq_i[0:1, :].rearrange("a (c q) -> a c q", c=LC)))
            step(dve.tensor_copy(qs[:], colq[:, 0]))
            step(dve.tensor_tensor(upw[:, 1], colq[:, 1], baseq_i[:], ALU.subtract))
            step(dve.tensor_scalar(upw[:, 0], upw[:, 1], -1.0, 1.0, ALU.mult, ALU.add))
            dve.sem_inc(s_set, 1)
            dve.sem_inc(s_out, 2)
            qs4 = qs[:].rearrange("p (c q) -> p c q", c=LC)
            upw4 = upw[:].rearrange("p w (c q) -> p w c q", c=LC)

            def hot_src(q, par):
                dve.wait_ge(s_b, q + 1)
                dve.wait_ge(s_v, q + 1)
                dve.tensor_scalar(hot[:, par, 0], ps_b[par][0][:], g.iotap[:, 0:1], None, ALU.is_equal).then_inc(s_hs, 1)

            def marks(q, par):
                dve.tensor_tensor(hotq[:, par], bcast(g.iota[:, 0:NT], 1, LC),
                                  qs4[:, :, bass.ds(q, 1)].to_broadcast([P, LC, NT]), ALU.is_equal).then_inc(s_dve, 1)

            def pick(q, par, n0, ahead=2):
                dve.wait_ge(s_v, q + 3)
                dve.wait_ge(s_dve, n0)
                v = ps_v[par][0][:, 0:LC * NT * HEADS].rearrange("p (c q h) -> p (c q) h", c=LC, q=NT)
                dve.tensor_tensor(hit[:, par].rearrange("p c q h -> p (c q) h"), v,
                                  bcast(hotq[:, par].rearrange("p c q -> p (c q)"), 2, HEADS), ALU.mult).then_inc(s_dve, 1)
                d = ps_v[par][1][:, 0:LC * 16].rearrange("p (c w a) -> p c w a", c=LC, w=2)
                which = bcast(upw4[:, :, :, bass.ds(q, 1)].rearrange("p w c a -> p c (w a)"), 3, 8)
                dve.tensor_tensor(two[:, par], d, which, ALU.mult).then_inc(s_dve, 1)
                if ahead == 2:
                    hot_src(q + 2, par)
                dve.wait_ge(s_dve, n0 + 1)
                dve.tensor_reduce(g.AS4[:, :, bass.ds(q, 1), 0:4].rearrange("p c a h -> p c (a h)"),
                                  hit[:, par].rearrange("p c q h -> p c h q"), AX.X, ALU.add).then_inc(s_dve, 1)
                if ahead >= 1:
                    marks(q + 1, 1 - par)
                dve.wait_ge(s_dve, n0 + 2)
                dve.tensor_reduce(g.AS4[:, :, bass.ds(q, 1), 4:12].rearrange("p c a h -> p c (a h)"),
                                  two[:, par].rearrange("p c w a -> p c a w"), AX.X, ALU.add).then_inc(s_out, 1)

            PER = 4
            hot_src(0, 0)
            hot_src(1, 1)
            marks(0, 0)
            n1 = step.n + 1
            with dve.Fori(0, LANES // 2 - 1) as i:
                for par in range(2):
                    q = i * 2 + par
                    pick(q, par, n1 + q * PER)
            pick(LANES - 2, 0, n1 + (LANES - 2) * PER, 1)
            pick(LANES - 1, 1, n1 + (LANES - 1) * PER, 0)

        @block.scalar
        def _(act):
            act.wait_ge(s_set, 1)
            with act.Fori(0, LANES // 2) as i:
                for par in range(2):
                    q = i * 2 + par
                    act.wait_ge(s_b, q + 1)
                    act.wait_ge(s_v, q + 1)
                    nc.scalar.activation(gap[:, par], ps_b[par][1][:], ACT.Abs, bias=negr[:]).then_inc(s_gap, 1)
                    act.wait_ge(s_gap, q + 1)
                    nc.scalar.activation(hot[:, par, 1], gap[:, par], ACT.Relu, bias=1.0, scale=-1.0).then_inc(s_hd, 1)

        @block.tensor
        def _(pe):
            pe.wait_ge(s_set, 1)
            pe.sem_inc(s_v, 2)

            def spread(q, par):
                for w in range(2):
                    ins = nc.tensor.matmul(ps_b[par][w][:], ident[0:LANES, bass.ds(q, 1)].to_broadcast([LANES, P]),
                                           rem[:, w].rearrange("q c f -> q (c f)"), start=True, stop=True)
                ins.then_inc(s_b, 1)

            def values(q, par):
                bqs = load_values(nc, mybir.EngineType.PE, g.baseq[0:1, bass.ds(q * LC, LC)], NT - 1)
                pe.wait_ge(s_out, q + 1)
                pe.wait_ge(s_hs, q + 1)
                for c in range(LC):
                    for j in range(3):
                        nc.tensor.matmul(ps_v[par][0][:, c * NT * HEADS:(c + 1) * NT * HEADS], hot[:, par, 0, c * P:(c + 1) * P],
                                         part[:, j, 0:NT, 0:HEADS], start=(j == 0), stop=(j == 2))
                pe.wait_ge(s_hd, q + 1)
                for c, bq in enumerate(bqs):
                    for j in range(3):
                        ins = nc.tensor.matmul(ps_v[par][1][:, c * 16:(c + 1) * 16], hot[:, par, 1, c * P:(c + 1) * P],
                                               part[:, j, bass.ds(bq, 2), :].rearrange("p q a -> p (q a)"), start=(j == 0), stop=(j == 2))
                ins.then_inc(s_v, 1)

            spread(0, 0)
            with pe.Fori(0, LANES // 2 - 1) as i:
                for par in range(2):
                    q = i * 2 + par
                    spread(q + 1, 1 - par)
                    values(q, par)
            spread(LANES - 1, 1)
            values(LANES - 2, 0)
            values(LANES - 1, 1)


def softmax_stage(nc, g):
    with ExitStack() as ctx:
        sb = lambda n, s, d: ctx.enter_context(nc.sbuf_tensor(n, s, d))
        L = sb("sm_L", [LANES, 12, LC, P], F32)
        fw = sb("sm_fw", [LANES, HEADS, LC, P], F32)
        bw = sb("sm_bw", [LANES, HEADS, LC, P], F32)
        tails = sb("sm_tails", [LANES, 2, LC, 8], F32)
        rowt = sb("sm_rowt", [HEADS, 2, 2, T], F32)
        inc = sb("sm_inc", [HEADS, 2, T + 1], F32)
        carry = sb("sm_carry", [LANES, 2, LC, HEADS], F32)
        notfirst = sb("sm_notfirst", [LANES, LC, P], F32)
        pe_out = sb("sm_p", [LANES, 8, LC, P], F32)
        ps = [ctx.enter_context(nc.psum_tensor(f"sm_ps{k}", [P, 512], F32)) for k in range(4)]
        ps_r = [ctx.enter_context(nc.psum_tensor(f"sm_row{k}", [HEADS, 512], F32)) for k in range(4)]
        s_tr = g.sem("sm_tr"); s_L = g.sem("sm_L"); s_dve = g.sem("sm_dve"); s_tail = g.sem("sm_tail")
        s_row = g.sem("sm_row"); s_inc = g.sem("sm_inc"); s_car = g.sem("sm_carry")
        s_z = g.sem("sm_z"); s_p = g.sem("sm_pe"); s_pt = g.sem("sm_pt"); s_cp = g.sem("sm_cp")
        block = ctx.enter_context(nc.Block())

        @block.tensor
        def _(pe):
            for a in range(12):
                if a >= 4:
                    pe.wait_ge(s_L, a - 3)
                for c in range(LC):
                    ins = nc.tensor.transpose(ps[a % 4][0:LANES, c * P:(c + 1) * P], g.AS[:, c * LANES:(c + 1) * LANES, a], g.ident[:])
                ins.then_inc(s_tr, 1)
            pe.wait_ge(s_tail, 1)
            for d in range(2):
                for w in range(2):
                    for c in range(LC):
                        ins = nc.tensor.transpose(ps_r[d * 2 + w][:, c * LANES:(c + 1) * LANES], tails[:, d, c, 4 * w:4 * w + 4], g.ident[0:LANES, 0:LANES])
            ins.then_inc(s_row, 1)
            pe.wait_ge(s_inc, 1)
            for d in range(2):
                for c in range(LC):
                    src = inc[:, 0, c * LANES:(c + 1) * LANES] if d == 0 else inc[:, 1, c * LANES + 1:(c + 1) * LANES + 1]
                    ins = nc.tensor.transpose(ps[0][0:LANES, (d * LC + c) * 4:(d * LC + c) * 4 + 4], src, g.ident[0:HEADS, 0:HEADS])
            ins.then_inc(s_car, 1)
            for a in range(8):
                pe.wait_ge(s_p, a + 1)
                if a >= 4:
                    pe.wait_ge(s_pt, a - 3)
                for c in range(LC):
                    ins = nc.tensor.transpose(ps[a % 4][:, c * LANES:(c + 1) * LANES], pe_out[:, a, c, :], g.ident[0:LANES, 0:LANES])
                ins.then_inc(s_cp, 1)

        @block.scalar
        def _(act):
            for a in range(12):
                act.wait_ge(s_tr, a + 1)
                nc.scalar.activation(L[:, a], ps[a % 4][0:LANES, :].rearrange("p (c f) -> p c f", c=LC), ACT.Copy).then_inc(s_L, 1)
            for a in range(8):
                act.wait_ge(s_z, a + 1)
                nc.scalar.activation(pe_out[:, a], pe_out[:, a], ACT.Exp).then_inc(s_p, 1)

        @block.vector
        def _(dve):
            step = Steps(dve, s_dve)
            step(dve.tensor_scalar(notfirst[:], g.first[:], 1.0, BIG, ALU.subtract, ALU.mult))
            dve.wait_ge(s_L, 12)

            def scan(out, d, c, h, initial):
                v, m = L[:, h, c, :], (g.firstneg if d == 0 else g.endneg)[:, c, :]
                o = out[:, h, c, :]
                if d:
                    v, m, o = v[:, ::-1], m[:, ::-1], o[:, ::-1]
                return dve.tensor_tensor_scan(o, m, v, initial, ALU.add, ALU.max)

            n = 0
            for d, out in ((0, fw), (1, bw)):
                for h in range(HEADS):
                    for c in range(LC):
                        scan(out, d, c, h, -BIG).then_inc(s_dve, 1)
                        n += 1
            step.n = step.n + n
            dve.wait_ge(s_dve, step.n)
            dve.tensor_copy(tails[:, 0, :, 0:4].rearrange("q c h -> q h c"), fw[:, :, :, P - 1])
            step(dve.tensor_copy(tails[:, 1, :, 0:4].rearrange("q c h -> q h c"), bw[:, :, :, 0]))
            step(dve.tensor_reduce(tails[:, 0, :, 4], g.firstneg[:], AX.X, ALU.min))
            step(dve.tensor_reduce(tails[:, 1, :, 4], g.endneg[:], AX.X, ALU.min))
            dve.tensor_copy(tails[:, 0, :, 5:8], bcast(tails[:, 0, :, 4], 2, 3))
            step(dve.tensor_copy(tails[:, 1, :, 5:8], bcast(tails[:, 1, :, 4], 2, 3)))
            dve.sem_inc(s_tail, 1)
            dve.memset(inc[:, 0, 0:1], -BIG)
            step(dve.memset(inc[:, 1, T:T + 1], -BIG))
            dve.wait_ge(s_row, 1)
            for d in range(2):
                for w in range(2):
                    step(dve.tensor_copy(rowt[:, d, w, :], ps_r[d * 2 + w][:, 0:T]))
            dve.tensor_tensor_scan(inc[:, 0, 1:T + 1], rowt[:, 0, 1, :], rowt[:, 0, 0, :], -BIG, ALU.add, ALU.max)
            step(dve.tensor_tensor_scan(inc[:, 1, 0:T][:, ::-1], rowt[:, 1, 1, :][:, ::-1], rowt[:, 1, 0, :][:, ::-1], -BIG, ALU.add, ALU.max))
            dve.sem_inc(s_inc, 1)
            dve.wait_ge(s_car, 1)
            step(dve.tensor_copy(carry[:], ps[0][0:LANES, 0:2 * LC * 4].rearrange("p (d c h) -> p d c h", d=2, c=LC)))
            for d, out in ((0, fw), (1, bw)):
                for h in range(HEADS):
                    for c in range(LC):
                        scan(out, d, c, h, carry[:, d, c, h:h + 1]).then_inc(s_dve, 1)
                        step.n += 1
            dve.wait_ge(s_dve, step.n)
            f2 = lambda ap: ap.rearrange("q h c f -> q (h c f)")
            a_s, a_sd, a_d = f2(L[:, 0:4]), f2(L[:, 4:8]), f2(L[:, 8:12])
            M, B = f2(fw[:]), f2(bw[:])
            step(dve.tensor_tensor(M, M, B, ALU.max))
            step(dve.tensor_tensor(M, M, a_sd, ALU.max))
            step(dve.tensor_tensor(M, M, a_d, ALU.add))
            step(dve.scalar_tensor_tensor(M, M, NEG_SLOPE, M, ALU.mult, ALU.max))
            for w, a in ((0, a_s), (1, a_sd)):
                z = f2(pe_out[:, 4 * w:4 * w + 4])
                step(dve.tensor_tensor(z, a, a_d, ALU.add))
                step(dve.scalar_tensor_tensor(z, z, NEG_SLOPE, z, ALU.mult, ALU.max))
                step(dve.tensor_tensor(z, z, M, ALU.subtract))
                if w == 1:
                    step(dve.tensor_tensor(pe_out[:, 4:8], pe_out[:, 4:8], bcast(notfirst[:], 1, HEADS), ALU.add))
                dve.sem_inc(s_z, 4)
            dve.wait_ge(s_p, 8)
            for a in range(8):
                dve.wait_ge(s_cp, a + 1)
                dve.tensor_copy(g.PT[:, 0:T, a], ps[a % 4][:, 0:T]).then_inc(s_pt, 1)


def edge_pass(nc, g, kind, table, index, n_pass):
    gat = kind == "gat"
    AHEAD = 3
    NBK = 5
    with ExitStack() as ctx:
        sb = lambda n, s, d=F32: ctx.enter_context(nc.sbuf_tensor(f"{n}{n_pass}", s, d))
        ix = sb("ix", [P, 2, HALF], I32)
        ring = sb("ring", [P, RING, D])
        hot = sb("hot", [P, RING, WIN])
        gap = sb("gap", [P, 2, WIN])
        negd = sb("negd", [P, T])
        p8 = sb("p8", [P, RING, 8])
        ps = [ctx.enter_context(nc.psum_tensor(f"ep{n_pass}_{k}", [P, 512], F32)) for k in range(NBK)]
        s_ix = g.sem("ep_idx"); s_turn = g.sem("ep_turn")
        s_g = [g.sem(f"ep_g{k}") for k in range(RING)]
        s_gap = g.sem("ep_gap"); s_hot = g.sem("ep_hot")
        s_p8 = g.sem("ep_p8"); s_msg = g.sem("ep_msg")
        s_mm = g.sem("ep_mm")
        s_acc = g.sem("ep_acc")
        s_zero = g.sem("ep_zero"); s_neg = g.sem("ep_neg")
        block = ctx.enter_context(nc.Block())

        def rounds(eng, body):
            with eng.Fori(0, T // RING - 1) as i:
                body(i, False)
            body(T // RING - 1, True)

        @block.gpsimd
        def _(pool):
            def fetch(i, last):
                for h in range(2):
                    pool.wait_ge(s_mm, i * RING + (h + 1) * HALF)
                    pool.sem_inc(s_turn, 1)
                    pool.tensor_copy(ix[:, h, :], index[:, bass.ds(i * RING + h * HALF, HALF)]).then_inc(s_ix, 1)
                    pool.wait_ge(s_ix, 2 * i + h + 1)
                    pool.sem_inc(s_turn, 1)
                    for k in range(HALF):
                        pool.indirect_dma_start(ring[:, h * HALF + k, :], None, table,
                                                bass.IndirectOffsetOnAxis(ix[:, h, k:k + 1], axis=0)).then_inc(s_g[h * HALF + k], 16)

            rounds(pool, fetch)

        @block.scalar
        def _(act):
            act.wait_ge(s_neg, 1)

            def one_hots(i, last):
                for k in range(RING):
                    tile = i * RING + k
                    act.wait_ge(s_mm, tile + 1)
                    nc.scalar.activation(gap[:, k % 2], g.iota[:], ACT.Abs, bias=negd[:, bass.ds(tile, 1)]).then_inc(s_gap, 1)
                    act.wait_ge(s_gap, tile + 1)
                    nc.scalar.activation(hot[:, k], gap[:, k % 2], ACT.Relu, bias=1.0, scale=-1.0).then_inc(s_hot, 1)
                    if gat:
                        nc.scalar.activation(p8[:, k, :], g.PT[:, bass.ds(tile, 1), :].rearrange("p a w -> p (a w)"), ACT.Copy).then_inc(s_p8, 1)

            rounds(act, one_hots)

        @block.tensor
        def _(pe):
            pe.sem_inc(s_mm, RING)

            def products(i, last):
                for k in range(RING):
                    tile = i * RING + k
                    pe.wait_ge(s_hot, tile + 1)
                    if gat:
                        pe.wait_ge(s_p8, tile + 1)
                        pe.wait_ge(s_msg, tile + 1)
                    else:
                        pe.wait_ge(s_g[k], 16 * i + 16)
                    pe.wait_ge(s_acc, tile + 1)
                    b = ps[k % NBK]
                    for j in range(KD):
                        ins = nc.tensor.matmul(b[:, j * WIN:(j + 1) * WIN], ring[:, k, j * P:(j + 1) * P], hot[:, k, :], start=True, stop=True)
                    if gat:
                        ins = nc.tensor.matmul(b[0:8, KD * WIN:(KD + 1) * WIN], p8[:, k, :], hot[:, k, :], start=True, stop=True)
                    ins.then_inc(s_mm, 1)

            rounds(pe, products)

        @block.vector
        def _(dve):
            dve.tensor_scalar(negd[:], g.dstrel[:, 0:T], -1.0, None, ALU.mult).then_inc(s_neg, 1)
            dve.memset(g.ACC[:], 0.0).then_inc(s_zero, 1)
            if gat:
                dve.memset(g.DEN[:], 0.0).then_inc(s_zero, 1)
            dve.wait_ge(s_zero, 2 if gat else 1)
            dve.sem_inc(s_acc, NBK)

            def weigh(tile, k, r):
                dve.wait_ge(s_g[k], r)
                rows = ring[:, k, :].rearrange("p (a c) -> p a c", a=HEADS)
                dve.tensor_tensor(rows, rows, bcast(g.PT[:, bass.ds(tile, 1), 0:4].rearrange("p a w -> p (a w)"), 2, CH), ALU.mult).then_inc(s_msg, 1)

            def sums(i, last):
                for h in range(2):
                    starts = load_values(nc, mybir.EngineType.DVE, g.base[0:1, bass.ds(i * RING + h * HALF, HALF)], N - 1)
                    for k in range(h * HALF, (h + 1) * HALF):
                        tile = i * RING + k
                        w = k + AHEAD
                        if gat and not (last and w >= RING):
                            weigh(tile + AHEAD, w % RING, 16 * i + 16 * (1 + w // RING))
                        dve.wait_ge(s_mm, tile + (RING + 1))
                        b = ps[k % NBK]
                        acc = g.ACC[:, :, bass.ds(starts[k - h * HALF], WIN)]
                        dve.wait_ge(s_acc, tile + NBK)
                        ins = dve.tensor_tensor(acc, acc, b[:, 0:KD * WIN].rearrange("p (j w) -> p j w", j=KD), ALU.add)
                        if gat:
                            den = g.DEN[:, bass.ds(starts[k - h * HALF], WIN)]
                            ins = dve.tensor_tensor(den, den, b[0:8, KD * WIN:(KD + 1) * WIN], ALU.add)
                        ins.then_inc(s_acc, 1)

            if gat:
                for k in range(AHEAD):
                    weigh(k, k, 16)
            rounds(dve, sums)


def gat_finish_stage(nc, g):
    with ExitStack() as ctx:
        sb = lambda n, s, d: ctx.enter_context(nc.sbuf_tensor(n, s, d))
        Hs = sb("gf_h", [P, NT, D], F32)
        den8 = sb("gf_den8", [P, NT, 8], F32)
        den = sb("gf_den", [P, NT, HEADS], F32)
        bias = sb("gf_bias", [P, D], F32)
        ps = [ctx.enter_context(nc.psum_tensor(f"gf_ps{k}", [P, 512], F32)) for k in range(4)]
        s_ld = g.sem("gf_load"); s_tr = g.sem("gf_tr"); s_cp = g.sem("gf_cp"); s_dve = g.sem("gf_dve")
        s_m = g.sem("gf_min"); s_e = g.sem("gf_exp")
        block = ctx.enter_context(nc.Block())

        @block.sync
        def _(sp):
            sp.dma_start(Hs[:], g.Htab.rearrange("(t p) d -> p t d", p=P)).then_inc(s_ld, 16)
            sp.dma_start(bias[:], g.gat_bias.partition_broadcast(P)).then_inc(s_ld, 16)

        @block.tensor
        def _(pe):
            for t in range(NT):
                if t >= 4:
                    pe.wait_ge(s_cp, t - 3)
                b = ps[t % 4]
                for j in range(KD):
                    nc.tensor.transpose(b[:, j * P:(j + 1) * P], g.ACC[:, j, t * P:(t + 1) * P], g.ident[:])
                nc.tensor.transpose(b[:, D:D + 8], g.DEN[:, t * P:(t + 1) * P], g.ident[0:8, 0:8]).then_inc(s_tr, 1)

        @block.scalar
        def _(act):
            for t in range(NT):
                act.wait_ge(s_tr, t + 1)
                nc.scalar.activation(g.Z[:, t, :], ps[t % 4][:, 0:D], ACT.Copy)
                nc.scalar.activation(den8[:, t, :], ps[t % 4][:, D:D + 8], ACT.Copy).then_inc(s_cp, 1)
            act.wait_ge(s_m, 1)
            nc.scalar.activation(Hs[:], Hs[:], ACT.Exp).then_inc(s_e, 1)

        @block.vector
        def _(dve):
            step = Steps(dve, s_dve)
            dve.wait_ge(s_ld, 32)
            step(dve.tensor_tensor(g.X[:], g.X[:], g.Y[:], ALU.add))
            dve.wait_ge(s_cp, NT)
            heads = lambda ap: ap.rearrange("p t (a c) -> p t a c", a=HEADS)
            step(dve.tensor_tensor(den[:], den8[:, :, 0:4], den8[:, :, 4:8], ALU.add))
            step(dve.tensor_scalar(den[:], den[:], 1e-16, None, ALU.add))
            step(dve.reciprocal(den[:], den[:]))
            step(dve.tensor_tensor(heads(Hs[:]), heads(Hs[:]), bcast(den8[:, :, 4:8], 3, CH), ALU.mult))
            step(dve.tensor_tensor(g.Z[:], g.Z[:], Hs[:], ALU.add))
            step(dve.tensor_tensor(heads(g.Z[:]), heads(g.Z[:]), bcast(den[:], 3, CH), ALU.mult))
            step(dve.tensor_tensor(g.Z[:], g.Z[:], bcast(bias[:], 1, NT), ALU.add))
            step(dve.tensor_scalar(Hs[:], g.Z[:], 0.0, None, ALU.min))
            dve.sem_inc(s_m, 1)
            step(dve.scalar_tensor_tensor(g.X[:], g.Z[:], 0.0, g.X[:], ALU.max, ALU.add))
            dve.wait_ge(s_e, 1)
            step(dve.scalar_tensor_tensor(g.X[:], Hs[:], -1.0, g.X[:], ALU.add, ALU.add))


def router_stage(nc, g, which):
    pre = f"rt{which}_"
    gw_dram, gb_dram = (g.gate_w, g.gate_b) if which == 0 else (g.Wr, g.br)
    trash = NE * B0 if which == 0 else NB1 * B1
    with ExitStack() as ctx:
        sb = lambda n, s, d=F32: ctx.enter_context(nc.sbuf_tensor(pre + n, s, d))
        gw = sb("gw", [P, KD, NE]); gb = sb("gb", [P, NE])
        xT = sb("xT", [P, 2, KD, P])
        L = sb("L", [P, NT, NE]); e1 = sb("e1", [P, NT, NE]); e2 = sb("e2", [P, NT, NE])
        oh = [sb("oh0", [P, NT, NE]), sb("oh1", [P, NT, NE])]
        both = sb("both", [P, NT, NE]); pos = sb("pos", [P, NT, NE]); tot = sb("tot", [P, NT, NE])
        run = sb("run", [P, NT, NE])
        mx = [sb("mx0", [P, NT]), sb("mx1", [P, NT])]
        low = sb("low", [P, NT]); a = sb("a", [P, NT]); b = sb("b", [P, NT]); c = sb("c", [P, NT])
        rtok = sb("rtok", [P, NT]); rtok_i = sb("rtok_i", [P, NT], I32)
        nblk = sb("nblk", [P, NE]); nblk_i = sb("nblk_i", [P, NE], I32); ends = sb("ends", [P, NE]); onesr = sb("onesr", [P, NT])
        start = sb("start", [P, NE]); blk = sb("blk", [1, NB1, NE]); blkn = sb("blkn", [1, NB1])
        slot = sb("slot", [P, 2, NT], I32)
        ps_t = [ctx.enter_context(nc.psum_tensor(f"{pre}t{k}", [P, 512], F32)) for k in range(2)]
        ps_l = ctx.enter_context(nc.psum_tensor(pre + "l", [P, 512], F32))
        ps_p = ctx.enter_context(nc.psum_tensor(pre + "p", [P, 512], F32))
        ps_q = ctx.enter_context(nc.psum_tensor(pre + "q", [P, 512], F32))
        s_ld = g.sem(pre + "load"); s_dve = g.sem(pre + "dve"); s_var = g.sem(pre + "var"); s_sq = g.sem(pre + "sqrt")
        s_ln = g.sem(pre + "ln"); s_tr = g.sem(pre + "tr"); s_xT = g.sem(pre + "xT"); s_lg = g.sem(pre + "logits")
        s_e = g.sem(pre + "exp"); s_ex = g.sem(pre + "exped"); s_oh = g.sem(pre + "onehot"); s_pp = g.sem(pre + "prefix")
        s_slot = g.sem(pre + "slot"); s_sc = g.sem(pre + "scatter"); s_z = g.sem(pre + "zeroed"); s_io = g.sem(pre + "iota")
        s_ln2 = g.sem(pre + "ln2")
        block = ctx.enter_context(nc.Block())
        tokens = g.Y if which == 0 else g.Z

        @block.sync
        def _(sp):
            sp.dma_start(gw[:], gw_dram.rearrange("(k p) e -> p k e", p=P)).then_inc(s_ld, 16)
            sp.dma_start(gb[:], gb_dram.partition_broadcast(P)).then_inc(s_ld, 16)
            rows = g.XB[0:trash, :].rearrange("(r p) d -> p r d", p=P)
            for r in range(0, trash // P, 16):
                sp.dma_start(rows[:, r:r + 16, :], bcast(g.zrow[:], 1, 16)).then_inc(s_z, 16)

        @block.tensor
        def _(pe):
            pe.wait_ge(s_ld, 32)
            pe.wait_ge(s_ln, 1)
            for t in range(NT + 1):
                if t < NT:
                    if t >= 2:
                        pe.wait_ge(s_xT, t - 1)
                    for k in range(KD):
                        ins = nc.tensor.transpose(ps_t[t % 2][:, k * P:(k + 1) * P], g.Y[:, t, k * P:(k + 1) * P], g.ident[:])
                    ins.then_inc(s_tr, 1)
                if t >= 1:
                    u = t - 1
                    pe.wait_ge(s_xT, u + 1)
                    for k in range(KD):
                        ins = nc.tensor.matmul(ps_l[:, u * NE:(u + 1) * NE], xT[:, u % 2, k, :], gw[:, k, :], start=(k == 0), stop=(k == KD - 1))
                    ins.then_inc(s_lg, 1)
            pe.wait_ge(s_oh, 1)
            src = both[:].rearrange("p t e -> p (t e)")
            nc.tensor.matmul(ps_p[:, 0:NT * NE], g.upper[:], src, start=True, stop=True)
            nc.tensor.matmul(ps_q[:, 0:NT * NE], g.ones[:], src, start=True, stop=True).then_inc(s_pp, 1)

        @block.scalar
        def _(act):
            act.wait_ge(s_var, 1)
            nc.scalar.activation(g.ln_s[:], g.ln_var[:], ACT.Sqrt).then_inc(s_sq, 1)
            for t in range(NT):
                act.wait_ge(s_tr, t + 1)
                if t >= 2:
                    act.wait_ge(s_lg, t - 1)
                nc.scalar.activation(xT[:, t % 2], ps_t[t % 2][:, 0:D].rearrange("p (k n) -> p k n", k=KD), ACT.Copy).then_inc(s_xT, 1)
            if which == 1:
                act.wait_ge(s_var, 2)
                nc.scalar.activation(g.ln_s[:], g.ln_var[:], ACT.Sqrt).then_inc(s_sq, 1)
            act.wait_ge(s_e, 1)
            if which == 0:
                nc.scalar.activation(e1[:], e1[:], ACT.Exp).then_inc(s_ex, 1)
            else:
                nc.scalar.activation(a[:], a[:], ACT.Exp).then_inc(s_ex, 1)

        @block.gpsimd
        def _(pool):
            pool.iota(rtok_i[:], [[P, NT]], base=trash, channel_multiplier=1).then_inc(s_io, 1)
            pool.wait_ge(s_slot, 1)
            pool.wait_ge(s_z, 16 * (-(-(trash // P) // 16)))
            n = 0
            for k in range(which + 1):
                for t in range(NT):
                    pool.indirect_dma_start(g.XB, bass.IndirectOffsetOnAxis(slot[:, k, t:t + 1], axis=0), tokens[:, t, :], None).then_inc(s_sc, 16)
                    n += 16
            pool.wait_ge(s_sc, n)

        @block.vector
        def _(dve):
            step = Steps(dve, s_dve)
            layernorm(nc, g, dve, step, s_var, s_sq, 1, g.X, g.Y)
            dve.sem_inc(s_ln, 1)
            if which == 1:
                layernorm(nc, g, dve, step, s_var, s_sq, 2, g.Y, g.Z)
            dve.wait_ge(s_lg, NT)
            lg = ps_l[:, 0:NT * NE].rearrange("p (t e) -> p t e", t=NT)
            step(dve.tensor_tensor(L[:], lg, bcast(gb[:], 1, NT), ALU.add))
            iota8 = bcast(g.iota[:, 0:NE], 1, NT)

            def best(values, m, hot):
                step(dve.tensor_reduce(m[:], values[:], AX.X, ALU.max))
                step(dve.tensor_tensor(hot[:], values[:], bcast(m[:], 2, NE), ALU.is_equal))
                step(dve.scalar_tensor_tensor(e2[:], hot[:], -64.0, iota8, ALU.mult, ALU.add))
                step(dve.tensor_reduce(low[:], e2[:], AX.X, ALU.min))
                step(dve.tensor_tensor(hot[:], e2[:], bcast(low[:], 2, NE), ALU.is_equal))

            best(L, mx[0], oh[0])
            if which == 0:
                step(dve.tensor_tensor(e1[:], L[:], bcast(mx[0][:], 2, NE), ALU.subtract))
            else:
                step(dve.scalar_tensor_tensor(L[:], oh[0][:], -BIG, L[:], ALU.mult, ALU.add))
                best(L, mx[1], oh[1])
                step(dve.tensor_tensor(a[:], mx[1][:], mx[0][:], ALU.subtract))
            dve.sem_inc(s_e, 1)
            for k in range(which + 1):
                step(dve.tensor_scalar(oh[k][:, NT - 1, :], oh[k][:, NT - 1, :], g.valid[:], None, ALU.mult))
            if which == 0:
                step(dve.tensor_copy(both[:], oh[0][:]))
            else:
                step(dve.tensor_tensor(both[:], oh[0][:], oh[1][:], ALU.add))
            dve.sem_inc(s_oh, 1)
            dve.wait_ge(s_ex, 1)
            if which == 0:
                step(dve.tensor_reduce(a[:], e1[:], AX.X, ALU.add))
                step(dve.reciprocal(g.wgt[:, 0, :], a[:]))
            else:
                step(dve.tensor_scalar(b[:], a[:], 1.0, None, ALU.add))
                step(dve.reciprocal(g.wgt[:, 0, :], b[:]))
                step(dve.tensor_tensor(g.wgt[:, 1, :], g.wgt[:, 0, :], a[:], ALU.mult))
            dve.wait_ge(s_pp, 1)
            flat = lambda x: x[:].rearrange("p t e -> p (t e)")
            step(dve.tensor_copy(flat(tot), ps_q[:, 0:NT * NE]))
            step(dve.memset(onesr[:], 1.0))
            for e in range(NE):
                dve.tensor_tensor_scan(run[:, :, e], onesr[:], tot[:, :, e], 0.0, ALU.mult, ALU.add).then_inc(s_dve, 1)
            step.n += NE
            dve.wait_ge(s_dve, step.n)
            step(dve.tensor_tensor(flat(pos), ps_p[:, 0:NT * NE], flat(run), ALU.add))
            step(dve.tensor_tensor(pos[:], pos[:], tot[:], ALU.subtract))
            if which == 0:
                step(dve.tensor_scalar(start[:], g.iota[:, 0:NE], float(B0), -1.0, ALU.mult, ALU.add))
            else:
                step(dve.tensor_scalar(nblk_i[:], run[:, NT - 1, :], float(B1 - 1), None, ALU.add))
                step(dve.tensor_scalar(nblk_i[:], nblk_i[:], B1.bit_length() - 1, None, ALU.arith_shift_right))
                step(dve.tensor_copy(nblk[:], nblk_i[:]))
                step(dve.tensor_tensor_scan(ends[:], onesr[:, 0:NE], nblk[:], 0.0, ALU.mult, ALU.add))
                step(dve.tensor_tensor(start[:], ends[:], nblk[:], ALU.subtract))
                step(dve.tensor_scalar(start[:], start[:], float(B1), -1.0, ALU.mult, ALU.add))
                step(dve.tensor_tensor(blk[:], bcast(ends[0:1, :], 1, NB1), bcast(g.iota[0:1, 0:NB1], 2, NE), ALU.is_le))
                step(dve.tensor_reduce(blkn[:], blk[:], AX.X, ALU.add))
                step(dve.tensor_scalar(blkn[:], blkn[:], float(NE - 1), None, ALU.min))
                step(dve.tensor_copy(g.blk_expert[:], blkn[:]))
            dve.wait_ge(s_io, 1)
            step(dve.tensor_copy(rtok[:], rtok_i[:]))
            step(dve.tensor_tensor(tot[:], pos[:], bcast(start[:], 1, NT), ALU.add))
            for k in range(which + 1):
                step(dve.tensor_tensor(e2[:], tot[:], oh[k][:], ALU.mult))
                step(dve.tensor_reduce(a[:], e2[:], AX.X, ALU.add))
                step(dve.tensor_reduce(c[:], oh[k][:], AX.X, ALU.add))
                if which == 0:
                    step(dve.tensor_tensor(e2[:], pos[:], oh[k][:], ALU.mult))
                    step(dve.tensor_reduce(b[:], e2[:], AX.X, ALU.add))
                    step(dve.tensor_scalar(low[:], b[:], float(CAP), None, ALU.is_le))
                    step(dve.tensor_tensor(c[:], c[:], low[:], ALU.mult))
                    step(dve.tensor_tensor(g.wgt[:, 0, :], g.wgt[:, 0, :], c[:], ALU.mult))
                    step(dve.tensor_scalar(low[:], b[:], float(CAP), 0.0, ALU.subtract, ALU.max))
                    step(dve.tensor_tensor(b[:], a[:], low[:], ALU.subtract))
                    step(dve.tensor_copy(g.gslot[:, k, :], b[:]))
                else:
                    step(dve.tensor_copy(g.gslot[:, k, :], a[:]))
                step(dve.tensor_tensor(a[:], a[:], rtok[:], ALU.subtract))
                step(dve.tensor_tensor(a[:], a[:], c[:], ALU.mult))
                step(dve.tensor_tensor(slot[:, k, :], a[:], rtok[:], ALU.add))
                step(dve.tensor_scalar(rtok[:], rtok[:], float(NP), None, ALU.add))
            dve.sem_inc(s_slot, 1)


def experts_stage(nc, g, which):
    pre = f"ex{which}_"
    B, NB = (B0, NE) if which == 0 else (B1, NB1)
    S = B // P
    W1, b1, W2, b2 = (g.f0_w1, g.f0_b1, g.f0_w2, g.f0_b2) if which == 0 else (g.f1_w1, g.f1_b1, g.f1_w2, g.f1_b2)
    func = ACT.Relu if which == 0 else ACT.Gelu
    with ExitStack() as ctx:
        sb = lambda n, s, d=F32: ctx.enter_context(nc.sbuf_tensor(pre + n, s, d))
        w1 = sb("w1", [P, 2, KD, F]); w2 = sb("w2", [P, 2, FC, D]); xb = sb("xb", [P, 2, S, D])
        xT = sb("xT", [P, 2, KD, B]); hT = sb("hT", [P, FC, B]); y = sb("y", [P, 2, S, D])
        b1r = sb("b1r", [NE * FC, P]); b1c = sb("b1c", [P, NE * FC]); b2b = sb("b2b", [P, NE, D])
        lnr = sb("lnr", [NE * KD, 2, P]); lnc = sb("lnc", [P, 2, NE * KD])
        ps_x = ctx.enter_context(nc.psum_tensor(pre + "px", [P, KD, 512], F32))
        ps_h = [ctx.enter_context(nc.psum_tensor(f"{pre}ph{k}", [P, 512], F32)) for k in range(2)]
        ps_y = [ctx.enter_context(nc.psum_tensor(f"{pre}py{k}", [P, 512], F32)) for k in range(2)]
        s_c = g.sem(pre + "const"); s_ct = g.sem(pre + "const_tr"); s_cc = g.sem(pre + "const_cp")
        s_w1 = [g.sem(f"{pre}w1_{k}") for k in range(2)]; s_w2 = [g.sem(f"{pre}w2_{k}") for k in range(2)]
        s_xb = [g.sem(f"{pre}xb_{k}") for k in range(2)]; s_yst = [g.sem(f"{pre}yst_{k}") for k in range(2)]
        s_tr = g.sem(pre + "tr")
        s_xT = g.sem(pre + "xT")
        s_h = g.sem(pre + "h")
        s_hT = g.sem(pre + "hT")
        s_y2 = g.sem(pre + "y2")
        s_py = g.sem(pre + "py")
        s_turn = g.sem(pre + "turn")
        block = ctx.enter_context(nc.Block())

        def rounds(eng, body):
            with eng.Fori(0, NB // 2 - 1) as i:
                body(i * 2, i, 0, False)
                body(i * 2 + 1, i, 1, False)
            body(NB - 2, NB // 2 - 1, 0, False)
            body(NB - 1, NB // 2 - 1, 1, True)

        def expert(eng, n):
            return n if which == 0 else eng.value_load(g.blk_expert[0:1, bass.ds(n, 1)], min_val=0, max_val=NE - 1)

        @block.sync
        def _(sp):
            sp.dma_start(b1r[:], b1.rearrange("e (c p) -> (e c) p", p=P)).then_inc(s_c, 16)
            sp.dma_start(b2b[:], b2.partition_broadcast(P)).then_inc(s_c, 16)
            if which == 1:
                sp.dma_start(lnr[:, 0, :], g.ln_g.rearrange("e (k p) -> (e k) p", p=P)).then_inc(s_c, 16)
                sp.dma_start(lnr[:, 1, :], g.ln_b.rearrange("e (k p) -> (e k) p", p=P)).then_inc(s_c, 16)

            def load(n, i, par, last):
                e = expert(sp, n)
                sp.wait_ge(s_h, (n + 1) * FC)
                sp.dma_start(xb[:, par], g.XB[bass.ds(n * B, B), :].rearrange("(s p) d -> p s d", p=P)).then_inc(s_xb[par], 16)
                sp.dma_start(w1[:, par], W1[bass.ds(e, 1)].rearrange("a (k p) f -> p (a k) f", p=P)).then_inc(s_w1[par], 16)
                sp.wait_ge(s_y2, (n + 1) * S)
                sp.dma_start(w2[:, par], W2[bass.ds(e, 1)].rearrange("a (c p) d -> p (a c) d", p=P)).then_inc(s_w2[par], 16)

            rounds(sp, load)

        @block.gpsimd
        def _(pool):
            def store(n, i, par, last):
                pool.wait_ge(s_py, n * S + (S + 2))
                pool.sem_inc(s_turn, 1)
                pool.dma_start(g.YB[bass.ds(n * B, B), :].rearrange("(s p) d -> p s d", p=P), y[:, par]).then_inc(s_yst[par], 16)

            for par in range(2):
                pool.dma_start(g.scrap[par:par + 1, :], g.zrow[0:1, :]).then_inc(s_yst[par], 16)
            rounds(pool, store)
            for par in range(2):
                pool.wait_ge(s_yst[par], 16 * (NB // 2) + 16)

        @block.tensor
        def _(pe):
            pe.wait_ge(s_c, 32 + 32 * which)
            ins = nc.tensor.transpose(ps_h[0][:, 0:NE * FC], b1r[:], g.ident[0:NE * FC, 0:NE * FC])
            if which == 1:
                for k in range(2):
                    ins = nc.tensor.transpose(ps_h[1][:, k * 16:k * 16 + 16], lnr[:, k, :], g.ident[0:NE * KD, 0:NE * KD])
            ins.then_inc(s_ct, 1)
            pe.wait_ge(s_cc, 2)
            pe.sem_inc(s_h, 2 * FC)
            pe.sem_inc(s_y2, 2 * S)

            def transposes(par, i):
                pe.wait_ge(s_xb[par], 16 * i + 16)
                for s in range(S):
                    for k in range(KD):
                        ins = nc.tensor.transpose(ps_x[:, k, s * P:(s + 1) * P], xb[:, par, s, k * P:(k + 1) * P], g.ident[:])
                ins.then_inc(s_tr, 1)

            def products(n, i, par, last):
                pe.wait_ge(s_w1[par], 16 * i + 16)
                pe.wait_ge(s_xT, n * KD + KD)
                for c in range(FC):
                    pe.wait_ge(s_hT, n * FC + (c + 1))
                    for k in range(KD):
                        ins = nc.tensor.matmul(ps_h[c % 2][:, 0:B], w1[:, par, k, c * P:(c + 1) * P], xT[:, par, k, :], start=(k == 0), stop=(k == KD - 1))
                    ins.then_inc(s_h, 1)
                if not last:
                    transposes(1 - par, i + par)
                pe.wait_ge(s_w2[par], 16 * i + 16)
                pe.wait_ge(s_hT, n * FC + (FC + 2))
                for s in range(S):
                    pe.wait_ge(s_py, n * S + (s + 1))
                    for c in range(FC):
                        ins = nc.tensor.matmul(ps_y[s % 2][:, 0:D], hT[:, c, s * P:(s + 1) * P], w2[:, par, c, :], start=(c == 0), stop=(c == FC - 1))
                    ins.then_inc(s_y2, 1)

            transposes(0, 0)
            rounds(pe, products)

        @block.scalar
        def _(act):
            act.wait_ge(s_ct, 1)
            nc.scalar.activation(b1c[:], ps_h[0][:, 0:NE * FC], ACT.Copy).then_inc(s_cc, 1)
            act.wait_ge(s_cc, 2)
            act.sem_inc(s_hT, 2)

            def activate(n, i, par, last):
                e = expert(act, n)
                act.wait_ge(s_y2, (n + 2) * S)
                for c in range(FC):
                    act.wait_ge(s_h, n * FC + (c + 1 + 2 * FC))
                    nc.scalar.activation(hT[:, c, :], ps_h[c % 2][:, 0:B], func, bias=b1c[:, bass.ds(e * FC + c, 1)]).then_inc(s_hT, 1)

            rounds(act, activate)

        @block.vector
        def _(dve):
            dve.wait_ge(s_ct, 1)
            if which == 1:
                nc.vector.tensor_copy(lnc[:], ps_h[1][:, 0:32].rearrange("p (a e) -> p a e", a=2)).then_inc(s_cc, 1)
                dve.wait_ge(s_cc, 2)
            else:
                dve.sem_inc(s_cc, 1)
            dve.sem_inc(s_py, 2)

            def copy_xT(n, par):
                dve.wait_ge(s_tr, n + 1)
                e = None if which == 0 else expert(dve, n)
                for k in range(KD):
                    if which == 0:
                        ins = nc.vector.tensor_copy(xT[:, par, k, :], ps_x[:, k, 0:B])
                    else:
                        ins = nc.vector.tensor_scalar(xT[:, par, k, :], ps_x[:, k, 0:B], lnc[:, 0, bass.ds(e * KD + k, 1)], lnc[:, 1, bass.ds(e * KD + k, 1)], ALU.mult, ALU.add)
                    ins.then_inc(s_xT, 1)

            def results(n, i, par, last):
                if not last:
                    copy_xT(n + 1, 1 - par)
                e = expert(dve, n)
                dve.wait_ge(s_yst[par], 16 * i + 16)
                for s in range(S):
                    dve.wait_ge(s_y2, n * S + (s + 1 + 2 * S))
                    nc.vector.tensor_tensor(y[:, par, s, :], ps_y[s % 2][:, 0:D], b2b[:, bass.ds(e, 1), :].rearrange("p a d -> p (a d)"), ALU.add).then_inc(s_py, 1)

            copy_xT(0, 0)
            rounds(dve, results)


def combine_stage(nc, g, which):
    pre = f"cb{which}_"
    with ExitStack() as ctx:
        sb = lambda n, s, d=F32: ctx.enter_context(nc.sbuf_tensor(pre + n, s, d))
        bad = sb("bad", [P, NT, D], I32)
        low = sb("low", [P, 3, D])
        s_g = g.sem(pre + "gather"); s_dve = g.sem(pre + "dve"); s_out = g.sem(pre + "out"); s_x = g.sem(pre + "x")
        block = ctx.enter_context(nc.Block())
        rows = (g.Z, g.Y)
        filled = g.YB[0:NE * B0 if which == 0 else NB1 * B1, :]

        @block.gpsimd
        def _(pool):
            for k in range(which + 1):
                for t in range(NT):
                    pool.indirect_dma_start(rows[k][:, t, :], None, filled, bass.IndirectOffsetOnAxis(g.gslot[:, k, t:t + 1], axis=0)).then_inc(s_g, 16)

        @block.vector
        def _(dve):
            step = Steps(dve, s_dve)
            dve.wait_ge(s_g, 16 * NT * (which + 1))
            for k in range(which + 1):
                r = rows[k]
                step(dve.tensor_tensor(r[:], r[:], bcast(g.wgt[:, k, :], 2, D), ALU.mult))
                if which == 0:
                    for j, v in enumerate((0.0, 1.0e4, -1.0e4)):
                        step(dve.memset(low[:, j, :], v))
                    step(dve.tensor_tensor(bad[:], r[:], r[:], ALU.not_equal))
                    step(dve.copy_predicated(r[:], bad[:], bcast(low[:, 0, :], 1, NT)))
                    step(dve.tensor_scalar(bad[:], r[:], 3.4028234e38, None, ALU.is_gt))
                    step(dve.copy_predicated(r[:], bad[:], bcast(low[:, 1, :], 1, NT)))
                    step(dve.tensor_scalar(bad[:], r[:], -3.4028234e38, None, ALU.is_lt))
                    step(dve.copy_predicated(r[:], bad[:], bcast(low[:, 2, :], 1, NT)))
                step(dve.tensor_tensor(g.X[:], g.X[:], r[:], ALU.add))
            dve.sem_inc(s_x, 1)

        @block.sync
        def _(sp):
            if which == 1:
                sp.wait_ge(s_x, 1)
                sp.dma_start(g.out[0:(NT - 1) * P, :].rearrange("(t p) d -> p t d", p=P), g.X[:, 0:NT - 1, :]).then_inc(s_out, 16)
                sp.dma_start(g.out[(NT - 1) * P:N, :], g.X[0:LAST, NT - 1, :]).then_inc(s_out, 16)
                sp.wait_ge(s_out, 32)


def rgcn_table_stage(nc, g, layer):
    pre = f"rg{layer}_"
    W, bias = (g.rW0, g.rb0) if layer == 0 else (g.rW1, g.rb1)
    R2 = NREL // 2
    with ExitStack() as ctx:
        sb = lambda n, s, d=F32: ctx.enter_context(nc.sbuf_tensor(pre + n, s, d))
        w = sb("w", [P, KD, NREL, D]); b2 = sb("b2", [P, 2, D]); xs = sb("xs", [P, 2, KD, P])
        rows = sb("rows", [P, 2, R2, 2 * D])
        ps_t = [ctx.enter_context(nc.psum_tensor(f"{pre}t{k}", [P, 512], F32)) for k in range(2)]
        ps = [ctx.enter_context(nc.psum_tensor(f"{pre}p{k}", [P, 512], F32)) for k in range(4)]
        s_ld = g.sem(pre + "load"); s_dve = g.sem(pre + "dve"); s_var = g.sem(pre + "var"); s_sq = g.sem(pre + "sqrt")
        s_ln = g.sem(pre + "ln"); s_tr = g.sem(pre + "tr"); s_T = g.sem(pre + "T")
        s_xs = g.sem(pre + "xs"); s_mm = g.sem(pre + "mm"); s_add = g.sem(pre + "add"); s_relu = g.sem(pre + "relu")
        s_st = [g.sem(f"{pre}st{k}") for k in range(2)]
        block = ctx.enter_context(nc.Block())

        def rounds(eng, body):
            with eng.Fori(0, NT // 2) as i:
                body(i * 2, i, 0)
                body(i * 2 + 1, i, 1)
            body(NT - 1, NT // 2, 0)

        @block.gpsimd
        def _(pool):
            pool.wait_ge(s_T, NT if layer == 0 else 1)

            def stage(t, i, par):
                pool.wait_ge(s_mm, t * R2 + R2)
                pool.sem_inc(s_ln, 1)
                pool.tensor_copy(xs[:, par], g.ACC[:, :, bass.ds(t * P, P)]).then_inc(s_xs, 1)

            rounds(pool, stage)

        @block.tensor
        def _(pe):
            if layer == 0:
                pe.wait_ge(s_ln, 1)
                for t in range(NT):
                    if t >= 2:
                        pe.wait_ge(s_T, t - 1)
                    for k in range(KD):
                        ins = nc.tensor.transpose(ps_t[t % 2][:, k * P:(k + 1) * P], g.Y[:, t, k * P:(k + 1) * P], g.ident[:])
                    ins.then_inc(s_tr, 1)
            pe.sem_inc(s_mm, 2 * R2)
            pe.wait_ge(s_ld, 48)

            def products(t, i, par):
                pe.wait_ge(s_xs, t + 1)
                for r in range(R2):
                    pe.wait_ge(s_add, t * R2 + (r + 1))
                    for k in range(KD):
                        ins = nc.tensor.matmul(ps[r][:], xs[:, par, k, :], w[:, k, 2 * r:2 * r + 2, :].rearrange("p r d -> p (r d)"), start=(k == 0), stop=(k == KD - 1))
                    ins.then_inc(s_mm, 1)

            rounds(pe, products)

        @block.vector
        def _(dve):
            step = Steps(dve, s_dve)
            if layer == 0:
                layernorm(nc, g, dve, step, s_var, s_sq, 1, g.X, g.Y)
                dve.sem_inc(s_ln, 1)
            dve.sem_inc(s_add, R2)
            dve.wait_ge(s_ld, 48)

            def add(t, i, par):
                dve.wait_ge(s_st[par], 16 * i + 16)
                for r in range(R2):
                    dve.wait_ge(s_mm, t * R2 + (r + 1 + 2 * R2))
                    nc.vector.tensor_tensor(rows[:, par, r, :], ps[r][:], b2[:].rearrange("p r d -> p (r d)"), ALU.add).then_inc(s_add, 1)

            rounds(dve, add)

        @block.scalar
        def _(act):
            if layer == 0:
                act.wait_ge(s_var, 1)
                nc.scalar.activation(g.ln_s[:], g.ln_var[:], ACT.Sqrt).then_inc(s_sq, 1)
                for t in range(NT):
                    act.wait_ge(s_tr, t + 1)
                    nc.scalar.activation(g.ACC[:, :, t * P:(t + 1) * P], ps_t[t % 2][:, 0:D].rearrange("p (k n) -> p k n", k=KD), ACT.Copy).then_inc(s_T, 1)
            else:
                act.sem_inc(s_T, 1)

            def relu(t, i, par):
                for r in range(R2):
                    act.wait_ge(s_add, t * R2 + (r + 1 + R2))
                    nc.scalar.activation(rows[:, par, r, :], rows[:, par, r, :], ACT.Relu).then_inc(s_relu, 1)

            rounds(act, relu)

        @block.sync
        def _(sp):
            sp.dma_start(w[:, 0], W[:, 0:P, :].rearrange("r p o -> p r o")).then_inc(s_ld, 16)
            sp.dma_start(w[:, 1], W[:, P:2 * P, :].rearrange("r p o -> p r o")).then_inc(s_ld, 16)
            sp.dma_start(b2[:], bcast(bias, 0, 2).partition_broadcast(P)).then_inc(s_ld, 16)
            table = g.Gtab[0:ZERO_ROW, :].rearrange("(r n) d -> n r d", n=NP)

            def store(t, i, par):
                sp.wait_ge(s_relu, t * R2 + R2)
                sp.dma_start(table[bass.ds(t * P, P), :, :], rows[:, par].rearrange("p a (b d) -> p (a b) d", b=2)).then_inc(s_st[par], 16)

            for par in range(2):
                sp.dma_start(g.scrap[par:par + 1, :], g.zrow[0:1, :]).then_inc(s_st[par], 16)
            rounds(sp, store)
            sp.wait_ge(s_st[0], 16 * (NT // 2 + 1) + 16)
            sp.wait_ge(s_st[1], 16 * (NT // 2) + 16)


def add_sums_stage(nc, g):
    with ExitStack() as ctx:
        ps = [ctx.enter_context(nc.psum_tensor(f"as_ps{k}", [P, 512], F32)) for k in range(4)]
        s_tr = g.sem("as_tr"); s_add = g.sem("as_add")
        block = ctx.enter_context(nc.Block())

        @block.tensor
        def _(pe):
            for t in range(NT):
                if t >= 4:
                    pe.wait_ge(s_add, t - 3)
                for j in range(KD):
                    ins = nc.tensor.transpose(ps[t % 4][:, j * P:(j + 1) * P], g.ACC[:, j, t * P:(t + 1) * P], g.ident[:])
                ins.then_inc(s_tr, 1)

        @block.vector
        def _(dve):
            for t in range(NT):
                dve.wait_ge(s_tr, t + 1)
                nc.vector.tensor_tensor(g.X[:, t, :], g.X[:, t, :], ps[t % 4][:, 0:D], ALU.add).then_inc(s_add, 1)


def build(nc, ins, out):
    with ExitStack() as top:
        g = Places()
        g.x, g.src, g.dst, g.typ, g.gat_w, g.att_src = (ins["x"], ins["src"], ins["dst"], ins["typ"], ins["gat_w"], ins["att_src"])
        g.att_dst, g.gat_bias, g.gate_w, g.gate_b, g.f0_w1, g.f0_b1 = (ins["att_dst"], ins["gat_bias"], ins["gate_w"], ins["gate_b"], ins["f0_w1"], ins["f0_b1"])
        g.f0_w2, g.f0_b2, g.rW0, g.rb0, g.rW1, g.rb1 = (ins["f0_w2"], ins["f0_b2"], ins["rW0"], ins["rb0"], ins["rW1"], ins["rb1"])
        g.Wr, g.br, g.ln_g, g.ln_b, g.f1_w1, g.f1_b1 = (ins["Wr"], ins["br"], ins["ln_g"], ins["ln_b"], ins["f1_w1"], ins["f1_b1"])
        g.f1_w2, g.f1_b2 = (ins["f1_w2"], ins["f1_b2"])
        g.out = out
        g.stages = 0
        dram = lambda name, shape, dt=F32: nc.dram_tensor(name, shape, dt, kind="Internal").ap()
        sb = lambda name, shape, dt=F32: top.enter_context(nc.sbuf_tensor(name, shape, dt))
        g.S_src, g.S_dst, g.S_typ = (dram(n, (E + 2 * EPAD,), I32) for n in ("s_src_d", "s_dst_d", "s_typ_d"))
        g.S_rec = dram("s_rec_d", (E, 4), I32)
        g.Htab = dram("h_table", (NP, D))
        g.Atab = dram("a_table", (NP, 8))
        g.Gtab = dram("rel_table", (ZERO_ROW + 1, D))
        g.XB = dram("slots_in", (NB1 * B1 + 2 * NP, D))
        g.YB = dram("slots_out", (NB1 * B1, D))
        g.scrap = dram("scrap", (2, D))
        g.iota_i = sb("iota_i", [P, P], I32); g.iotap_i = sb("iotap_i", [P, P], I32)
        g.iota = sb("iota", [P, P]); g.iotap = sb("iotap", [P, P]); g.ident = sb("ident", [P, P])
        g.upper = sb("upper", [P, P]); g.ones = sb("ones", [P, P]); g.zrow = sb("zrow", [P, D]); g.valid = sb("valid", [P, 1])
        g.unsorted = sb("unsorted", [1, 1], I32)
        g.ln_st = sb("ln_st", [P, NT, 6])
        g.ln_mean, g.ln_var, g.ln_r, g.ln_t1, g.ln_t2, g.ln_s = (sb(f"ln_{n}", [P, NT]) for n in ("mean", "var", "r", "t1", "t2", "s"))
        g.wgt = sb("wgt", [P, 2, NT]); g.gslot = sb("gslot", [P, 2, NT], I32); g.blk_expert = sb("blk_expert", [1, NB1], I32)

        stage(nc, g, edges_stage)
        stage(nc, g, sort_stage)
        TP = T + HALF
        g.relI = sb("relI", [P, TP], I32); g.dstrel = sb("dstrel", [P, TP]); g.base = sb("base", [1, T], I32)
        g.X = sb("X", [P, NT, D]); g.Y = sb("Y", [P, NT, D])
        with ExitStack() as gat:
            gsb = lambda name, shape, dt=F32: gat.enter_context(nc.sbuf_tensor(name, shape, dt))
            g.srcI = gsb("srcI", [P, TP], I32); g.dstI = gsb("dstI", [P, TP], I32)
            g.PT = gsb("PT", [P, TP, 8])
            with ExitStack() as lanes:
                lsb = lambda name, shape, dt=F32: lanes.enter_context(nc.sbuf_tensor(name, shape, dt))
                g.first = lsb("first", [LANES, LC, P]); g.firstneg = lsb("firstneg", [LANES, LC, P]); g.endneg = lsb("endneg", [LANES, LC, P])
                stage(nc, g, tables_stage)
                stage(nc, g, gat_table_stage)
                g.AS = lsb("AS", [P, T, 12]); g.baseq = lsb("baseq", [1, T], I32)
                g.AS4 = g.AS[:].rearrange("p (c q) a -> p c q a", c=LC)
                stage(nc, g, scores_stage)
                stage(nc, g, softmax_stage)
            g.ACC = gsb("ACC", [P, KD, AW]); g.DEN = gsb("DEN", [8, AW])
            stage(nc, g, edge_pass, "gat", g.Htab, g.srcI, 0)
            g.Z = gsb("Z", [P, NT, D])
            stage(nc, g, gat_finish_stage)
        g.Z = sb("Z1", [P, NT, D])
        stage(nc, g, router_stage, 0)
        stage(nc, g, experts_stage, 0)
        stage(nc, g, combine_stage, 0)
        with ExitStack() as rg:
            g.ACC = rg.enter_context(nc.sbuf_tensor("ACC1", [P, KD, AW], F32))
            for layer in range(2):
                stage(nc, g, rgcn_table_stage, layer)
                stage(nc, g, edge_pass, "rgcn", g.Gtab, g.relI, 1 + layer)
            stage(nc, g, add_sums_stage)
        stage(nc, g, router_stage, 1)
        stage(nc, g, experts_stage, 1)
        stage(nc, g, combine_stage, 1)


NAMES = {
    "x": "x", "src": "src", "dst": "dst", "edge_type_8": "typ",
    "L0_gnn_W": "gat_w", "L0_gnn_att_src": "att_src", "L0_gnn_att_dst": "att_dst", "L0_gnn_bias": "gat_bias",
    "L0_ffn_gate_w": "gate_w", "L0_ffn_gate_b": "gate_b",
    "L0_ffn_w1": "f0_w1", "L0_ffn_b1": "f0_b1", "L0_ffn_w2": "f0_w2", "L0_ffn_b2": "f0_b2",
    "L1_gnn_W0": "rW0", "L1_gnn_b0": "rb0", "L1_gnn_W1": "rW1", "L1_gnn_b1": "rb1",
    "L1_ffn_Wr": "Wr", "L1_ffn_br": "br", "L1_ffn_ln_g": "ln_g", "L1_ffn_ln_b": "ln_b",
    "L1_ffn_W1": "f1_w1", "L1_ffn_b1": "f1_b1", "L1_ffn_W2": "f1_w2", "L1_ffn_b2": "f1_b2",
}


def kernel(**inputs):
    import concourse.bacc as bacc
    from concourse.bass_utils import run_bass_kernel_spmd

    nc = bacc.Bacc("TRN2", target_bir_lowering=False, num_devices=1)
    arrays, ins = {}, {}
    for name, short in NAMES.items():
        a = np.ascontiguousarray(inputs[name])
        arrays["in_" + name] = a
        ins[short] = nc.dram_tensor("in_" + name, a.shape, mybir.dt.from_np(a.dtype), kind="ExternalInput").ap()
    out = nc.dram_tensor("out_0", (N, D), F32, kind="ExternalOutput").ap()
    build(nc, ins, out)
    r = run_bass_kernel_spmd(nc, [arrays], core_ids=[0])
    return r.results[0]["out_0"]
```

```python
import numpy as np
import concourse.bass as bass
from concourse import mybir
from contextlib import ExitStack

F32 = mybir.dt.float32
I32 = mybir.dt.int32
BF16 = mybir.dt.bfloat16
F32R = mybir.dt.float32r
ALU = mybir.AluOpType
ACT = mybir.ActivationFunctionType
AX = mybir.AxisListType

P = 128
N = 3125
D = 256
KD = D // P
NT = -(-N // P)
NP = NT * P
LAST = N - (NT - 1) * P
HEADS, CH = 4, 64
E0 = 53125
T = 440
E = T * P
HALF = 10
RING = 2 * HALF
LANES, LC = 110, 4
EPAD = 128
WIN = P
AW = NP + WIN
HROW = D + 2 * HEADS
FILL_SRC = NP - 1
NREL = 8
FILL_TYPE = NREL
ZERO_ROW = NREL * NP
BIG = 1.0e30
NEG_SLOPE = 0.2
EPS = 1e-5
NE = 8
F = 1024
FC = F // P
CAP = -(-5 * N // (4 * NE))
B0 = 512
B1 = 256
NB1 = (2 * N + NE * (B1 - 1)) // B1
NB1_MIN = -(-2 * N // B1)
assert (T * P >= E0 + N) and CAP <= B0


class Places:
    pass


class Steps:

    def __init__(self, eng, sem):
        self.eng, self.sem, self.n = eng, sem, 0

    def __call__(self, ins):
        ins.then_inc(self.sem, 1)
        self.n = self.n + 1
        self.eng.wait_ge(self.sem, self.n)


def stage(nc, g, program, *args):
    taken = []
    g.stages += 1

    def sem(name):
        taken.append(nc.alloc_semaphore(name=f"{name}_s{g.stages}"))
        return taken[-1]

    g.sem = sem
    program(nc, g, *args)
    nc.clear_and_free_semaphores(taken)
    nc.all_engine_barrier()


def load_values(nc, engine, ap, most):
    return nc.values_load_multi_w_load_instructions(ap, engines=(engine,), min_val=0, max_val=most)[1]


def bcast(ap, axis, n):
    a = ap.unsqueeze(axis)
    shape = list(a.shape)
    shape[axis] = n
    return a.to_broadcast(shape)


def edges_stage(nc, g):
    with ExitStack() as ctx:
        fill = ctx.enter_context(nc.sbuf_tensor("fill", [1, 3, E - E0], I32))
        edge = ctx.enter_context(nc.sbuf_tensor("edge", [1, 2], I32))
        di = ctx.enter_context(nc.sbuf_tensor("di", [P, T], I32))
        dp = ctx.enter_context(nc.sbuf_tensor("dp", [P, T], I32))
        diff = ctx.enter_context(nc.sbuf_tensor("diff", [P, T], F32))
        b1 = ctx.enter_context(nc.sbuf_tensor("brk1", [P, T], F32))
        b2 = ctx.enter_context(nc.sbuf_tensor("brk2", [P, T], F32))
        bs = ctx.enter_context(nc.sbuf_tensor("brks", [P, 1], F32))
        tot = ctx.enter_context(nc.psum_tensor("brk_tot", [1, 1], F32))
        s_fill = g.sem("fill"); s_copy = g.sem("edge_copy"); s_load = g.sem("edge_load")
        s_chain = g.sem("edge_dve"); s_tot = g.sem("edge_tot"); s_sum = g.sem("edge_sum")
        block = ctx.enter_context(nc.Block())

        @block.gpsimd
        def _(pool):
            pool.memset(fill[:, 0, :], FILL_SRC).then_inc(s_fill, 1)
            pool.memset(fill[:, 1, :], N - 1).then_inc(s_fill, 1)
            pool.memset(fill[:, 2, :], FILL_TYPE).then_inc(s_fill, 1)
            pool.memset(edge[:, 0:1], -1).then_inc(s_fill, 1)
            pool.memset(edge[:, 1:2], N).then_inc(s_fill, 1)
            pool.iota(g.iota_i[:], [[1, P]], base=0, channel_multiplier=0).then_inc(s_fill, 1)
            pool.iota(g.iotap_i[:], [[0, P]], base=0, channel_multiplier=1).then_inc(s_fill, 1)
            pool.memset(g.ones[:], 1.0).then_inc(s_fill, 1)
            pool.memset(g.zrow[:], 0.0).then_inc(s_fill, 1)

        @block.sync
        def _(sp):
            for dram, a in ((g.S_src, g.src), (g.S_dst, g.dst), (g.S_typ, g.typ)):
                sp.dma_start(dram[EPAD:EPAD + E0].rearrange("(a b) -> a b", b=425),
                             a.rearrange("(a b) -> a b", b=425)).then_inc(s_copy, 16)
            sp.wait_ge(s_fill, 5)
            for k, dram in enumerate((g.S_src, g.S_dst, g.S_typ)):
                sp.dma_start(dram[EPAD + E0:EPAD + E].unsqueeze(0), fill[:, k, :]).then_inc(s_copy, 16)
            sp.dma_start(g.S_dst[EPAD - 1:EPAD].unsqueeze(0), edge[:, 0:1]).then_inc(s_copy, 16)
            sp.dma_start(g.S_dst[EPAD + E:EPAD + E + 1].unsqueeze(0), edge[:, 1:2]).then_inc(s_copy, 16)
            sp.wait_ge(s_copy, 8 * 16)
            sp.dma_start(di[:], g.S_dst[EPAD:EPAD + E].rearrange("(p j) -> p j", p=P)).then_inc(s_load, 16)
            sp.dma_start(dp[:], g.S_dst[EPAD - 1:EPAD - 1 + E].rearrange("(p j) -> p j", p=P)).then_inc(s_load, 16)

        @block.vector
        def _(dve):
            step = Steps(dve, s_chain)
            dve.wait_ge(s_fill, 9)
            dve.tensor_copy(g.iota[:], g.iota_i[:]).then_inc(s_fill, 1)
            step(dve.tensor_copy(g.iotap[:], g.iotap_i[:]))
            dve.wait_ge(s_fill, 10)
            step(dve.tensor_tensor(g.ident[:], g.iota[:], g.iotap[:], ALU.is_equal))
            step(dve.tensor_tensor(g.upper[:], g.iota[:], g.iotap[:], ALU.is_ge))
            step(dve.tensor_scalar(g.valid[:], g.iotap[:, 0:1], float(LAST), None, ALU.is_lt))
            dve.wait_ge(s_load, 32)
            step(dve.tensor_tensor(diff[:], di[:], dp[:], ALU.subtract))
            step(dve.tensor_scalar(b1[:], diff[:], 0.0, None, ALU.is_lt))
            step(dve.tensor_scalar(b2[:], diff[:], 1.0, None, ALU.is_gt))
            step(dve.tensor_tensor(b1[:], b1[:], b2[:], ALU.add))
            dve.tensor_reduce(bs[:], b1[:], AX.X, ALU.add).then_inc(s_sum, 1)
            dve.wait_ge(s_tot, 1)
            step(dve.tensor_copy(g.unsorted[:], tot[:]))

        @block.tensor
        def _(pe):
            pe.wait_ge(s_sum, 1)
            nc.tensor.matmul(tot[:], g.ones[:, 0:1], bs[:], start=True, stop=True).then_inc(s_tot, 1)


def sort_stage(nc, g):
    CH_E = 3520
    with ExitStack() as ctx:
        sb = lambda n, s, d: ctx.enter_context(nc.sbuf_tensor(n, s, d))
        node = sb("srt_node", [1, N], I32)
        rec = sb("srt_rec", [P, T, 4], I32)
        cols = sb("srt_cols", [P, 3, T], I32)
        dcol = sb("srt_dcol", [P, T], F32)
        ecol_i = sb("srt_ecol_i", [P, T], I32)
        ecol = sb("srt_ecol", [P, T], F32)
        rank = sb("srt_rank", [P, T], F32)
        rank_i = sb("srt_rank_i", [P, T], I32)
        row_i = sb("srt_row_i", [P, CH_E], I32)
        row = sb("srt_row", [P, CH_E], F32)
        place_i = sb("srt_place_i", [P, CH_E], I32)
        place = sb("srt_place", [P, CH_E], F32)
        before = sb("srt_before", [P, CH_E], F32)
        junk = sb("srt_junk", [P, CH_E], F32)
        lt = sb("srt_lt", [P, 1], F32)
        eq = sb("srt_eq", [P, 1], F32)
        idx1 = sb("srt_idx1", [P, 1], I32)
        rec1 = sb("srt_rec1", [P, 4], I32)
        s_io = g.sem("srt_iota"); s_dma = g.sem("srt_dma"); s_row = g.sem("srt_row")
        s_used = g.sem("srt_row_used"); s_rank = g.sem("srt_ranked"); s_st = g.sem("srt_staged")
        s_sc = g.sem("srt_scattered"); s_dve = g.sem("srt_dve"); s_out = g.sem("srt_out")
        s_sep = g.sem("srt_separate"); s_turn = g.sem("srt_turn")
        block = ctx.enter_context(nc.Block())
        arrays = (g.S_dst, g.S_src, g.S_typ)

        def flat(a):
            return a[EPAD:EPAD + E].rearrange("(p j) -> p j", p=P)

        @block.sync
        def _(sp):
            unsorted = sp.value_load(g.unsorted[0:1, 0:1], min_val=0, max_val=E)
            with sp.If(unsorted > 0):
                sp.wait_ge(s_io, 3)
                sp.dma_start(g.S_dst[EPAD + E0:EPAD + E0 + N].unsqueeze(0), node[:]).then_inc(s_dma, 16)
                sp.wait_ge(s_dma, 16)
                for k, a in enumerate(arrays):
                    sp.dma_start(cols[:, k, :], flat(a)).then_inc(s_dma, 16)
                with sp.Fori(0, E // CH_E) as c:
                    sp.wait_ge(s_used, c + 1)
                    sp.dma_start(row_i[:], g.S_dst[bass.ds(c * CH_E + EPAD, CH_E)].partition_broadcast(P)).then_inc(s_row, 16)
                sp.wait_ge(s_sc, 16 * T)
                sp.dma_start(rec[:], g.S_rec.rearrange("(p j) w -> p j w", p=P)).then_inc(s_out, 16)
                sp.wait_ge(s_sep, 1)
                for k, a in enumerate(arrays):
                    sp.dma_start(flat(a), cols[:, k, :]).then_inc(s_out, 16)
                sp.wait_ge(s_out, 64)

        @block.gpsimd
        def _(pool):
            unsorted = pool.value_load(g.unsorted[0:1, 0:1], min_val=0, max_val=E)
            with pool.If(unsorted > 0):
                pool.iota(node[:], [[1, N]], base=0, channel_multiplier=0).then_inc(s_io, 1)
                pool.iota(ecol_i[:], [[1, T]], base=0, channel_multiplier=T).then_inc(s_io, 1)
                pool.iota(place_i[:], [[1, CH_E]], base=0, channel_multiplier=0).then_inc(s_io, 1)
                pool.wait_ge(s_rank, 1)
                with pool.Fori(0, T) as j:
                    pool.tensor_copy(idx1[:], rank_i[:, bass.ds(j, 1)]).then_inc(s_st, 1)
                    pool.tensor_copy(rec1[:], rec[:, bass.ds(j, 1), :].rearrange("p a w -> p (a w)")).then_inc(s_st, 1)
                    pool.wait_ge(s_st, 2 * j + 2)
                    pool.sem_inc(s_turn, 1)
                    pool.indirect_dma_start(g.S_rec, bass.IndirectOffsetOnAxis(idx1[:], axis=0), rec1[:], None).then_inc(s_sc, 16)
                    pool.wait_ge(s_sc, 16 * j + 16)

        @block.vector
        def _(dve):
            unsorted = dve.value_load(g.unsorted[0:1, 0:1], min_val=0, max_val=E)
            with dve.If(unsorted > 0):
                step = Steps(dve, s_dve)
                dve.wait_ge(s_io, 3)
                dve.wait_ge(s_dma, 64)
                step(dve.memset(rec[:], 0))
                for k in range(3):
                    step(dve.tensor_copy(rec[:, :, k], cols[:, k, :]))
                step(dve.tensor_copy(dcol[:], cols[:, 0, :]))
                step(dve.tensor_copy(ecol[:], ecol_i[:]))
                step(dve.tensor_copy(place[:], place_i[:]))
                step(dve.memset(rank[:], 0.0))
                dve.sem_inc(s_used, 1)
                n0 = step.n
                per = 2 + 5 * T
                with dve.Fori(0, E // CH_E) as c:
                    step.n = n0 + c * per
                    dve.wait_ge(s_row, 16 * c + 16)
                    step(dve.tensor_copy(row[:], row_i[:]))
                    dve.sem_inc(s_used, 1)
                    n1 = step.n
                    with dve.Fori(0, T) as j:
                        step.n = n1 + j * 5
                        d1, e1, r1 = (x[:, bass.ds(j, 1)] for x in (dcol, ecol, rank))
                        step(dve.tensor_scalar(before[:], place[:], e1, None, ALU.is_lt))
                        dve.scalar_tensor_tensor(junk[:], row[:], d1, before[:], ALU.is_equal, ALU.mult, accum_out=eq[:]).then_inc(s_dve, 1)
                        dve.wait_ge(s_dve, step.n + 1)
                        dve.tensor_scalar(junk[:], row[:], d1, 0.0, ALU.is_lt, ALU.add, accum_out=lt[:]).then_inc(s_dve, 1)
                        step.n = step.n + 2
                        dve.wait_ge(s_dve, step.n)
                        step(dve.tensor_tensor(r1, r1, lt[:], ALU.add))
                        step(dve.tensor_tensor(r1, r1, eq[:], ALU.add))
                    step.n = n1 + 5 * T
                    step(dve.tensor_scalar(ecol[:], ecol[:], float(CH_E), None, ALU.subtract))
                dve.tensor_copy(rank_i[:], rank[:]).then_inc(s_rank, 1)
                dve.wait_ge(s_out, 16)
                for k in range(3):
                    ins = dve.tensor_copy(cols[:, k, :], rec[:, :, k])
                ins.then_inc(s_sep, 1)


def tables_stage(nc, g):
    with ExitStack() as ctx:
        sb = lambda n, s, d: ctx.enter_context(nc.sbuf_tensor(n, s, d))
        lane_i = sb("lane_i", [LANES, 3, LC, P], I32)
        prev_i = sb("prev_i", [LANES, 2, LC, P], I32)
        lane = sb("lane", [LANES, 3, LC, P], F32)
        dstT = sb("dstT", [P, T], F32)
        ps = [ctx.enter_context(nc.psum_tensor(f"tab_ps{k}", [P, 512], F32)) for k in range(4)]
        s_ld = g.sem("tab_load"); s_dve = g.sem("tab_dve"); s_lane = g.sem("tab_lane")
        s_z = g.sem("tab_zero"); s_x = g.sem("tab_x")
        s_tr = g.sem("tab_tr"); s_dT = g.sem("tab_dT"); s_base = g.sem("tab_base")
        block = ctx.enter_context(nc.Block())

        def lanes(a, shift=0):
            return a[EPAD + shift:EPAD + shift + E].rearrange("(c q f) -> q c f", c=LC, f=P)

        @block.sync
        def _(sp):
            for k, a in enumerate((g.S_dst, g.S_src, g.S_typ)):
                sp.dma_start(lane_i[:, k], lanes(a)).then_inc(s_ld, 16)
            sp.dma_start(prev_i[:, 0], lanes(g.S_dst, -1)).then_inc(s_ld, 16)
            sp.dma_start(prev_i[:, 1], lanes(g.S_dst, 1)).then_inc(s_ld, 16)
            sp.dma_start(g.X[:, 0:NT - 1, :], g.x[0:(NT - 1) * P, :].rearrange("(t p) d -> p t d", p=P)).then_inc(s_x, 16)
            sp.wait_ge(s_z, 1)
            sp.dma_start(g.X[0:LAST, NT - 1, :], g.x[(NT - 1) * P:N, :]).then_inc(s_x, 16)
            sp.wait_ge(s_x, 32)

        @block.vector
        def _(dve):
            step = Steps(dve, s_dve)
            dve.memset(g.X[:, NT - 1, :], 0.0).then_inc(s_z, 1)
            dve.wait_ge(s_ld, 80)
            step(dve.tensor_copy(lane[:], lane_i[:]))
            step(dve.scalar_tensor_tensor(lane[:, 2], lane[:, 2], float(NP), lane[:, 1], ALU.mult, ALU.add))
            step(dve.tensor_scalar(lane[:, 2], lane[:, 2], float(ZERO_ROW), None, ALU.min))
            step(dve.tensor_tensor(g.first[:], lane[:, 0], prev_i[:, 0], ALU.not_equal))
            dve.tensor_tensor(g.endneg[:], lane[:, 0], prev_i[:, 1], ALU.not_equal).then_inc(s_lane, 1)
            step(dve.tensor_scalar(g.firstneg[:], g.first[:], -BIG, None, ALU.mult))
            dve.wait_ge(s_lane, 1)
            step(dve.tensor_scalar(g.endneg[:], g.endneg[:], -BIG, None, ALU.mult))
            dve.memset(g.srcI[:, T:], 0).then_inc(s_dve, 1)
            dve.memset(g.relI[:, T:], 0).then_inc(s_dve, 1)
            dve.memset(g.dstI[:, T:], 0).then_inc(s_dve, 1)
            step.n += 3
            step(dve.memset(g.dstrel[:, T:], 0.0))
            dve.wait_ge(s_tr, 1)
            dve.tensor_copy(dstT[:], ps[0][:, 0:T]).then_inc(s_dT, 1)
            step(dve.tensor_copy(g.dstI[:, 0:T], ps[0][:, 0:T]))
            dve.wait_ge(s_tr, 2)
            step(dve.tensor_copy(g.srcI[:, 0:T], ps[1][:, 0:T]))
            dve.wait_ge(s_tr, 3)
            step(dve.tensor_copy(g.relI[:, 0:T], ps[2][:, 0:T]))
            dve.wait_ge(s_base, 1)
            step(dve.tensor_tensor(g.dstrel[:, 0:T], dstT[:], ps[3][:, 0:T], ALU.subtract))
            step(dve.tensor_copy(g.base[:], ps[3][0:1, 0:T]))

        @block.tensor
        def _(pe):
            pe.wait_ge(s_lane, 1)
            for k in range(3):
                for c in range(LC):
                    ins = nc.tensor.transpose(ps[k][:, c * LANES:(c + 1) * LANES], lane[:, k, c, :], g.ident[0:LANES, 0:LANES])
                ins.then_inc(s_tr, 1)
            pe.wait_ge(s_dT, 1)
            nc.tensor.matmul(ps[3][:, 0:T], g.ones[0:1, :], dstT[0:1, :], start=True, stop=True).then_inc(s_base, 1)


def layernorm(nc, g, dve, step, s_var, s_sqrt, k, src, dst, s_done):
    TURN = 5
    assert NT % TURN == 0
    tile = lambda a, t: a[:, bass.ds(t, 1), :].rearrange("p a w -> p (a w)")
    st, mean, var, r, t1, t2 = g.ln_st, g.ln_mean, g.ln_var, g.ln_r, g.ln_t1, g.ln_t2
    n0 = step.n
    with dve.Fori(0, NT // TURN) as i:
        for j in range(TURN):
            t = i * TURN + j
            nc.vector.bn_stats(tile(st, t), tile(src, t)).then_inc(step.sem, 1)
    step.n = n0 + NT
    dve.wait_ge(step.sem, step.n)
    step(dve.tensor_tensor(mean[:], st[:, :, 1], st[:, :, 4], ALU.add))
    step(dve.tensor_scalar(mean[:], mean[:], 0.5, None, ALU.mult))
    step(dve.tensor_tensor(t1[:], st[:, :, 1], st[:, :, 4], ALU.subtract))
    step(dve.tensor_tensor(t1[:], t1[:], t1[:], ALU.mult))
    step(dve.tensor_tensor(t2[:], st[:, :, 2], st[:, :, 5], ALU.add))
    step(dve.scalar_tensor_tensor(t1[:], t1[:], float(D) / 4, t2[:], ALU.mult, ALU.add))
    step(dve.tensor_scalar(var[:], t1[:], 1.0 / D, EPS, ALU.mult, ALU.add))
    dve.sem_inc(s_var, 1)
    dve.wait_ge(s_sqrt, k)
    step(dve.reciprocal(r[:], g.ln_s[:]))
    step(dve.tensor_tensor(t1[:], r[:], r[:], ALU.mult))
    step(dve.tensor_tensor(t1[:], t1[:], var[:], ALU.mult))
    step(dve.tensor_scalar(t1[:], t1[:], -0.5, 1.5, ALU.mult, ALU.add))
    step(dve.tensor_tensor(r[:], r[:], t1[:], ALU.mult))
    with dve.Fori(0, NT // TURN) as i:
        for j in range(TURN):
            t = i * TURN + j
            nc.vector.tensor_scalar(tile(dst, t), tile(src, t), mean[:, bass.ds(t, 1)], r[:, bass.ds(t, 1)],
                                    ALU.subtract, ALU.mult).then_inc(s_done, 1)
    dve.wait_ge(s_done, NT)


def gat_table_stage(nc, g):
    with ExitStack() as ctx:
        sb = lambda n, s, d: ctx.enter_context(nc.sbuf_tensor(n, s, d))
        w = sb("gat_w", [P, KD, D], F32)
        attT = sb("gat_attT", [8, P], F32)
        att = sb("gat_att", [P, KD, 8], F32)
        wt = sb("gat_wt", [P, KD, HROW], F32)
        xT = sb("gat_xT", [P, 4, KD, P], F32)
        hst = sb("gat_hst", [P, 2, HROW], F32)
        pads = sb("gat_pads", [P, 1], F32)
        ps_t = [ctx.enter_context(nc.psum_tensor(f"gt_t{k}", [P, 512], F32)) for k in range(4)]
        ps_h = [ctx.enter_context(nc.psum_tensor(f"gt_h{k}", [P, 512], F32)) for k in range(2)]
        ps_w = ctx.enter_context(nc.psum_tensor("gt_w", [P, 512], F32))
        s_ld = g.sem("gt_load"); s_dve = g.sem("gt_dve"); s_act = g.sem("gt_act"); s_var = g.sem("gt_var")
        s_ln = g.sem("gt_ln"); s_tr = g.sem("gt_tr"); s_xT = g.sem("gt_xT")
        s_h = g.sem("gt_h"); s_hst = g.sem("gt_hst"); s_w = g.sem("gt_wtr"); s_wt = g.sem("gt_wt"); s_att = g.sem("gt_att")
        s_st = [g.sem("gt_store0"), g.sem("gt_store1")]
        s_a = g.sem("gt_attT"); s_wa = g.sem("gt_wa"); s_zr = g.sem("gt_zr")
        block = ctx.enter_context(nc.Block())

        @block.sync
        def _(sp):
            sp.dma_start(w[:], g.gat_w.rearrange("(k p) i -> p k i", p=P)).then_inc(s_ld, 16)
            sp.dma_start(attT[0:2, :], g.att_src.rearrange("(k h) c -> k (h c)", k=KD)).then_inc(s_ld, 16)
            sp.dma_start(attT[2:4, :], g.att_dst.rearrange("(k h) c -> k (h c)", k=KD)).then_inc(s_ld, 16)
            sp.dma_start(g.Gtab[ZERO_ROW:ZERO_ROW + 1, :], g.zrow[0:1, 0:D]).then_inc(s_zr, 16)
            for t in range(NT):
                sp.wait_ge(s_hst, t + 1)
                sp.dma_start(g.Htab[t * P:(t + 1) * P, :], hst[:, t % 2, 0:D]).then_inc(s_st[t % 2], 16)
                sp.dma_start(g.Atab[t * P:(t + 1) * P, :], hst[:, t % 2, D:HROW]).then_inc(s_st[t % 2], 16)
            sp.wait_ge(s_st[0], 32 * ((NT + 1) // 2))
            sp.wait_ge(s_st[1], 32 * (NT // 2))
            sp.wait_ge(s_zr, 16)

        @block.vector
        def _(dve):
            step = Steps(dve, s_dve)
            step(dve.memset(att[:], 0.0))
            dve.wait_ge(s_a, 1)
            for k in range(KD):
                for h in range(2):
                    sl = slice(h * CH, (h + 1) * CH)
                    dve.tensor_copy(att[sl, k, 2 * k + h:2 * k + h + 1], ps_w[sl, k:k + 1])
                    ins = dve.tensor_copy(att[sl, k, 4 + 2 * k + h:5 + 2 * k + h], ps_w[sl, 2 + k:3 + k])
            ins.then_inc(s_att, 1)
            layernorm(nc, g, dve, step, s_var, s_act, 1, g.X, g.Y, s_ln)
            step(dve.tensor_scalar(pads[:], g.valid[:], 1.0, BIG, ALU.subtract, ALU.mult))
            for t in range(NT):
                dve.wait_ge(s_h, t + 1)
                if t >= 2:
                    dve.wait_ge(s_st[t % 2], 32 * (t // 2))
                if t < NT - 1:
                    dve.tensor_copy(hst[:, t % 2, :], ps_h[t % 2][:, 0:HROW]).then_inc(s_hst, 1)
                else:
                    step(dve.tensor_copy(hst[:, t % 2, :], ps_h[t % 2][:, 0:HROW]))
                    dve.tensor_scalar(hst[:, t % 2, D:D + HEADS], ps_h[t % 2][:, D:D + HEADS], pads[:], None, ALU.add).then_inc(s_hst, 1)

        @block.scalar
        def _(act):
            act.wait_ge(s_w, 1)
            for j in range(KD):
                ins = nc.scalar.activation(wt[:, j, 0:D], ps_t[j][:, 0:D], ACT.Copy)
            ins.then_inc(s_wt, 1)
            act.wait_ge(s_wa, 1)
            nc.scalar.activation(wt[:, :, D:HROW], ps_w[:, 16:16 + KD * 8].rearrange("p (k a) -> p k a", k=KD), ACT.Copy).then_inc(s_wt, 1)
            act.wait_ge(s_var, 1)
            nc.scalar.activation(g.ln_s[:], g.ln_var[:], ACT.Sqrt).then_inc(s_act, 1)
            for t in range(NT):
                act.wait_ge(s_tr, t + 1)
                if t >= 4:
                    act.wait_ge(s_h, t - 3)
                nc.scalar.activation(xT[:, t % 4], ps_t[t % 4][:, 0:D].rearrange("p (k n) -> p k n", k=KD), ACT.Copy).then_inc(s_xT, 1)

        @block.tensor
        def _(pe):
            pe.wait_ge(s_ld, 48)
            nc.tensor.transpose(ps_w[:, 0:4], attT[0:4, :], g.ident[0:4, 0:4]).then_inc(s_a, 1)
            for j in range(KD):
                for k in range(KD):
                    ins = nc.tensor.transpose(ps_t[j][:, k * P:(k + 1) * P], w[:, k, j * P:(j + 1) * P], g.ident[:])
            ins.then_inc(s_w, 1)
            pe.wait_ge(s_att, 1)
            for j in range(KD):
                for k in range(KD):
                    ins = nc.tensor.matmul(ps_w[:, 16 + j * 8:24 + j * 8], w[:, k, j * P:(j + 1) * P], att[:, k, :], start=(k == 0), stop=(k == KD - 1))
            ins.then_inc(s_wa, 1)
            pe.wait_ge(s_wt, 2)

            def transposes(t):
                pe.wait_ge(s_ln, t + 1)
                if t >= 4:
                    pe.wait_ge(s_xT, t - 3)
                for k in range(KD):
                    ins = nc.tensor.transpose(ps_t[t % 4][:, k * P:(k + 1) * P], g.Y[:, t, k * P:(k + 1) * P], g.ident[:])
                ins.then_inc(s_tr, 1)

            for t in range(3):
                transposes(t)
            for t in range(NT):
                if t + 3 < NT:
                    transposes(t + 3)
                pe.wait_ge(s_xT, t + 1)
                if t >= 2:
                    pe.wait_ge(s_hst, t - 1)
                for k in range(KD):
                    ins = nc.tensor.matmul(ps_h[t % 2][:, 0:HROW], xT[:, t % 4, k, :], wt[:, k, :], start=(k == 0), stop=(k == KD - 1))
                ins.then_inc(s_h, 1)


def scores_stage(nc, g):
    with ExitStack() as ctx:
        sb = lambda n, s, d=F32: ctx.enter_context(nc.sbuf_tensor(n, s, d))
        QBITS = NT.bit_length()
        NQ = (1 << QBITS) + 1
        vals = sb("sc_vals", [P, NQ, 8])
        rest = sb("sc_rest", [P, NQ, 8])
        part = sb("sc_part", [P, 3, NQ, 8], BF16)
        ident = sb("sc_ident", [P, P], BF16)
        lane_i = sb("sc_lane_i", [LANES, 2, LC, P], I32)
        rem_i = sb("sc_rem_i", [LANES, 2, LC, P], I32)
        rem = sb("sc_rem", [LANES, 2, LC, P], BF16)
        colq = sb("sc_colq", [P, 2, T], I32)
        baseq_i = sb("sc_baseq_i", [P, T], I32)
        baseq = sb("sc_baseq", [P, T])
        qs = sb("sc_qs", [P, T]); upw = sb("sc_upw", [P, 2, T])
        hot = sb("sc_hot", [P, 2, 2, LC * P], BF16)
        gap = sb("sc_gap", [P, 2, LC * P])
        hotq = sb("sc_hotq", [P, 2, LC, NT])
        hit = sb("sc_hit", [P, 2, LC, NT, HEADS])
        two = sb("sc_two", [P, 2, LC, 2, 8])
        negr = sb("sc_negr", [P, 1])
        ps_b = [[ctx.enter_context(nc.psum_tensor(f"sc_b{k}{w}", [P, 512], F32)) for w in range(2)] for k in range(2)]
        ps_v = [[ctx.enter_context(nc.psum_tensor(f"sc_v{k}{w}", [P, 512], F32)) for w in range(2)] for k in range(2)]
        s_ld = g.sem("sc_load"); s_dve = g.sem("sc_dve"); s_set = g.sem("sc_set")
        s_b = g.sem("sc_bcast")
        s_hs = g.sem("sc_hot_src"); s_hd = g.sem("sc_hot_dst"); s_gap = g.sem("sc_gap")
        s_v = g.sem("sc_values")
        s_out = g.sem("sc_out")
        block = ctx.enter_context(nc.Block())
        MASK, SHIFT = P - 1, P.bit_length() - 1

        @block.sync
        def _(sp):
            for k, a in enumerate((g.S_src, g.S_dst)):
                sp.dma_start(lane_i[:, k], a[EPAD:EPAD + E].rearrange("(c q f) -> q c f", c=LC, f=P)).then_inc(s_ld, 16)
            sp.dma_start(vals[:, 0:NT, :], g.Atab.rearrange("(t p) a -> p t a", p=P)).then_inc(s_ld, 16)

        @block.vector
        def _(dve):
            step = Steps(dve, s_dve)
            step(dve.memset(vals[:, NT:NQ, :], 0.0))
            step(dve.tensor_copy(ident[:], g.ident[:]))
            step(dve.tensor_scalar(negr[:], g.iotap[:, 0:1], -1.0, None, ALU.mult))
            dve.wait_ge(s_ld, 48)
            step(dve.tensor_scalar(rem_i[:], lane_i[:], MASK, None, ALU.bitwise_and))
            step(dve.tensor_copy(rem[:], rem_i[:]))
            step(dve.tensor_copy(part[:, 0], vals[:]))
            step(dve.tensor_tensor(rest[:], vals[:], part[:, 0], ALU.subtract))
            step(dve.tensor_copy(part[:, 1], rest[:]))
            step(dve.tensor_tensor(rest[:], rest[:], part[:, 1], ALU.subtract))
            step(dve.tensor_copy(part[:, 2], rest[:]))
            step(dve.tensor_scalar(colq[:, 0], g.srcI[:, 0:T], SHIFT, None, ALU.arith_shift_right))
            step(dve.tensor_scalar(colq[:, 1], g.dstI[:, 0:T], SHIFT, None, ALU.arith_shift_right))
            step(dve.tensor_tensor(baseq_i[:], g.dstI[:, 0:T], g.dstrel[:, 0:T], ALU.subtract))
            step(dve.tensor_scalar(baseq_i[:], baseq_i[:], SHIFT, None, ALU.arith_shift_right))
            q4 = baseq_i[0:1, :].rearrange("a (c q) -> a c q", c=LC)
            step(dve.tensor_copy(g.baseq[:], q4[:, LC - 1, :]))
            for c in range(LC - 2, -1, -1):
                step(dve.scalar_tensor_tensor(g.baseq[:], g.baseq[:], float(1 << QBITS), q4[:, c, :], ALU.mult, ALU.add))
            step(dve.tensor_copy(qs[:], colq[:, 0]))
            step(dve.tensor_tensor(upw[:, 1], colq[:, 1], baseq_i[:], ALU.subtract))
            step(dve.tensor_scalar(upw[:, 0], upw[:, 1], -1.0, 1.0, ALU.mult, ALU.add))
            dve.sem_inc(s_set, 1)
            dve.sem_inc(s_out, 2)
            qs4 = qs[:].rearrange("p (c q) -> p c q", c=LC)
            upw4 = upw[:].rearrange("p w (c q) -> p w c q", c=LC)

            def hot_src(q, par):
                dve.wait_ge(s_b, q + 1)
                dve.wait_ge(s_v, q + 1)
                dve.tensor_scalar(hot[:, par, 0], ps_b[par][0][:], g.iotap[:, 0:1], None, ALU.is_equal).then_inc(s_hs, 1)

            def marks(q, par):
                dve.tensor_tensor(hotq[:, par], bcast(g.iota[:, 0:NT], 1, LC),
                                  qs4[:, :, bass.ds(q, 1)].to_broadcast([P, LC, NT]), ALU.is_equal).then_inc(s_dve, 1)

            def pick(q, par, n0, ahead=2):
                dve.wait_ge(s_v, q + 3)
                dve.wait_ge(s_dve, n0)
                v = ps_v[par][0][:, 0:LC * NT * HEADS].rearrange("p (c q h) -> p (c q) h", c=LC, q=NT)
                dve.tensor_tensor(hit[:, par].rearrange("p c q h -> p (c q) h"), v,
                                  bcast(hotq[:, par].rearrange("p c q -> p (c q)"), 2, HEADS), ALU.mult).then_inc(s_dve, 1)
                d = ps_v[par][1][:, 0:LC * 16].rearrange("p (c w a) -> p c w a", c=LC, w=2)
                which = bcast(upw4[:, :, :, bass.ds(q, 1)].rearrange("p w c a -> p c (w a)"), 3, 8)
                dve.tensor_tensor(two[:, par], d, which, ALU.mult).then_inc(s_dve, 1)
                if ahead == 2:
                    hot_src(q + 2, par)
                dve.wait_ge(s_dve, n0 + 1)
                dve.tensor_reduce(g.AS4[:, :, bass.ds(q, 1), 0:4].rearrange("p c a h -> p c (a h)"),
                                  hit[:, par].rearrange("p c q h -> p c h q"), AX.X, ALU.add).then_inc(s_dve, 1)
                if ahead >= 1:
                    marks(q + 1, 1 - par)
                dve.wait_ge(s_dve, n0 + 2)
                dve.tensor_reduce(g.AS4[:, :, bass.ds(q, 1), 4:12].rearrange("p c a h -> p c (a h)"),
                                  two[:, par].rearrange("p c w a -> p c a w"), AX.X, ALU.add).then_inc(s_out, 1)

            PER = 4
            hot_src(0, 0)
            hot_src(1, 1)
            marks(0, 0)
            n1 = step.n + 1
            TURN = 12
            assert (LANES - 2) % TURN == 0
            with dve.Fori(0, (LANES - 2) // TURN) as i:
                for k in range(TURN):
                    q = i * TURN + k
                    pick(q, k % 2, n1 + q * PER)
            pick(LANES - 2, 0, n1 + (LANES - 2) * PER, 1)
            pick(LANES - 1, 1, n1 + (LANES - 1) * PER, 0)

        @block.scalar
        def _(act):
            act.wait_ge(s_set, 1)
            TURN = 10
            assert LANES % TURN == 0
            with act.Fori(0, LANES // TURN) as i:
                for k in range(TURN):
                    q, par = i * TURN + k, k % 2
                    act.wait_ge(s_b, q + 1)
                    act.wait_ge(s_v, q + 1)
                    nc.scalar.activation(gap[:, par], ps_b[par][1][:], ACT.Abs, bias=negr[:]).then_inc(s_gap, 1)
                    act.wait_ge(s_gap, q + 1)
                    nc.scalar.activation(hot[:, par, 1], gap[:, par], ACT.Relu, bias=1.0, scale=-1.0).then_inc(s_hd, 1)

        @block.tensor
        def _(pe):
            pe.wait_ge(s_set, 1)
            pe.sem_inc(s_v, 2)

            def spread(q, par):
                for w in range(2):
                    ins = nc.tensor.matmul(ps_b[par][w][:], ident[0:LANES, bass.ds(q, 1)].to_broadcast([LANES, P]),
                                           rem[:, w].rearrange("q c f -> q (c f)"), start=True, stop=True)
                ins.then_inc(s_b, 1)

            def bases(q, steps):
                packed = load_values(nc, mybir.EngineType.PE, g.baseq[0:1, bass.ds(q, steps)], (1 << LC * QBITS) - 1)
                return [(v >> (QBITS * c)) & ((1 << QBITS) - 1) for v in packed for c in range(LC)]

            def values(q, par, bqs):
                pe.wait_ge(s_out, q + 1)
                pe.wait_ge(s_hs, q + 1)
                for c in range(LC):
                    for j in range(3):
                        nc.tensor.matmul(ps_v[par][0][:, c * NT * HEADS:(c + 1) * NT * HEADS], hot[:, par, 0, c * P:(c + 1) * P],
                                         part[:, j, 0:NT, 0:HEADS], start=(j == 0), stop=(j == 2))
                pe.wait_ge(s_hd, q + 1)
                for c, bq in enumerate(bqs):
                    for j in range(3):
                        ins = nc.tensor.matmul(ps_v[par][1][:, c * 16:(c + 1) * 16], hot[:, par, 1, c * P:(c + 1) * P],
                                               part[:, j, bass.ds(bq, 2), :].rearrange("p q a -> p (q a)"), start=(j == 0), stop=(j == 2))
                ins.then_inc(s_v, 1)

            spread(0, 0)
            TURN = 12
            with pe.Fori(0, (LANES - 2) // TURN) as i:
                for k in range(TURN):
                    q = i * TURN + k
                    if k % 2 == 0:
                        bqs = bases(q, 2)
                    spread(q + 1, (k + 1) % 2)
                    values(q, k % 2, bqs[k % 2 * LC:(k % 2 + 1) * LC])
            bqs = bases(LANES - 2, 2)
            spread(LANES - 1, 1)
            values(LANES - 2, 0, bqs[0:LC])
            values(LANES - 1, 1, bqs[LC:])


def softmax_stage(nc, g):
    with ExitStack() as ctx:
        sb = lambda n, s, d: ctx.enter_context(nc.sbuf_tensor(n, s, d))
        L = sb("sm_L", [LANES, 12, LC, P], F32)
        fw = sb("sm_fw", [LANES, HEADS, LC, P], F32)
        bw = sb("sm_bw", [LANES, HEADS, LC, P], F32)
        tails = sb("sm_tails", [LANES, 2, LC, 8], F32)
        rowt = sb("sm_rowt", [HEADS, 2, 2, T], F32)
        inc = sb("sm_inc", [HEADS, 2, T + 1], F32)
        carry = sb("sm_carry", [LANES, 2, LC, HEADS], F32)
        notfirst = sb("sm_notfirst", [LANES, LC, P], F32)
        pe_out = sb("sm_p", [LANES, 8, LC, P], F32)
        ps = [ctx.enter_context(nc.psum_tensor(f"sm_ps{k}", [P, 512], F32)) for k in range(4)]
        ps_r = [ctx.enter_context(nc.psum_tensor(f"sm_row{k}", [HEADS, 512], F32)) for k in range(4)]
        s_tr = g.sem("sm_tr"); s_L = g.sem("sm_L"); s_dve = g.sem("sm_dve"); s_tail = g.sem("sm_tail")
        s_row = g.sem("sm_row"); s_inc = g.sem("sm_inc"); s_car = g.sem("sm_carry")
        s_z = g.sem("sm_z"); s_p = g.sem("sm_pe"); s_pt = g.sem("sm_pt"); s_cp = g.sem("sm_cp")
        block = ctx.enter_context(nc.Block())

        @block.tensor
        def _(pe):
            for a in range(12):
                if a >= 4:
                    pe.wait_ge(s_L, a - 3)
                for c in range(LC):
                    ins = nc.tensor.transpose(ps[a % 4][0:LANES, c * P:(c + 1) * P], g.AS[:, c * LANES:(c + 1) * LANES, a], g.ident[:])
                ins.then_inc(s_tr, 1)
            pe.wait_ge(s_tail, 1)
            for d in range(2):
                for w in range(2):
                    for c in range(LC):
                        ins = nc.tensor.transpose(ps_r[d * 2 + w][:, c * LANES:(c + 1) * LANES], tails[:, d, c, 4 * w:4 * w + 4], g.ident[0:LANES, 0:LANES])
            ins.then_inc(s_row, 1)
            pe.wait_ge(s_inc, 1)
            for d in range(2):
                for c in range(LC):
                    src = inc[:, 0, c * LANES:(c + 1) * LANES] if d == 0 else inc[:, 1, c * LANES + 1:(c + 1) * LANES + 1]
                    ins = nc.tensor.transpose(ps[0][0:LANES, (d * LC + c) * 4:(d * LC + c) * 4 + 4], src, g.ident[0:HEADS, 0:HEADS])
            ins.then_inc(s_car, 1)
            for a in range(8):
                pe.wait_ge(s_p, a + 1)
                if a >= 4:
                    pe.wait_ge(s_pt, a - 3)
                for c in range(LC):
                    ins = nc.tensor.transpose(ps[a % 4][:, c * LANES:(c + 1) * LANES], pe_out[:, a, c, :], g.ident[0:LANES, 0:LANES])
                ins.then_inc(s_cp, 1)

        @block.scalar
        def _(act):
            for a in range(12):
                act.wait_ge(s_tr, a + 1)
                nc.scalar.activation(L[:, a], ps[a % 4][0:LANES, :].rearrange("p (c f) -> p c f", c=LC), ACT.Copy).then_inc(s_L, 1)
            for a in range(8):
                act.wait_ge(s_z, a + 1)
                nc.scalar.activation(pe_out[:, a], pe_out[:, a], ACT.Exp).then_inc(s_p, 1)

        @block.vector
        def _(dve):
            step = Steps(dve, s_dve)
            step(dve.tensor_scalar(notfirst[:], g.first[:], 1.0, BIG, ALU.subtract, ALU.mult))
            dve.wait_ge(s_L, 12)

            def scan(out, d, c, h, initial):
                v, m = L[:, h, c, :], (g.firstneg if d == 0 else g.endneg)[:, c, :]
                o = out[:, h, c, :]
                if d:
                    v, m, o = v[:, ::-1], m[:, ::-1], o[:, ::-1]
                return dve.tensor_tensor_scan(o, m, v, initial, ALU.add, ALU.max)

            n = 0
            for d, out in ((0, fw), (1, bw)):
                for h in range(HEADS):
                    for c in range(LC):
                        scan(out, d, c, h, -BIG).then_inc(s_dve, 1)
                        n += 1
            step.n = step.n + n
            dve.wait_ge(s_dve, step.n)
            dve.tensor_copy(tails[:, 0, :, 0:4].rearrange("q c h -> q h c"), fw[:, :, :, P - 1])
            step(dve.tensor_copy(tails[:, 1, :, 0:4].rearrange("q c h -> q h c"), bw[:, :, :, 0]))
            step(dve.tensor_reduce(tails[:, 0, :, 4], g.firstneg[:], AX.X, ALU.min))
            step(dve.tensor_reduce(tails[:, 1, :, 4], g.endneg[:], AX.X, ALU.min))
            dve.tensor_copy(tails[:, 0, :, 5:8], bcast(tails[:, 0, :, 4], 2, 3))
            step(dve.tensor_copy(tails[:, 1, :, 5:8], bcast(tails[:, 1, :, 4], 2, 3)))
            dve.sem_inc(s_tail, 1)
            dve.memset(inc[:, 0, 0:1], -BIG)
            step(dve.memset(inc[:, 1, T:T + 1], -BIG))
            dve.wait_ge(s_row, 1)
            for d in range(2):
                for w in range(2):
                    step(dve.tensor_copy(rowt[:, d, w, :], ps_r[d * 2 + w][:, 0:T]))
            dve.tensor_tensor_scan(inc[:, 0, 1:T + 1], rowt[:, 0, 1, :], rowt[:, 0, 0, :], -BIG, ALU.add, ALU.max)
            step(dve.tensor_tensor_scan(inc[:, 1, 0:T][:, ::-1], rowt[:, 1, 1, :][:, ::-1], rowt[:, 1, 0, :][:, ::-1], -BIG, ALU.add, ALU.max))
            dve.sem_inc(s_inc, 1)
            dve.wait_ge(s_car, 1)
            step(dve.tensor_copy(carry[:], ps[0][0:LANES, 0:2 * LC * 4].rearrange("p (d c h) -> p d c h", d=2, c=LC)))
            for d, out in ((0, fw), (1, bw)):
                for h in range(HEADS):
                    for c in range(LC):
                        scan(out, d, c, h, carry[:, d, c, h:h + 1]).then_inc(s_dve, 1)
                        step.n += 1
            dve.wait_ge(s_dve, step.n)
            f2 = lambda ap: ap.rearrange("q h c f -> q (h c f)")
            a_s, a_sd, a_d = f2(L[:, 0:4]), f2(L[:, 4:8]), f2(L[:, 8:12])
            M, B = f2(fw[:]), f2(bw[:])
            step(dve.tensor_tensor(M, M, B, ALU.max))
            step(dve.tensor_tensor(M, M, a_sd, ALU.max))
            step(dve.tensor_tensor(M, M, a_d, ALU.add))
            step(dve.scalar_tensor_tensor(M, M, NEG_SLOPE, M, ALU.mult, ALU.max))
            for w, a in ((0, a_s), (1, a_sd)):
                z = f2(pe_out[:, 4 * w:4 * w + 4])
                step(dve.tensor_tensor(z, a, a_d, ALU.add))
                step(dve.scalar_tensor_tensor(z, z, NEG_SLOPE, z, ALU.mult, ALU.max))
                step(dve.tensor_tensor(z, z, M, ALU.subtract))
                if w == 1:
                    step(dve.tensor_tensor(pe_out[:, 4:8], pe_out[:, 4:8], bcast(notfirst[:], 1, HEADS), ALU.add))
                dve.sem_inc(s_z, 4)
            dve.wait_ge(s_p, 8)
            for a in range(8):
                dve.wait_ge(s_cp, a + 1)
                dve.tensor_copy(g.PT[:, 0:T, a], ps[a % 4][:, 0:T]).then_inc(s_pt, 1)


def edge_pass(nc, g, kind, table, index, n_pass):
    gat = kind == "gat"
    KA = KD + 1 if gat else KD
    TURNS = T // RING
    assert (TURNS - 1) * RING * P >= E0
    AHEAD = 8
    NBK = 5
    with ExitStack() as ctx:
        sb = lambda n, s, d=F32: ctx.enter_context(nc.sbuf_tensor(f"{n}{n_pass}", s, d))
        ix = sb("ix", [P, 2, HALF], I32)
        ring = sb("ring", [P, RING, D])
        hot = sb("hot", [P, RING, WIN])
        gap = sb("gap", [P, 2, WIN])
        negd = sb("negd", [P, T])
        p8 = sb("p8", [P, RING, P if gat else 8])
        ps = [ctx.enter_context(nc.psum_tensor(f"ep{n_pass}_{k}", [P, 512], F32)) for k in range(NBK)]
        s_ix = g.sem("ep_idx"); s_turn = g.sem("ep_turn")
        s_g = [g.sem(f"ep_g{k}") for k in range(RING)]
        s_gap = g.sem("ep_gap"); s_hot = g.sem("ep_hot")
        s_p8 = g.sem("ep_p8"); s_msg = g.sem("ep_msg")
        s_mm = g.sem("ep_mm")
        s_acc = g.sem("ep_acc")
        s_zero = g.sem("ep_zero"); s_neg = g.sem("ep_neg")
        block = ctx.enter_context(nc.Block())

        def rounds(eng, body):
            unsorted = eng.value_load(g.unsorted[0:1, 0:1], min_val=0, max_val=E)
            with eng.Fori(0, TURNS - 2) as i:
                body(i, True, False)
            body(TURNS - 2, False, False)
            with eng.If(unsorted > 0):
                body(TURNS - 1, False, True)

        @block.gpsimd
        def _(pool):
            def fetch(i, follows, alone):
                for h in range(2):
                    pool.wait_ge(s_mm, i * RING + (h + 1) * HALF)
                    pool.sem_inc(s_turn, 1)
                    pool.tensor_copy(ix[:, h, :], index[:, bass.ds(i * RING + h * HALF, HALF)]).then_inc(s_ix, 1)
                    pool.wait_ge(s_ix, 2 * i + h + 1)
                    pool.sem_inc(s_turn, 1)
                    for k in range(HALF):
                        pool.indirect_dma_start(ring[:, h * HALF + k, :], None, table,
                                                bass.IndirectOffsetOnAxis(ix[:, h, k:k + 1], axis=0)).then_inc(s_g[h * HALF + k], 16)

            rounds(pool, fetch)

        @block.scalar
        def _(act):
            act.wait_ge(s_neg, 2 if gat else 1)

            def one_hots(i, follows, alone):
                for k in range(RING):
                    tile = i * RING + k
                    act.wait_ge(s_mm, tile + 1)
                    nc.scalar.activation(gap[:, k % 2], g.iota[:], ACT.Abs, bias=negd[:, bass.ds(tile, 1)]).then_inc(s_gap, 1)
                    act.wait_ge(s_gap, tile + 1)
                    nc.scalar.activation(hot[:, k], gap[:, k % 2], ACT.Relu, bias=1.0, scale=-1.0).then_inc(s_hot, 1)
                    if gat:
                        nc.scalar.activation(p8[:, k, 0:8], g.PT[:, bass.ds(tile, 1), :].rearrange("p a w -> p (a w)"), ACT.Copy).then_inc(s_p8, 1)

            rounds(act, one_hots)

        @block.tensor
        def _(pe):
            pe.sem_inc(s_mm, RING)

            def products(i, follows, alone):
                for k in range(RING):
                    tile = i * RING + k
                    pe.wait_ge(s_hot, tile + 1)
                    if gat:
                        pe.wait_ge(s_p8, tile + 1)
                        pe.wait_ge(s_msg, tile + 1)
                    else:
                        pe.wait_ge(s_g[k], 16 * i + 16)
                    pe.wait_ge(s_acc, tile + 1)
                    b = ps[k % NBK]
                    for j in range(KD):
                        ins = nc.tensor.matmul(b[:, j * WIN:(j + 1) * WIN], ring[:, k, j * P:(j + 1) * P], hot[:, k, :], start=True, stop=True)
                    if gat:
                        ins = nc.tensor.matmul(b[:, KD * WIN:(KD + 1) * WIN], p8[:, k, :], hot[:, k, :], start=True, stop=True)
                    ins.then_inc(s_mm, 1)

            rounds(pe, products)

        @block.vector
        def _(dve):
            dve.tensor_scalar(negd[:], g.dstrel[:, 0:T], -1.0, None, ALU.mult).then_inc(s_neg, 1)
            dve.memset(g.ACC[:], 0.0).then_inc(s_zero, 1)
            if gat:
                dve.memset(p8[:], 0.0).then_inc(s_neg, 1)
            dve.wait_ge(s_zero, 1)
            dve.sem_inc(s_acc, NBK)

            def weigh(tile, k, r):
                dve.wait_ge(s_g[k], r)
                rows = ring[:, k, :].rearrange("p (a c) -> p a c", a=HEADS)
                dve.tensor_tensor(rows, rows, bcast(g.PT[:, bass.ds(tile, 1), 0:4].rearrange("p a w -> p (a w)"), 2, CH), ALU.mult).then_inc(s_msg, 1)

            def sums(i, follows, alone):
                if gat and alone:
                    for k in range(AHEAD):
                        weigh(i * RING + k, k, 16 * i + 16)
                for h in range(2):
                    starts = load_values(nc, mybir.EngineType.DVE, g.base[0:1, bass.ds(i * RING + h * HALF, HALF)], N - 1)
                    for k in range(h * HALF, (h + 1) * HALF):
                        tile = i * RING + k
                        w = k + AHEAD
                        if gat and (follows or w < RING):
                            weigh(tile + AHEAD, w % RING, 16 * i + 16 * (1 + w // RING))
                        dve.wait_ge(s_mm, tile + (RING + 1))
                        b = ps[k % NBK]
                        acc = g.ACC[:, :, bass.ds(starts[k - h * HALF], WIN)]
                        dve.wait_ge(s_acc, tile + NBK)
                        dve.tensor_tensor(acc, acc, b[:, 0:KA * WIN].rearrange("p (j w) -> p j w", j=KA), ALU.add).then_inc(s_acc, 1)

            if gat:
                for k in range(AHEAD):
                    weigh(k, k, 16)
            rounds(dve, sums)


def gat_finish_stage(nc, g):
    with ExitStack() as ctx:
        sb = lambda n, s, d: ctx.enter_context(nc.sbuf_tensor(n, s, d))
        Hs = sb("gf_h", [P, NT, D], F32)
        den8 = sb("gf_den8", [P, NT, 8], F32)
        den = sb("gf_den", [P, NT, HEADS], F32)
        bias = sb("gf_bias", [P, D], F32)
        ps = [ctx.enter_context(nc.psum_tensor(f"gf_ps{k}", [P, 512], F32)) for k in range(4)]
        s_ld = g.sem("gf_load"); s_tr = g.sem("gf_tr"); s_cp = g.sem("gf_cp"); s_dve = g.sem("gf_dve")
        s_m = g.sem("gf_sums"); s_e = g.sem("gf_exp")
        block = ctx.enter_context(nc.Block())

        @block.sync
        def _(sp):
            sp.dma_start(Hs[:], g.Htab.rearrange("(t p) d -> p t d", p=P)).then_inc(s_ld, 16)
            sp.dma_start(bias[:], g.gat_bias.partition_broadcast(P)).then_inc(s_ld, 16)

        @block.tensor
        def _(pe):
            for t in range(NT):
                if t >= 4:
                    pe.wait_ge(s_cp, t - 3)
                b = ps[t % 4]
                for j in range(KD):
                    nc.tensor.transpose(b[:, j * P:(j + 1) * P], g.ACC[:, j, t * P:(t + 1) * P], g.ident[:])
                nc.tensor.transpose(b[:, D:D + 8], g.ACC[0:8, KD, t * P:(t + 1) * P], g.ident[0:8, 0:8]).then_inc(s_tr, 1)

        @block.scalar
        def _(act):
            for t in range(NT):
                act.wait_ge(s_tr, t + 1)
                nc.scalar.activation(g.Z[:, t, :], ps[t % 4][:, 0:D], ACT.Copy)
                nc.scalar.activation(den8[:, t, :], ps[t % 4][:, D:D + 8], ACT.Copy).then_inc(s_cp, 1)
            act.wait_ge(s_m, 1)
            nc.scalar.activation(Hs[:], g.Z[:], ACT.Exp).then_inc(s_e, 1)

        @block.vector
        def _(dve):
            step = Steps(dve, s_dve)
            dve.wait_ge(s_ld, 32)
            step(dve.scalar_tensor_tensor(g.X[:], g.X[:], -1.0, g.Y[:], ALU.add, ALU.add))
            dve.wait_ge(s_cp, NT)
            heads = lambda ap: ap.rearrange("p t (a c) -> p t a c", a=HEADS)
            step(dve.tensor_tensor(den[:], den8[:, :, 0:4], den8[:, :, 4:8], ALU.add))
            step(dve.tensor_scalar(den[:], den[:], 1e-16, None, ALU.add))
            step(dve.reciprocal(den[:], den[:]))
            step(dve.tensor_tensor(heads(Hs[:]), heads(Hs[:]), bcast(den8[:, :, 4:8], 3, CH), ALU.mult))
            step(dve.tensor_tensor(g.Z[:], g.Z[:], Hs[:], ALU.add))
            step(dve.tensor_tensor(heads(g.Z[:]), heads(g.Z[:]), bcast(den[:], 3, CH), ALU.mult))
            step(dve.tensor_tensor(g.Z[:], g.Z[:], bcast(bias[:], 1, NT), ALU.add))
            dve.sem_inc(s_m, 1)
            step(dve.scalar_tensor_tensor(g.X[:], g.Z[:], 0.0, g.X[:], ALU.max, ALU.add))
            dve.wait_ge(s_e, 1)
            step(dve.scalar_tensor_tensor(g.X[:], Hs[:], 1.0, g.X[:], ALU.min, ALU.add))


def router_stage(nc, g, which):
    pre = f"rt{which}_"
    gw_dram, gb_dram = (g.gate_w, g.gate_b) if which == 0 else (g.Wr, g.br)
    trash = NE * B0 if which == 0 else NB1 * B1
    with ExitStack() as ctx:
        sb = lambda n, s, d=F32: ctx.enter_context(nc.sbuf_tensor(pre + n, s, d))
        gw = sb("gw", [P, KD, NE]); gb = sb("gb", [P, NE])
        xT = sb("xT", [P, 4, KD, P])
        L = sb("L", [P, NT, NE]); e1 = sb("e1", [P, NT, NE]); e2 = sb("e2", [P, NT, NE])
        oh = [sb("oh0", [P, NT, NE]), sb("oh1", [P, NT, NE])]
        both = sb("both", [P, NT, NE]); pos = sb("pos", [P, NT, NE]); tot = sb("tot", [P, NT, NE])
        run = sb("run", [P, NT, NE])
        mx = [sb("mx0", [P, NT]), sb("mx1", [P, NT])]
        low = sb("low", [P, NT]); a = sb("a", [P, NT]); b = sb("b", [P, NT]); c = sb("c", [P, NT])
        rtok = sb("rtok", [P, NT]); rtok_i = sb("rtok_i", [P, NT], I32)
        nblk = sb("nblk", [P, NE]); nblk_i = sb("nblk_i", [P, NE], I32); ends = sb("ends", [P, NE]); onesr = sb("onesr", [P, NT])
        start = sb("start", [P, NE]); blk = sb("blk", [1, NB1, NE]); blkn = sb("blkn", [1, NB1])
        slot = sb("slot", [P, 2, NT], I32)
        ps_t = [ctx.enter_context(nc.psum_tensor(f"{pre}t{k}", [P, 512], F32)) for k in range(4)]
        ps_l = ctx.enter_context(nc.psum_tensor(pre + "l", [P, 512], F32))
        ps_p = ctx.enter_context(nc.psum_tensor(pre + "p", [P, 512], F32))
        ps_q = ctx.enter_context(nc.psum_tensor(pre + "q", [P, 512], F32))
        s_ld = g.sem(pre + "load"); s_dve = g.sem(pre + "dve"); s_var = g.sem(pre + "var"); s_sq = g.sem(pre + "sqrt")
        s_ln = g.sem(pre + "ln"); s_tr = g.sem(pre + "tr"); s_xT = g.sem(pre + "xT"); s_lg = g.sem(pre + "logits")
        s_e = g.sem(pre + "exp"); s_ex = g.sem(pre + "exped"); s_oh = g.sem(pre + "onehot"); s_pp = g.sem(pre + "prefix")
        s_slot = g.sem(pre + "slot"); s_sc = g.sem(pre + "scatter"); s_z = g.sem(pre + "zeroed"); s_io = g.sem(pre + "iota")
        s_ln2 = g.sem(pre + "ln2"); s_zy = g.sem(pre + "zeroed_results")
        block = ctx.enter_context(nc.Block())
        tokens = g.Y if which == 0 else g.Z

        @block.sync
        def _(sp):
            sp.dma_start(gw[:], gw_dram.rearrange("(k p) e -> p k e", p=P)).then_inc(s_ld, 16)
            sp.dma_start(gb[:], gb_dram.partition_broadcast(P)).then_inc(s_ld, 16)
            rows = g.XB[0:trash, :].rearrange("(r p) d -> p r d", p=P)
            for r in range(0, trash // P, 16):
                sp.dma_start(rows[:, r:r + 16, :], bcast(g.zrow[:], 1, 16)).then_inc(s_z, 16)
            if which == 1:
                rows = g.YB[NB1_MIN * B1:NB1 * B1, :].rearrange("(r p) d -> p r d", p=P)
                sp.dma_start(rows, bcast(g.zrow[:], 1, (NB1 - NB1_MIN) * B1 // P)).then_inc(s_zy, 16)
                sp.wait_ge(s_zy, 16)

        @block.tensor
        def _(pe):
            pe.wait_ge(s_ld, 32)
            for t in range(NT + 3):
                if t < NT:
                    pe.wait_ge(s_ln, t + 1)
                    if t >= 4:
                        pe.wait_ge(s_xT, t - 3)
                    for k in range(KD):
                        ins = nc.tensor.transpose(ps_t[t % 4][:, k * P:(k + 1) * P], g.Y[:, t, k * P:(k + 1) * P], g.ident[:])
                    ins.then_inc(s_tr, 1)
                if t >= 3:
                    u = t - 3
                    pe.wait_ge(s_xT, u + 1)
                    for k in range(KD):
                        ins = nc.tensor.matmul(ps_l[:, u * NE:(u + 1) * NE], xT[:, u % 4, k, :], gw[:, k, :], start=(k == 0), stop=(k == KD - 1))
                    ins.then_inc(s_lg, 1)
            pe.wait_ge(s_oh, 1)
            src = both[:].rearrange("p t e -> p (t e)")
            nc.tensor.matmul(ps_p[:, 0:NT * NE], g.upper[:], src, start=True, stop=True)
            nc.tensor.matmul(ps_q[:, 0:NT * NE], g.ones[:], src, start=True, stop=True).then_inc(s_pp, 1)

        @block.scalar
        def _(act):
            act.wait_ge(s_var, 1)
            nc.scalar.activation(g.ln_s[:], g.ln_var[:], ACT.Sqrt).then_inc(s_sq, 1)
            for t in range(NT):
                act.wait_ge(s_tr, t + 1)
                if t >= 4:
                    act.wait_ge(s_lg, t - 3)
                nc.scalar.activation(xT[:, t % 4], ps_t[t % 4][:, 0:D].rearrange("p (k n) -> p k n", k=KD), ACT.Copy).then_inc(s_xT, 1)
            if which == 1:
                act.wait_ge(s_var, 2)
                nc.scalar.activation(g.ln_s[:], g.ln_var[:], ACT.Sqrt).then_inc(s_sq, 1)
            act.wait_ge(s_e, 1)
            if which == 0:
                nc.scalar.activation(e1[:], e1[:], ACT.Exp).then_inc(s_ex, 1)
            else:
                nc.scalar.activation(a[:], a[:], ACT.Exp).then_inc(s_ex, 1)

        @block.gpsimd
        def _(pool):
            pool.iota(rtok_i[:], [[P, NT]], base=trash, channel_multiplier=1).then_inc(s_io, 1)
            pool.wait_ge(s_slot, 1)
            pool.wait_ge(s_z, 16 * (-(-(trash // P) // 16)))
            n = 0
            for k in range(which + 1):
                for t in range(NT):
                    pool.indirect_dma_start(g.XB, bass.IndirectOffsetOnAxis(slot[:, k, t:t + 1], axis=0), tokens[:, t, :], None).then_inc(s_sc, 16)
                    n += 16
            pool.wait_ge(s_sc, n)

        @block.vector
        def _(dve):
            step = Steps(dve, s_dve)
            layernorm(nc, g, dve, step, s_var, s_sq, 1, g.X, g.Y, s_ln)
            if which == 1:
                layernorm(nc, g, dve, step, s_var, s_sq, 2, g.Y, g.Z, s_ln2)
            dve.wait_ge(s_lg, NT)
            lg = ps_l[:, 0:NT * NE].rearrange("p (t e) -> p t e", t=NT)
            step(dve.tensor_tensor(L[:], lg, bcast(gb[:], 1, NT), ALU.add))
            iota8 = bcast(g.iota[:, 0:NE], 1, NT)

            def best(values, m, hot):
                step(dve.tensor_reduce(m[:], values[:], AX.X, ALU.max))
                step(dve.tensor_tensor(hot[:], values[:], bcast(m[:], 2, NE), ALU.is_equal))
                step(dve.scalar_tensor_tensor(e2[:], hot[:], -64.0, iota8, ALU.mult, ALU.add))
                step(dve.tensor_reduce(low[:], e2[:], AX.X, ALU.min))
                step(dve.tensor_tensor(hot[:], e2[:], bcast(low[:], 2, NE), ALU.is_equal))

            best(L, mx[0], oh[0])
            if which == 0:
                step(dve.tensor_tensor(e1[:], L[:], bcast(mx[0][:], 2, NE), ALU.subtract))
            else:
                step(dve.scalar_tensor_tensor(L[:], oh[0][:], -BIG, L[:], ALU.mult, ALU.add))
                best(L, mx[1], oh[1])
                step(dve.tensor_tensor(a[:], mx[1][:], mx[0][:], ALU.subtract))
            dve.sem_inc(s_e, 1)
            for k in range(which + 1):
                step(dve.tensor_scalar(oh[k][:, NT - 1, :], oh[k][:, NT - 1, :], g.valid[:], None, ALU.mult))
            if which == 0:
                step(dve.tensor_copy(both[:], oh[0][:]))
            else:
                step(dve.tensor_tensor(both[:], oh[0][:], oh[1][:], ALU.add))
            dve.sem_inc(s_oh, 1)
            dve.wait_ge(s_ex, 1)
            if which == 0:
                step(dve.tensor_reduce(a[:], e1[:], AX.X, ALU.add))
                step(dve.reciprocal(g.wgt[:, 0, :], a[:]))
            else:
                step(dve.tensor_scalar(b[:], a[:], 1.0, None, ALU.add))
                step(dve.reciprocal(g.wgt[:, 0, :], b[:]))
                step(dve.tensor_tensor(g.wgt[:, 1, :], g.wgt[:, 0, :], a[:], ALU.mult))
            dve.wait_ge(s_pp, 1)
            flat = lambda x: x[:].rearrange("p t e -> p (t e)")
            step(dve.tensor_copy(flat(tot), ps_q[:, 0:NT * NE]))
            step(dve.memset(onesr[:], 1.0))
            for e in range(NE):
                dve.tensor_tensor_scan(run[:, :, e], onesr[:], tot[:, :, e], 0.0, ALU.mult, ALU.add).then_inc(s_dve, 1)
            step.n += NE
            dve.wait_ge(s_dve, step.n)
            step(dve.tensor_tensor(flat(pos), ps_p[:, 0:NT * NE], flat(run), ALU.add))
            step(dve.tensor_tensor(pos[:], pos[:], tot[:], ALU.subtract))
            if which == 0:
                step(dve.tensor_scalar(start[:], g.iota[:, 0:NE], float(B0), -1.0, ALU.mult, ALU.add))
            else:
                step(dve.tensor_scalar(nblk_i[:], run[:, NT - 1, :], float(B1 - 1), None, ALU.add))
                step(dve.tensor_scalar(nblk_i[:], nblk_i[:], B1.bit_length() - 1, None, ALU.arith_shift_right))
                step(dve.tensor_copy(nblk[:], nblk_i[:]))
                step(dve.tensor_tensor_scan(ends[:], onesr[:, 0:NE], nblk[:], 0.0, ALU.mult, ALU.add))
                step(dve.tensor_tensor(start[:], ends[:], nblk[:], ALU.subtract))
                step(dve.tensor_scalar(start[:], start[:], float(B1), -1.0, ALU.mult, ALU.add))
                step(dve.tensor_tensor(blk[:], bcast(ends[0:1, :], 1, NB1), bcast(g.iota[0:1, 0:NB1], 2, NE), ALU.is_le))
                step(dve.tensor_reduce(blkn[:], blk[:], AX.X, ALU.add))
                step(dve.tensor_scalar(blkn[:], blkn[:], float(NE - 1), None, ALU.min))
                step(dve.tensor_copy(g.blk_expert[:], blkn[:]))
                step(dve.tensor_copy(g.blk_used[:], ends[0:1, NE - 1:NE]))
            dve.wait_ge(s_io, 1)
            step(dve.tensor_copy(rtok[:], rtok_i[:]))
            step(dve.tensor_tensor(tot[:], pos[:], bcast(start[:], 1, NT), ALU.add))
            for k in range(which + 1):
                step(dve.tensor_tensor(e2[:], tot[:], oh[k][:], ALU.mult))
                step(dve.tensor_reduce(a[:], e2[:], AX.X, ALU.add))
                step(dve.tensor_reduce(c[:], oh[k][:], AX.X, ALU.add))
                if which == 0:
                    step(dve.tensor_tensor(e2[:], pos[:], oh[k][:], ALU.mult))
                    step(dve.tensor_reduce(b[:], e2[:], AX.X, ALU.add))
                    step(dve.tensor_scalar(low[:], b[:], float(CAP), None, ALU.is_le))
                    step(dve.tensor_tensor(c[:], c[:], low[:], ALU.mult))
                    step(dve.tensor_tensor(g.wgt[:, 0, :], g.wgt[:, 0, :], c[:], ALU.mult))
                    step(dve.tensor_scalar(low[:], b[:], float(CAP), 0.0, ALU.subtract, ALU.max))
                    step(dve.tensor_tensor(b[:], a[:], low[:], ALU.subtract))
                    step(dve.tensor_copy(g.gslot[:, k, :], b[:]))
                else:
                    step(dve.tensor_copy(g.gslot[:, k, :], a[:]))
                step(dve.tensor_tensor(a[:], a[:], rtok[:], ALU.subtract))
                step(dve.tensor_tensor(a[:], a[:], c[:], ALU.mult))
                step(dve.tensor_tensor(slot[:, k, :], a[:], rtok[:], ALU.add))
                step(dve.tensor_scalar(rtok[:], rtok[:], float(NP), None, ALU.add))
            dve.sem_inc(s_slot, 1)


def experts_stage(nc, g, which):
    pre = f"ex{which}_"
    B, NB = (B0, NE) if which == 0 else (B1, NB1)
    S = B // P
    G = 2
    NG = FC // G
    LAG = 2
    W1, b1, W2, b2 = (g.f0_w1, g.f0_b1, g.f0_w2, g.f0_b2) if which == 0 else (g.f1_w1, g.f1_b1, g.f1_w2, g.f1_b2)
    func = ACT.Relu if which == 0 else ACT.Gelu
    with ExitStack() as ctx:
        sb = lambda n, s, d=F32: ctx.enter_context(nc.sbuf_tensor(pre + n, s, d))
        w1, w2, xb, y = [], [], [], []
        for free in (g.Y, g.Z):
            flat = free[:].rearrange("p t d -> p (t d)")
            w1.append(flat[:, 0:KD * F].rearrange("p (k f) -> p k f", k=KD))
            w2.append(flat[:, KD * F:2 * KD * F].rearrange("p (c d) -> p c d", c=FC))
            xb.append(flat[:, 2 * KD * F:2 * KD * F + S * D].rearrange("p (s d) -> p s d", s=S))
            y.append(flat[:, 2 * KD * F + S * D:2 * KD * F + 2 * S * D].rearrange("p (s d) -> p s d", s=S))
        w1_hi = sb("w1_hi", [P, 2, KD, F], F32R); w1_lo = sb("w1_lo", [P, 2, KD, F], F32R)
        w2_hi = sb("w2_hi", [P, FC, D], F32R); w2_lo = sb("w2_lo", [P, FC, D], F32R)
        xT = sb("xT", [P, KD, B]); x_hi = sb("x_hi", [P, 2, KD, B], F32R); x_lo = sb("x_lo", [P, 2, KD, B], F32R)
        hT = sb("hT", [P, 2, B]); h_hi = sb("h_hi", [P, FC, B], F32R); h_lo = sb("h_lo", [P, FC, B], F32R)
        b1r = sb("b1r", [NE * FC, P]); b1c = sb("b1c", [P, NE * FC]); b2b = sb("b2b", [P, NE, D])
        lnr = sb("lnr", [NE * KD, 2, P]); lnc = sb("lnc", [P, 2, NE * KD])
        ps_x = ctx.enter_context(nc.psum_tensor(pre + "px", [P, KD, 512], F32))
        ps_h = [ctx.enter_context(nc.psum_tensor(f"{pre}ph{k}", [P, 512], F32)) for k in range(2)]
        ps_y = [ctx.enter_context(nc.psum_tensor(f"{pre}py{k}", [P, 512], F32)) for k in range(S)]
        s_c = g.sem(pre + "const"); s_ct = g.sem(pre + "const_tr"); s_cc = g.sem(pre + "const_cp")
        s_w1 = [g.sem(f"{pre}w1_{k}") for k in range(2)]; s_w2 = [g.sem(f"{pre}w2_{k}") for k in range(2)]
        s_xb = [g.sem(f"{pre}xb_{k}") for k in range(2)]; s_yst = [g.sem(f"{pre}yst_{k}") for k in range(2)]
        s_tr = g.sem(pre + "tr")
        s_x = g.sem(pre + "x")
        s_xl = g.sem(pre + "x_lo")
        s_w1h = g.sem(pre + "w1_hi"); s_w1l = g.sem(pre + "w1_lo")
        s_w2h = g.sem(pre + "w2_hi"); s_w2l = g.sem(pre + "w2_lo")
        s_h = g.sem(pre + "h")
        s_act = g.sem(pre + "act")
        s_hh = g.sem(pre + "h_hi")
        s_hl = g.sem(pre + "h_lo")
        s_y2 = g.sem(pre + "y2")
        s_py = g.sem(pre + "py")
        s_turn = g.sem(pre + "turn")
        block = ctx.enter_context(nc.Block())

        def rounds(eng, body, ahead=0):
            sure = NB - 2 if which == 0 else NB1_MIN // 8 * 8
            used = None if which == 0 else eng.value_load(g.blk_used[0:1, 0:1], min_val=0, max_val=NB1)
            turn = 3 if which == 0 else 4
            with eng.Fori(0, sure // 2 // turn) as j:
                for m in range(turn):
                    i = j * turn + m
                    body(i * 2, i, 0, False)
                    body(i * 2 + 1, i, 1, False)
            for n in range(sure, NB):
                if which == 0 or n < NB1_MIN + ahead:
                    body(n, n // 2, n % 2, n == NB - 1)
                else:
                    with eng.If(used > n - ahead):
                        body(n, n // 2, n % 2, n == NB - 1)

        def expert(eng, n):
            return n if which == 0 else eng.value_load(g.blk_expert[0:1, bass.ds(n, 1)], min_val=0, max_val=NE - 1)

        @block.sync
        def _(sp):
            sp.dma_start(b1r[:], b1.rearrange("e (c p) -> (e c) p", p=P)).then_inc(s_c, 16)
            sp.dma_start(b2b[:], b2.partition_broadcast(P)).then_inc(s_c, 16)
            if which == 1:
                sp.dma_start(lnr[:, 0, :], g.ln_g.rearrange("e (k p) -> (e k) p", p=P)).then_inc(s_c, 16)
                sp.dma_start(lnr[:, 1, :], g.ln_b.rearrange("e (k p) -> (e k) p", p=P)).then_inc(s_c, 16)

            def load(n, i, par, last):
                e = expert(sp, n)
                sp.wait_ge(s_tr, n + 1)
                sp.dma_start(xb[par], g.XB[bass.ds(n * B, B), :].rearrange("(s p) d -> p s d", p=P)).then_inc(s_xb[par], 16)
                sp.wait_ge(s_w1l, n * NG + NG)
                sp.dma_start(w1[par], W1[bass.ds(e, 1)].rearrange("a (k p) f -> p (a k) f", p=P)).then_inc(s_w1[par], 16)
                sp.wait_ge(s_w2l, n * NG + NG)
                sp.dma_start(w2[par], W2[bass.ds(e, 1)].rearrange("a (c p) d -> p (a c) d", p=P)).then_inc(s_w2[par], 16)
                if which == 1 and isinstance(n, int) and n >= NB1_MIN:
                    sp.wait_ge(s_w2[par], 16 * i + 16)

            rounds(sp, load, 1)

        @block.gpsimd
        def _(pool):
            def store(n, i, par, last):
                pool.wait_ge(s_py, n * S + 2 * S)
                pool.sem_inc(s_turn, 1)
                pool.dma_start(g.YB[bass.ds(n * B, B), :].rearrange("(s p) d -> p s d", p=P), y[par]).then_inc(s_yst[par], 16)
                if which == 1 and isinstance(n, int) and n >= NB1_MIN:
                    pool.wait_ge(s_yst[par], 16 * i + 32)

            for par in range(2):
                pool.dma_start(g.scrap[par:par + 1, :], g.zrow[0:1, :]).then_inc(s_yst[par], 16)
            rounds(pool, store)
            for par in range(2):
                sure = NB if which == 0 else NB1_MIN
                pool.wait_ge(s_yst[par], 16 * ((sure + 1 - par) // 2) + 16)

        @block.tensor
        def _(pe):
            pe.wait_ge(s_c, 32 + 32 * which)
            ins = nc.tensor.transpose(ps_h[0][:, 0:NE * FC], b1r[:], g.ident[0:NE * FC, 0:NE * FC])
            if which == 1:
                for k in range(2):
                    ins = nc.tensor.transpose(ps_h[1][:, k * 16:k * 16 + 16], lnr[:, k, :], g.ident[0:NE * KD, 0:NE * KD])
            ins.then_inc(s_ct, 1)
            pe.wait_ge(s_cc, 2)
            pe.sem_inc(s_h, 2 * FC)
            pe.sem_inc(s_y2, FC)
            pe.sem_inc(s_tr, 2)

            def transposes(par, i):
                pe.wait_ge(s_xb[par], 16 * i + 16)
                for s in range(S):
                    for k in range(KD):
                        ins = nc.tensor.transpose(ps_x[:, k, s * P:(s + 1) * P], xb[par][:, s, k * P:(k + 1) * P], g.ident[:])
                ins.then_inc(s_tr, 1)

            def product(out, left, right, first, last):
                nc.tensor.matmul(out, left[0], right[1], start=first, stop=False)
                nc.tensor.matmul(out, left[1], right[0], start=False, stop=False)
                return nc.tensor.matmul(out, left[0], right[0], start=False, stop=last)

            def second(n, par, c):
                pe.wait_ge(s_hl, n * FC + (c + 3))
                if c % G == 0:
                    pe.wait_ge(s_w2l, n * NG + (c // G + 1 + 2 * NG))
                for s in range(S):
                    sl = slice(s * P, (s + 1) * P)
                    ins = product(ps_y[s][:, 0:D], (h_hi[:, c, sl], h_lo[:, c, sl]), (w2_hi[:, c, :], w2_lo[:, c, :]), c == 0, c == FC - 1)
                ins.then_inc(s_y2, 1)

            def products(n, i, par, last):
                pe.wait_ge(s_xl, n * KD + KD)
                for c in range(FC):
                    if c % G == 0:
                        pe.wait_ge(s_w1l, n * NG + (c // G + 1 + 2 * NG))
                    pe.wait_ge(s_hh, n * FC + (c + 1))
                    sl = slice(c * P, (c + 1) * P)
                    for k in range(KD):
                        ins = product(ps_h[c % 2][:, 0:B], (w1_hi[:, par, k, sl], w1_lo[:, par, k, sl]),
                                      (x_hi[:, par, k, :], x_lo[:, par, k, :]), k == 0, k == KD - 1)
                    ins.then_inc(s_h, 1)
                    if c == 2 and not last:
                        transposes(1 - par, i + par)
                    if c == LAG:
                        pe.wait_ge(s_py, n * S + S)
                    if c >= LAG:
                        second(n, par, c - LAG)
                for c in range(FC - LAG, FC):
                    second(n, par, c)

            transposes(0, 0)
            rounds(pe, products)

        @block.scalar
        def _(act):
            act.wait_ge(s_ct, 1)
            nc.scalar.activation(b1c[:], ps_h[0][:, 0:NE * FC], ACT.Copy).then_inc(s_cc, 1)
            act.wait_ge(s_cc, 2)
            act.sem_inc(s_hh, 2)

            def split_w1(par, i, j):
                if j == 0:
                    act.wait_ge(s_w1[par], 16 * i + 16)
                sl = slice(j * G * P, (j + 1) * G * P)
                nc.scalar.activation(w1_hi[:, par, :, sl], w1[par][:, :, sl], ACT.Copy).then_inc(s_w1h, 1)

            def activate(n, i, par, last):
                e = expert(act, n)
                act.wait_ge(s_w2[par], 16 * i + 16)
                for c in range(FC):
                    if c % G == 0:
                        act.wait_ge(s_y2, n * FC + (c + G))
                        nc.scalar.activation(w2_hi[:, c:c + G, :], w2[par][:, c:c + G, :], ACT.Copy).then_inc(s_w2h, 1)
                    act.wait_ge(s_h, n * FC + (c + 1 + 2 * FC))
                    act.wait_ge(s_hl, n * FC + (c + 1))
                    bias = b1c[:, bass.ds(e * FC + c, 1)]
                    nc.scalar.activation(hT[:, c % 2, :], ps_h[c % 2][:, 0:B], func, bias=bias).then_inc(s_act, 1)
                    nc.scalar.activation(h_hi[:, c, :], ps_h[c % 2][:, 0:B], func, bias=bias).then_inc(s_hh, 1)
                    if c % G == G - 1 and not last:
                        split_w1(1 - par, i + par, c // G)

            for j in range(NG):
                split_w1(0, 0, j)
            rounds(act, activate)

        @block.vector
        def _(dve):
            dve.wait_ge(s_ct, 1)
            if which == 1:
                nc.vector.tensor_copy(lnc[:], ps_h[1][:, 0:32].rearrange("p (a e) -> p a e", a=2)).then_inc(s_cc, 1)
                dve.wait_ge(s_cc, 2)
            else:
                dve.sem_inc(s_cc, 1)
            dve.sem_inc(s_py, S)
            dve.sem_inc(s_hl, 2)

            dve.sem_inc(s_w1l, 2 * NG)
            dve.sem_inc(s_w2l, 2 * NG)

            def scaled(n, out, e):
                for k in range(KD):
                    if which == 0:
                        ins = nc.vector.tensor_copy(out[:, k, :], ps_x[:, k, 0:B])
                    else:
                        ins = nc.vector.tensor_scalar(out[:, k, :], ps_x[:, k, 0:B], lnc[:, 0, bass.ds(e * KD + k, 1)], lnc[:, 1, bass.ds(e * KD + k, 1)], ALU.mult, ALU.add)
                    ins.then_inc(s_x, 1)

            def split_x(n, par, part, e):
                if part == 0:
                    dve.wait_ge(s_tr, n + 3)
                    scaled(n, xT, e)
                elif part == 1:
                    scaled(n, x_hi[:, par], e)
                else:
                    dve.wait_ge(s_x, n * (2 * KD) + 2 * KD)
                    for k in range(KD):
                        dve.tensor_tensor(x_lo[:, par, k, :], xT[:, k, :], x_hi[:, par, k, :], ALU.subtract).then_inc(s_xl, 1)

            def split_w1(n, par, j):
                dve.wait_ge(s_w1h, n * NG + (j + 1))
                sl = slice(j * G * P, (j + 1) * G * P)
                dve.tensor_tensor(w1_lo[:, par, :, sl], w1[par][:, :, sl], w1_hi[:, par, :, sl], ALU.subtract).then_inc(s_w1l, 1)

            def results(n, i, par, last):
                e1 = None if last else expert(dve, n + 1)
                for c in range(FC):
                    if c % G == 0:
                        dve.wait_ge(s_w2h, n * NG + (c // G + 1))
                        dve.tensor_tensor(w2_lo[:, c:c + G, :], w2[par][:, c:c + G, :], w2_hi[:, c:c + G, :], ALU.subtract).then_inc(s_w2l, 1)
                    dve.wait_ge(s_hh, n * FC + (c + 3))
                    dve.tensor_tensor(h_lo[:, c, :], hT[:, c % 2, :], h_hi[:, c, :], ALU.subtract).then_inc(s_hl, 1)
                    if not last:
                        if c % G == G - 1:
                            split_w1(n + 1, 1 - par, c // G)
                        if c in (4, 5, 6):
                            split_x(n + 1, 1 - par, c - 4, e1)
                e = expert(dve, n)
                dve.wait_ge(s_yst[par], 16 * i + 16)
                dve.wait_ge(s_y2, n * FC + 2 * FC)
                for s in range(S):
                    nc.vector.tensor_tensor(y[par][:, s, :], ps_y[s][:, 0:D], b2b[:, bass.ds(e, 1), :].rearrange("p a d -> p (a d)"), ALU.add).then_inc(s_py, 1)

            e0 = expert(dve, 0)
            for part in range(3):
                split_x(0, 0, part, e0)
            for j in range(NG):
                split_w1(0, 0, j)
            rounds(dve, results)


def combine_stage(nc, g, which):
    pre = f"cb{which}_"
    GT = 5
    NG = NT // GT
    assert NG * GT == NT
    with ExitStack() as ctx:
        sb = lambda n, s, d=F32: ctx.enter_context(nc.sbuf_tensor(pre + n, s, d))
        bad = sb("bad", [P, GT, D], I32)
        low = sb("low", [P, 3, D])
        s_g = [g.sem(f"{pre}gather{k}") for k in range(NG)]
        s_dve = g.sem(pre + "dve"); s_out = g.sem(pre + "out"); s_x = g.sem(pre + "x")
        block = ctx.enter_context(nc.Block())
        rows = (g.Z, g.Y)
        filled = g.YB[0:NE * B0 if which == 0 else NB1 * B1, :]

        @block.gpsimd
        def _(pool):
            for t in range(NT):
                for k in range(which + 1):
                    pool.indirect_dma_start(rows[k][:, t, :], None, filled, bass.IndirectOffsetOnAxis(g.gslot[:, k, t:t + 1], axis=0)).then_inc(s_g[t // GT], 16)

        @block.vector
        def _(dve):
            step = Steps(dve, s_dve)
            if which == 0:
                for j, v in enumerate((0.0, 1.0e4, -1.0e4)):
                    step(dve.memset(low[:, j, :], v))
            for q in range(NG):
                dve.wait_ge(s_g[q], 16 * GT * (which + 1))
                sl = slice(q * GT, (q + 1) * GT)
                x = g.X[:, sl, :]
                for k in range(which + 1):
                    r = rows[k][:, sl, :]
                    step(dve.tensor_tensor(r, r, bcast(g.wgt[:, k, sl], 2, D), ALU.mult))
                    if which == 0:
                        step(dve.tensor_tensor(bad[:], r, r, ALU.not_equal))
                        step(dve.copy_predicated(r, bad[:], bcast(low[:, 0, :], 1, GT)))
                        step(dve.tensor_scalar(bad[:], r, 3.4028234e38, None, ALU.is_gt))
                        step(dve.copy_predicated(r, bad[:], bcast(low[:, 1, :], 1, GT)))
                        step(dve.tensor_scalar(bad[:], r, -3.4028234e38, None, ALU.is_lt))
                        step(dve.copy_predicated(r, bad[:], bcast(low[:, 2, :], 1, GT)))
                    step(dve.tensor_tensor(x, x, r, ALU.add))
                dve.sem_inc(s_x, 1)

        @block.sync
        def _(sp):
            if which == 1:
                for q in range(NG):
                    sp.wait_ge(s_x, q + 1)
                    full = GT if q < NG - 1 else GT - 1
                    sp.dma_start(g.out[q * GT * P:(q * GT + full) * P, :].rearrange("(t p) d -> p t d", p=P), g.X[:, q * GT:q * GT + full, :]).then_inc(s_out, 16)
                sp.dma_start(g.out[(NT - 1) * P:N, :], g.X[0:LAST, NT - 1, :]).then_inc(s_out, 16)
                sp.wait_ge(s_out, 16 * (NG + 1))


def rgcn_table_stage(nc, g, layer):
    pre = f"rg{layer}_"
    W, bias = (g.rW0, g.rb0) if layer == 0 else (g.rW1, g.rb1)
    R2 = NREL // 2
    with ExitStack() as ctx:
        sb = lambda n, s, d=F32: ctx.enter_context(nc.sbuf_tensor(pre + n, s, d))
        w = sb("w", [P, KD, NREL, D]); w_hi = sb("w_hi", [P, KD, NREL, D], F32R); w_lo = sb("w_lo", [P, KD, NREL, D], F32R)
        b2 = sb("b2", [P, 2, D]); x_hi = sb("x_hi", [P, 2, KD, P], F32R); x_lo = sb("x_lo", [P, 2, KD, P], F32R)
        rows = sb("rows", [P, 2, R2, 2 * D])
        ps_t = [ctx.enter_context(nc.psum_tensor(f"{pre}t{k}", [P, 512], F32)) for k in range(4)]
        ps = [ctx.enter_context(nc.psum_tensor(f"{pre}p{k}", [P, 512], F32)) for k in range(4)]
        s_ld = g.sem(pre + "load"); s_dve = g.sem(pre + "dve"); s_var = g.sem(pre + "var"); s_sq = g.sem(pre + "sqrt")
        s_ln = g.sem(pre + "ln"); s_tr = g.sem(pre + "tr"); s_T = g.sem(pre + "T")
        s_xs = g.sem(pre + "xs"); s_mm = g.sem(pre + "mm"); s_add = g.sem(pre + "add"); s_relu = g.sem(pre + "relu")
        s_turn = g.sem(pre + "turn"); s_whi = g.sem(pre + "w_hi"); s_wlo = g.sem(pre + "w_lo"); s_xl = g.sem(pre + "x_lo")
        s_st = [g.sem(f"{pre}st{k}") for k in range(2)]
        block = ctx.enter_context(nc.Block())

        def rounds(eng, body):
            with eng.Fori(0, NT // 2) as i:
                body(i * 2, i, 0)
                body(i * 2 + 1, i, 1)
            body(NT - 1, NT // 2, 0)

        @block.gpsimd
        def _(pool):
            pool.wait_ge(s_T, NT if layer == 0 else 1)

            def stage(t, i, par):
                pool.wait_ge(s_mm, t * R2 + R2)
                pool.sem_inc(s_turn, 1)
                pool.tensor_copy(x_hi[:, par], g.ACC[:, :, bass.ds(t * P, P)]).then_inc(s_xs, 1)

            rounds(pool, stage)

        @block.tensor
        def _(pe):
            if layer == 0:
                for t in range(NT):
                    pe.wait_ge(s_ln, t + 1)
                    if t >= 4:
                        pe.wait_ge(s_T, t - 3)
                    for k in range(KD):
                        ins = nc.tensor.transpose(ps_t[t % 4][:, k * P:(k + 1) * P], g.Y[:, t, k * P:(k + 1) * P], g.ident[:])
                    ins.then_inc(s_tr, 1)
            pe.sem_inc(s_mm, 2 * R2)
            pe.wait_ge(s_wlo, KD)

            def products(t, i, par):
                pe.wait_ge(s_xs, t + 1)
                pe.wait_ge(s_xl, t + 1)
                for r in range(R2):
                    pe.wait_ge(s_add, t * R2 + (r + 1))
                    for k in range(KD):
                        for x, m in ((x_lo, w_hi), (x_hi, w_lo), (x_hi, w_hi)):
                            ins = nc.tensor.matmul(ps[r][:], x[:, par, k, :], m[:, k, 2 * r:2 * r + 2, :].rearrange("p r d -> p (r d)"),
                                                   start=(k == 0 and x is x_lo), stop=(k == KD - 1 and m is w_hi and x is x_hi))
                    ins.then_inc(s_mm, 1)

            rounds(pe, products)

        @block.vector
        def _(dve):
            step = Steps(dve, s_dve)
            dve.wait_ge(s_ld, 48)
            for k in range(KD):
                dve.wait_ge(s_whi, k + 1)
                dve.tensor_tensor(w_lo[:, k], w[:, k], w_hi[:, k], ALU.subtract).then_inc(s_wlo, 1)
            if layer == 0:
                layernorm(nc, g, dve, step, s_var, s_sq, 1, g.X, g.Y, s_ln)
            dve.sem_inc(s_add, R2)

            def low(t, par):
                dve.wait_ge(s_xs, t + 1)
                dve.tensor_tensor(x_lo[:, par], g.ACC[:, :, bass.ds(t * P, P)], x_hi[:, par], ALU.subtract).then_inc(s_xl, 1)

            low(0, 0)

            def add(t, i, par):
                if not (par == 0 and isinstance(t, int)):
                    low(t + 1, 1 - par)
                dve.wait_ge(s_st[par], 16 * i + 16)
                for r in range(R2):
                    dve.wait_ge(s_mm, t * R2 + (r + 1 + 2 * R2))
                    nc.vector.tensor_tensor(rows[:, par, r, :], ps[r][:], b2[:].rearrange("p r d -> p (r d)"), ALU.add).then_inc(s_add, 1)

            rounds(dve, add)

        @block.scalar
        def _(act):
            act.wait_ge(s_ld, 48)
            for k in range(KD):
                nc.scalar.activation(w_hi[:, k], w[:, k], ACT.Copy).then_inc(s_whi, 1)
            if layer == 0:
                act.wait_ge(s_var, 1)
                nc.scalar.activation(g.ln_s[:], g.ln_var[:], ACT.Sqrt).then_inc(s_sq, 1)
                for t in range(NT):
                    act.wait_ge(s_tr, t + 1)
                    nc.scalar.activation(g.ACC[:, :, t * P:(t + 1) * P], ps_t[t % 4][:, 0:D].rearrange("p (k n) -> p k n", k=KD), ACT.Copy).then_inc(s_T, 1)
            else:
                act.sem_inc(s_T, 1)

            def relu(t, i, par):
                for r in range(R2):
                    act.wait_ge(s_add, t * R2 + (r + 1 + R2))
                    nc.scalar.activation(rows[:, par, r, :], rows[:, par, r, :], ACT.Relu).then_inc(s_relu, 1)

            rounds(act, relu)

        @block.sync
        def _(sp):
            sp.dma_start(w[:, 0], W[:, 0:P, :].rearrange("r p o -> p r o")).then_inc(s_ld, 16)
            sp.dma_start(w[:, 1], W[:, P:2 * P, :].rearrange("r p o -> p r o")).then_inc(s_ld, 16)
            sp.dma_start(b2[:], bcast(bias, 0, 2).partition_broadcast(P)).then_inc(s_ld, 16)
            table = g.Gtab[0:ZERO_ROW, :].rearrange("(r n) d -> n r d", n=NP)

            def store(t, i, par):
                sp.wait_ge(s_relu, t * R2 + R2)
                sp.dma_start(table[bass.ds(t * P, P), :, :], rows[:, par].rearrange("p a (b d) -> p (a b) d", b=2)).then_inc(s_st[par], 16)

            for par in range(2):
                sp.dma_start(g.scrap[par:par + 1, :], g.zrow[0:1, :]).then_inc(s_st[par], 16)
            rounds(sp, store)
            sp.wait_ge(s_st[0], 16 * (NT // 2 + 1) + 16)
            sp.wait_ge(s_st[1], 16 * (NT // 2) + 16)


def add_sums_stage(nc, g):
    with ExitStack() as ctx:
        ps = [ctx.enter_context(nc.psum_tensor(f"as_ps{k}", [P, 512], F32)) for k in range(4)]
        s_tr = g.sem("as_tr"); s_add = g.sem("as_add")
        block = ctx.enter_context(nc.Block())

        @block.tensor
        def _(pe):
            for t in range(NT):
                if t >= 4:
                    pe.wait_ge(s_add, t - 3)
                for j in range(KD):
                    ins = nc.tensor.transpose(ps[t % 4][:, j * P:(j + 1) * P], g.ACC[:, j, t * P:(t + 1) * P], g.ident[:])
                ins.then_inc(s_tr, 1)

        @block.vector
        def _(dve):
            for t in range(NT):
                dve.wait_ge(s_tr, t + 1)
                nc.vector.tensor_tensor(g.X[:, t, :], g.X[:, t, :], ps[t % 4][:, 0:D], ALU.add).then_inc(s_add, 1)


def build(nc, ins, out):
    with ExitStack() as top:
        g = Places()
        g.x, g.src, g.dst, g.typ, g.gat_w, g.att_src = (ins["x"], ins["src"], ins["dst"], ins["typ"], ins["gat_w"], ins["att_src"])
        g.att_dst, g.gat_bias, g.gate_w, g.gate_b, g.f0_w1, g.f0_b1 = (ins["att_dst"], ins["gat_bias"], ins["gate_w"], ins["gate_b"], ins["f0_w1"], ins["f0_b1"])
        g.f0_w2, g.f0_b2, g.rW0, g.rb0, g.rW1, g.rb1 = (ins["f0_w2"], ins["f0_b2"], ins["rW0"], ins["rb0"], ins["rW1"], ins["rb1"])
        g.Wr, g.br, g.ln_g, g.ln_b, g.f1_w1, g.f1_b1 = (ins["Wr"], ins["br"], ins["ln_g"], ins["ln_b"], ins["f1_w1"], ins["f1_b1"])
        g.f1_w2, g.f1_b2 = (ins["f1_w2"], ins["f1_b2"])
        g.out = out
        g.stages = 0
        dram = lambda name, shape, dt=F32: nc.dram_tensor(name, shape, dt, kind="Internal").ap()
        sb = lambda name, shape, dt=F32: top.enter_context(nc.sbuf_tensor(name, shape, dt))
        g.S_src, g.S_dst, g.S_typ = (dram(n, (E + 2 * EPAD,), I32) for n in ("s_src_d", "s_dst_d", "s_typ_d"))
        g.S_rec = dram("s_rec_d", (E, 4), I32)
        g.Htab = dram("h_table", (NP, D))
        g.Atab = dram("a_table", (NP, 8))
        g.Gtab = dram("rel_table", (ZERO_ROW + 1, D))
        g.XB = dram("slots_in", (NB1 * B1 + 2 * NP, D))
        g.YB = dram("slots_out", (NB1 * B1, D))
        g.scrap = dram("scrap", (2, D))
        g.iota_i = sb("iota_i", [P, P], I32); g.iotap_i = sb("iotap_i", [P, P], I32)
        g.iota = sb("iota", [P, P]); g.iotap = sb("iotap", [P, P]); g.ident = sb("ident", [P, P])
        g.upper = sb("upper", [P, P]); g.ones = sb("ones", [P, P]); g.zrow = sb("zrow", [P, D]); g.valid = sb("valid", [P, 1])
        g.unsorted = sb("unsorted", [1, 1], I32)
        g.ln_st = sb("ln_st", [P, NT, 6])
        g.ln_mean, g.ln_var, g.ln_r, g.ln_t1, g.ln_t2, g.ln_s = (sb(f"ln_{n}", [P, NT]) for n in ("mean", "var", "r", "t1", "t2", "s"))
        g.wgt = sb("wgt", [P, 2, NT]); g.gslot = sb("gslot", [P, 2, NT], I32); g.blk_expert = sb("blk_expert", [1, NB1], I32)
        g.blk_used = sb("blk_used", [1, 1], I32)

        stage(nc, g, edges_stage)
        stage(nc, g, sort_stage)
        TP = T + HALF
        g.relI = sb("relI", [P, TP], I32); g.dstrel = sb("dstrel", [P, TP]); g.base = sb("base", [1, T], I32)
        g.X = sb("X", [P, NT, D]); g.Y = sb("Y", [P, NT, D])
        with ExitStack() as gat:
            gsb = lambda name, shape, dt=F32: gat.enter_context(nc.sbuf_tensor(name, shape, dt))
            g.srcI = gsb("srcI", [P, TP], I32); g.dstI = gsb("dstI", [P, TP], I32)
            g.PT = gsb("PT", [P, TP, 8])
            with ExitStack() as lanes:
                lsb = lambda name, shape, dt=F32: lanes.enter_context(nc.sbuf_tensor(name, shape, dt))
                g.first = lsb("first", [LANES, LC, P]); g.firstneg = lsb("firstneg", [LANES, LC, P]); g.endneg = lsb("endneg", [LANES, LC, P])
                stage(nc, g, tables_stage)
                stage(nc, g, gat_table_stage)
                g.AS = lsb("AS", [P, T, 12]); g.baseq = lsb("baseq", [1, LANES], I32)
                g.AS4 = g.AS[:].rearrange("p (c q) a -> p c q a", c=LC)
                stage(nc, g, scores_stage)
                stage(nc, g, softmax_stage)
            g.ACC = gsb("ACC", [P, KD + 1, AW])
            stage(nc, g, edge_pass, "gat", g.Htab, g.srcI, 0)
            g.Z = gsb("Z", [P, NT, D])
            stage(nc, g, gat_finish_stage)
        g.Z = sb("Z1", [P, NT, D])
        stage(nc, g, router_stage, 0)
        stage(nc, g, experts_stage, 0)
        stage(nc, g, combine_stage, 0)
        with ExitStack() as rg:
            g.ACC = rg.enter_context(nc.sbuf_tensor("ACC1", [P, KD, AW], F32))
            for layer in range(2):
                stage(nc, g, rgcn_table_stage, layer)
                stage(nc, g, edge_pass, "rgcn", g.Gtab, g.relI, 1 + layer)
            stage(nc, g, add_sums_stage)
        stage(nc, g, router_stage, 1)
        stage(nc, g, experts_stage, 1)
        stage(nc, g, combine_stage, 1)


NAMES = {
    "x": "x", "src": "src", "dst": "dst", "edge_type_8": "typ",
    "L0_gnn_W": "gat_w", "L0_gnn_att_src": "att_src", "L0_gnn_att_dst": "att_dst", "L0_gnn_bias": "gat_bias",
    "L0_ffn_gate_w": "gate_w", "L0_ffn_gate_b": "gate_b",
    "L0_ffn_w1": "f0_w1", "L0_ffn_b1": "f0_b1", "L0_ffn_w2": "f0_w2", "L0_ffn_b2": "f0_b2",
    "L1_gnn_W0": "rW0", "L1_gnn_b0": "rb0", "L1_gnn_W1": "rW1", "L1_gnn_b1": "rb1",
    "L1_ffn_Wr": "Wr", "L1_ffn_br": "br", "L1_ffn_ln_g": "ln_g", "L1_ffn_ln_b": "ln_b",
    "L1_ffn_W1": "f1_w1", "L1_ffn_b1": "f1_b1", "L1_ffn_W2": "f1_w2", "L1_ffn_b2": "f1_b2",
}


def kernel(**inputs):
    import concourse.bacc as bacc
    from concourse.bass_utils import run_bass_kernel_spmd

    nc = bacc.Bacc("TRN2", target_bir_lowering=False, num_devices=1)
    arrays, ins = {}, {}
    for name, short in NAMES.items():
        a = np.ascontiguousarray(inputs[name])
        arrays["in_" + name] = a
        ins[short] = nc.dram_tensor("in_" + name, a.shape, mybir.dt.from_np(a.dtype), kind="ExternalInput").ap()
    out = nc.dram_tensor("out_0", (N, D), F32, kind="ExternalOutput").ap()
    build(nc, ins, out)
    r = run_bass_kernel_spmd(nc, [arrays], core_ids=[0])
    return r.results[0]["out_0"]
```
